# Optimizing a Trainium2 kernel written in Bass

```python
import numpy as np
import jax
import jax.numpy as jnp

def _softmax(x, axis=-1):
    return jax.nn.softmax(x, axis=axis)

def _gelu(x):
    return jax.nn.gelu(x, approximate=True)

def _silu(x):
    return jax.nn.silu(x)

def _sigmoid(x):
    return jax.nn.sigmoid(x)

def _layernorm(x, axis=-1, eps=1e-05):
    m = jnp.mean(x, axis=axis, keepdims=True)
    v = jnp.var(x, axis=axis, keepdims=True)
    return (x - m) / jnp.sqrt(v + eps)

def _scatter_add(tgt, idx, src, axis=0):
    return tgt.at[idx].add(src)

def _segment_sum(src, seg, n):
    return jax.ops.segment_sum(src, seg, n)
kernel_name = 'mk_audio_tower_d1_tok_aud1d512_r4_7c423b'

def setup_inputs(seed: int=0):
    np.random.seed(seed)
    _w = jnp.asarray

    def _rec_inputs():
        import jax
        import jax.numpy as jnp
        _rk = jax.random.key(seed)
        x = 0.00021031 + 1.00007 * jax.random.normal(jax.random.fold_in(_rk, 1), (64, 20000), jnp.float32)
        return x
    x = _rec_inputs()

    def _L0_tok_setup():
        import jax, jax.numpy as jnp
        import numpy as np
        FRAME_LENGTH = 256
        B, T = (16, 524288)

        def _mdct_matrix(length):
            L2 = length
            Lh = L2 // 2
            n = jnp.arange(L2, dtype=jnp.float32) + 0.5
            k = jnp.pi / Lh * n[:Lh]
            n = n + Lh / 2
            z = jnp.sqrt(jnp.float32(2.0 / Lh * 2.0))
            return z * jnp.cos(n[:, None] * k[None, :])
        key = jax.random.key(seed)
        x = jax.random.normal(key, (B, T), dtype=jnp.float32)
        return {'x': x}
    _L0_tok_all = _L0_tok_setup()
    _L0_tok_in = {k: v for k, v in _L0_tok_all.items() if k in ()}
    del _L0_tok_all

    def _L0_attn_setup():
        import jax, jax.numpy as jnp
        import numpy as np
        S, B, H, D, IN = (128, 8, 8, 64, 128)
        PROJ = H * (5 * D + 2)
        key = jax.random.key(seed)
        k0, k1, k2 = jax.random.split(key, 3)
        x = jax.random.normal(k0, (S, B, IN), jnp.float32)
        W_slow = jax.random.normal(k1, (PROJ, IN), jnp.float32) / np.sqrt(IN).astype(np.float32)
        W_out = jax.random.normal(k2, (IN, H * D), jnp.float32) / np.sqrt(H * D).astype(np.float32)
        ln_gamma = jnp.ones((IN,), jnp.float32)
        ln_beta = jnp.zeros((IN,), jnp.float32)
        return dict(x=x, W_slow=W_slow, W_out=W_out, ln_gamma=ln_gamma, ln_beta=ln_beta)
    _L0_attn_all = _L0_attn_setup()
    _L0_attn_in = {k: v for k, v in _L0_attn_all.items() if k in ('W_slow', 'W_out', 'ln_gamma', 'ln_beta')}
    del _L0_attn_all

    def _L0_ffn_setup():
        import jax, jax.numpy as jnp
        import numpy as np
        B, S, D, F, E, NS, K = (2, 512, 128, 512, 8, 2, 2)
        key = jax.random.key(seed)
        ks = jax.random.split(key, 6)
        scale = 0.02

        def p(k, shape):
            return jax.random.normal(k, shape, jnp.float32) * scale
        return {'x': jax.random.normal(ks[0], (B, S, D), jnp.float32), 'gate_w': p(ks[1], (E, D)), 'gate_b': jnp.zeros((E,), jnp.float32), 'sw1': p(ks[2], (NS, F, D)), 'sb1': jnp.zeros((NS, F), jnp.float32), 'sw2': p(ks[3], (NS, D, F)), 'sb2': jnp.zeros((NS, D), jnp.float32), 'rw1': p(ks[4], (E, F, D)), 'rb1': jnp.zeros((E, F), jnp.float32), 'rw2': p(ks[5], (E, D, F)), 'rb2': jnp.zeros((E, D), jnp.float32)}
    _L0_ffn_all = _L0_ffn_setup()
    _L0_ffn_in = {k: v for k, v in _L0_ffn_all.items() if k in ('gate_w', 'gate_b', 'sw1', 'sb1', 'sw2', 'sb2', 'rw1', 'rb1', 'rw2', 'rb2')}
    del _L0_ffn_all
    return {'x': x, 'L0_attn_W_slow': _L0_attn_in['W_slow'], 'L0_attn_W_out': _L0_attn_in['W_out'], 'L0_attn_ln_gamma': _L0_attn_in['ln_gamma'], 'L0_attn_ln_beta': _L0_attn_in['ln_beta'], 'L0_ffn_gate_w': _L0_ffn_in['gate_w'], 'L0_ffn_gate_b': _L0_ffn_in['gate_b'], 'L0_ffn_sw1': _L0_ffn_in['sw1'], 'L0_ffn_sb1': _L0_ffn_in['sb1'], 'L0_ffn_sw2': _L0_ffn_in['sw2'], 'L0_ffn_sb2': _L0_ffn_in['sb2'], 'L0_ffn_rw1': _L0_ffn_in['rw1'], 'L0_ffn_rb1': _L0_ffn_in['rb1'], 'L0_ffn_rw2': _L0_ffn_in['rw2'], 'L0_ffn_rb2': _L0_ffn_in['rb2']}

def reference(x, L0_attn_W_slow, L0_attn_W_out, L0_attn_ln_gamma, L0_attn_ln_beta, L0_ffn_gate_w, L0_ffn_gate_b, L0_ffn_sw1, L0_ffn_sb1, L0_ffn_sw2, L0_ffn_sb2, L0_ffn_rw1, L0_ffn_rb1, L0_ffn_rw2, L0_ffn_rb2):
    import jax
    import jax.numpy as jnp

    def _L0_tok_ref(x):
        import jax, jax.numpy as jnp
        import numpy as np
        FRAME_LENGTH = 256
        B, T = (16, 524288)

        def _mdct_matrix(length):
            L2 = length
            Lh = L2 // 2
            n = jnp.arange(L2, dtype=jnp.float32) + 0.5
            k = jnp.pi / Lh * n[:Lh]
            n = n + Lh / 2
            z = jnp.sqrt(jnp.float32(2.0 / Lh * 2.0))
            return z * jnp.cos(n[:, None] * k[None, :])
        L = FRAME_LENGTH
        hop = L // 2
        xp = jnp.pad(x, ((0, 0), (L // 2, hop + (L - 1) // 2)))
        n_frames = (xp.shape[-1] - L) // hop + 1
        idx = jnp.arange(n_frames)[:, None] * hop + jnp.arange(L)[None, :]
        frames = xp[:, idx]
        w = jnp.sin(jnp.pi * (jnp.arange(L, dtype=jnp.float32) + 0.5) / L)
        Wm = _mdct_matrix(L)
        return jnp.einsum('bnl,lk->bnk', frames * w, Wm)

    def _L0_attn_ref(x, W_slow, W_out, ln_gamma, ln_beta):
        import jax, jax.numpy as jnp
        import numpy as np
        S, B, H, D, IN = (128, 8, 8, 64, 128)
        PROJ = H * (5 * D + 2)
        slen, bsz, in_dim = x.shape
        mu = x.mean(-1, keepdims=True)
        var = x.var(-1, keepdims=True)
        normed = (x - mu) / jnp.sqrt(var + 1e-05) * ln_gamma + ln_beta
        qkvb = (normed @ W_slow.T).reshape(slen, bsz, H, 5 * D + 2)
        q, k, v, rk, rv, beta, rbeta = jnp.split(qkvb, [D, 2 * D, 3 * D, 4 * D, 5 * D, 5 * D + 1], axis=-1)
        q = jax.nn.softmax(q, axis=-1)
        k = jax.nn.softmax(k, axis=-1)
        rk = jax.nn.softmax(rk, axis=-1)
        beta = jax.nn.sigmoid(beta)
        rbeta = jax.nn.sigmoid(rbeta)
        W0 = jnp.zeros((bsz, H, D, D), x.dtype)

        def fw_step(W, inp):
            qt, kt, vt, bt = inp
            v_old = jnp.einsum('bhij,bhj->bhi', W, kt)
            W = W + (bt * (vt - v_old))[..., :, None] * kt[..., None, :]
            z = jnp.einsum('bhij,bhj->bhi', W, qt)
            return (W, z)
        _, z = jax.lax.scan(fw_step, W0, (q, k, v, beta))
        R0 = jnp.zeros((bsz, H, D, D), x.dtype)
        h0 = jnp.zeros((bsz, H, D), x.dtype)

        def rec_step(carry, inp):
            R, h = carry
            zt, kt, vt, bt = inp
            qh = jax.nn.softmax(h, axis=-1)
            v_old = jnp.einsum('bhij,bhj->bhi', R, kt)
            R = R + (bt * (vt - v_old))[..., :, None] * kt[..., None, :]
            h = zt + jnp.einsum('bhij,bhj->bhi', R, qh)
            return ((R, h), h)
        _, hs = jax.lax.scan(rec_step, (R0, h0), (z, rk, rv, rbeta))
        out = hs.reshape(slen, bsz, H * D) @ W_out.T
        return x + out

    def _L0_ffn_ref(x, gate_w, gate_b, sw1, sb1, sw2, sb2, rw1, rb1, rw2, rb2):
        import jax, jax.numpy as jnp
        import numpy as np
        B, S, D, F, E, NS, K = (2, 512, 128, 512, 8, 2, 2)
        b, s, d = x.shape
        t = x.reshape(-1, d)
        T = t.shape[0]
        hs = jax.nn.gelu(jnp.einsum('td,nfd->ntf', t, sw1) + sb1[:, None, :], approximate=False)
        shared = jnp.einsum('ntf,ndf->td', hs, sw2) + sb2.sum(axis=0)
        logits = t @ gate_w.T + gate_b
        probs = jax.nn.softmax(logits, axis=-1)
        top_v, top_i = jax.lax.top_k(probs, K)
        cw = jnp.zeros_like(probs).at[jnp.arange(T)[:, None], top_i].add(top_v)
        hr = jax.nn.gelu(jnp.einsum('td,efd->etf', t, rw1) + rb1[:, None, :], approximate=False)
        oe = jnp.einsum('etf,edf->etd', hr, rw2) + rb2[:, None, :]
        routed = jnp.einsum('etd,te->td', oe, cw)
        return (shared + routed).reshape(b, s, d)
    h = _L0_tok_ref(x)
    h = h + _L0_attn_ref(_layernorm(h, axis=-1), L0_attn_W_slow, L0_attn_W_out, L0_attn_ln_gamma, L0_attn_ln_beta)
    h = h + _L0_ffn_ref(_layernorm(h, axis=-1), L0_ffn_gate_w, L0_ffn_gate_b, L0_ffn_sw1, L0_ffn_sb1, L0_ffn_sw2, L0_ffn_sb2, L0_ffn_rw1, L0_ffn_rb1, L0_ffn_rw2, L0_ffn_rb2)
    return h

_drawn_inputs = setup_inputs


def setup_inputs(seed=0):
    import zlib

    import numpy as np

    out = dict(_drawn_inputs(seed))
    spreads = {'L0_attn_ln_gamma': (1.0, 0.6),
     'L0_attn_ln_beta': (0.0, 0.589),
     'L0_ffn_gate_b': (0.0, 0.8),
     'L0_ffn_sb1': (0.0, 0.561),
     'L0_ffn_sb2': (0.0, 0.1),
     'L0_ffn_rb1': (0.0, 0.8),
     'L0_ffn_rb2': (0.0, 0.783)}
    factors = {'L0_ffn_gate_w': 5.858, 'L0_ffn_rw1': 8.0, 'L0_ffn_rw2': 8.0}
    for name, (base, spread) in spreads.items():
        noise = np.random.default_rng([zlib.crc32(name.encode()), seed]).standard_normal(out[name].shape)
        drawn = base * np.exp(spread * noise) if base else spread * noise
        out[name] = jnp.asarray(drawn.astype(out[name].dtype))
    for name, factor in factors.items():
        out[name] = (out[name] * factor).astype(out[name].dtype)
    return out
```

```python
from contextlib import ExitStack

import concourse.bass as bass
import numpy as np
from concourse import mybir

F32 = mybir.dt.float32
ALU = mybir.AluOpType
ACT = mybir.ActivationFunctionType
AX_X = mybir.AxisListType.X

P = 128
S, NF = 64, 158
LEN = 20000
HOP = 128
IN = 128
H, D = 8, 64
HD = H * D
NE, NSH, F = 8, 2, 512
EXPERTS = NE + NSH
FC = F // P
TILES = 80
REAL_TILES = NF // 2
FRAMES = 2 * TILES
UNITS = 4
GROUP = 16
PAIRS = FRAMES // GROUP // 2
BATCH = 4
EPS = 1e-5

COL = {"k": 0, "q": HD, "rk": 2 * HD, "v": 3 * HD, "rv": 4 * HD, "b": 5 * HD}
PROJ = 5 * HD + 2 * H


def delta_rule_tiles(nc, frames_d, mdct_d, wslow_d, gamma_d, beta_d, masks_d, res_d, rk_d, u_d, z_d):
    with ExitStack() as ctx:
        def sb(name, shape):
            return ctx.enter_context(nc.sbuf_tensor(name, shape, F32))

        def ps(name, shape):
            return ctx.enter_context(nc.psum_tensor(name, shape, F32))

        def sem(name):
            return ctx.enter_context(nc.semaphore(name))

        wslow = sb("wslow", [P, PROJ])
        mdct = sb("mdct", [P, 2, IN])
        gamma = sb("gamma", [P, 1])
        beta = sb("beta", [P, 1])
        masks = sb("masks", [P, 3, P])
        ident, mask_strict, mask_causal = masks[:, 0, :], masks[:, 1, :], masks[:, 2, :]
        minus_half = sb("minus_half", [P, 1])
        frames = sb("frames", [P, 3 * S])
        stats = sb("stats", [P, 2, 6])
        meanvar = sb("meanvar", [P, 2, 2])
        vareps = sb("vareps", [P, 2])
        rstd = sb("rstd", [P, 2])
        x1 = sb("x1", [P, IN])
        res = sb("res", [P, IN])
        normed = sb("normed", [P, IN])
        normedT = sb("normedT", [P, P])
        bexp = sb("bexp", [P, 2 * H])
        bexp1 = sb("bexp1", [P, 2 * H])
        rate = sb("rate", [P, 2 * H])
        rowmax = sb("rowmax", [P, 3, H])
        rowsum = sb("rowsum", [P, 3, H])
        rowinv = sb("rowinv", [P, 3, H])
        expd = sb("expd", [P, 3, HD])
        soft = sb("soft", [P, 3, HD])
        values = sb("values", [P, 2, HD])
        kqT = sb("kqT", [P, H // 2, 2, P])
        rkT = sb("rkT", [P, H // 2, P])
        PX = [sb(f"PX{u}", [P, 4, 192]) for u in range(UNITS)]
        Q = [sb(f"Q{u}", [P, 4, P]) for u in range(UNITS)]
        W = sb("W", [P, UNITS, 4, D])
        AT = sb("AT", [P, H, P])
        zrow = sb("zrow", [P, HD])

        ab = [ps(f"ab{n}", [P, 512]) for n in range(2)]
        pxp = [ps(f"pxp{n}", [P, 2, 512]) for n in range(2)]
        tbp = [ps(f"tbp{n}", [P, 512]) for n in range(2)]

        held = sem("held")
        consts_in = sem("consts_in")
        half_set = sem("half_set")
        frames_in = sem("frames_in")
        ab_full = sem("ab_full")
        stats_ok = sem("stats_ok")
        meanvar_ok = sem("meanvar_ok")
        vareps_ok = sem("vareps_ok")
        rstd_ok = sem("rstd_ok")
        x1_ok = sem("x1_ok")
        res_ok = sem("res_ok")
        normed_ok = sem("normed_ok")
        normedT_ok = sem("normedT_ok")
        bexp_ok = sem("bexp_ok")
        bexp1_ok = sem("bexp1_ok")
        rate_ok = sem("rate_ok")
        rowmax_ok = sem("rowmax_ok")
        shifted_ok = sem("shifted_ok")
        exp_ok = sem("exp_ok")
        rowsum_ok = sem("rowsum_ok")
        rowinv_ok = sem("rowinv_ok")
        soft_ok = sem("soft_ok")
        values_ok = sem("values_ok")
        turned_ok = sem("turned_ok")
        pxp_full = sem("pxp_full")
        power0_ok = sem("power0_ok")
        x0_ok = sem("x0_ok")
        added_ok = sem("added_ok")
        power_ok = sem("power_ok")
        tbp_full = sem("tbp_full")
        qdve_ok = sem("qdve_ok")
        qact_ok = sem("qact_ok")
        w_ok = sem("w_ok")
        z_ok = sem("z_ok")
        res_out = sem("res_out")
        rk_out = sem("rk_out")
        u_out = sem("u_out")
        z_out = sem("z_out")

        def head_cols(slot, width):
            return pxp[slot][:, :, 0:2 * width].rearrange("p b (j c) -> p b j c", j=2)

        def heads(t):
            return t.rearrange("p (b j) c -> p b j c", b=2)

        def schedule(eng, prologue, body):
            prologue()
            body(0, 1, 2)
            with eng.Fori(1, TILES - 2) as i:
                body(i, i + 1, i + 2)
            body(TILES - 2, TILES - 1, None)
            body(TILES - 1, None, None)

        block = ctx.enter_context(nc.Block())

        @block.sync
        def _(sp):
            def load_frames(j):
                if not (isinstance(j, int) and j == 0):
                    sp.wait_ge(ab_full, 11 * (j - 1) + 1)
                    sp.sem_inc(held, 1)
                sp.dma_start(frames[:], frames_d[:, bass.ds(j * 2 * S, 3 * S)]).then_inc(frames_in, 16)

            def per_chain(dram, j, w):
                return dram.rearrange("(j w) h t d -> w j t h d", w=2)[w, bass.ds(j, 1), :, :, :]\
                    .rearrange("j t h d -> (j t) h d")

            def store_rk(j):
                sp.wait_ge(soft_ok, 3 * j + 3)
                sp.sem_inc(held, 1)
                for w in range(2):
                    sp.dma_start(per_chain(rk_d, j, w), soft[w * S:(w + 1) * S, 2, :]
                                 .rearrange("p (h d) -> p h d", h=H)).then_inc(rk_out, 16)

            def store_res(j):
                sp.wait_ge(res_ok, j + 1)
                sp.sem_inc(held, 1)
                sp.dma_start(res_d[bass.ds(j * P, P), :], res[:]).then_inc(res_out, 16)

            def prologue():
                for t, d in ((mdct[:], mdct_d), (masks[:], masks_d), (gamma[:], gamma_d), (beta[:], beta_d),
                             (wslow[:], wslow_d)):
                    sp.dma_start(t, d).then_inc(consts_in, 16)
                load_frames(0)
                store_res(0)
                load_frames(1)
                store_rk(0)
                store_res(1)

            def body(i, rest, ln):
                if ln is not None:
                    load_frames(ln)
                if rest is not None:
                    store_rk(rest)
                if ln is not None:
                    store_res(ln)
                sp.wait_ge(w_ok, 12 * i + 12)
                sp.sem_inc(held, 1)
                for w in range(2):
                    sp.dma_start(per_chain(u_d, i, w), W[w * S:(w + 1) * S, 2:4, :, :]
                                 .rearrange("p u h d -> p (u h) d")).then_inc(u_out, 16)
                sp.wait_ge(z_ok, 2 * i + 2)
                sp.sem_inc(held, 1)
                for w in range(2):
                    sp.dma_start(per_chain(z_d, i, w), zrow[w * S:(w + 1) * S, :]
                                 .rearrange("p (h d) -> p h d", h=H)).then_inc(z_out, 16)

            schedule(sp, prologue, body)
            sp.wait_ge(res_out, 16 * TILES)
            sp.wait_ge(rk_out, 32 * TILES)
            sp.wait_ge(u_out, 32 * TILES)
            sp.wait_ge(z_out, 32 * TILES)

        @block.tensor
        def _(pe):
            def project(j, name, slot):
                c = COL[name]
                n = 2 * H if name == "b" else HD
                pe.matmul(ab[slot][:, 0:n], normedT[:], wslow[:, c:c + n], start=True, stop=True)\
                    .then_inc(ab_full, 1)

            def frame_products(j):
                pe.wait_ge(frames_in, 16 * (j + 1))
                if not (isinstance(j, int) and j == 0):
                    pe.wait_ge(turned_ok, 3 * j)
                pe.matmul(ab[0][:, 0:IN], frames[:, 0:P], mdct[:, 0, :], start=True, stop=False)
                pe.matmul(ab[0][:, 0:IN], frames[:, S:S + P], mdct[:, 1, :], start=False, stop=True)\
                    .then_inc(ab_full, 1)

            def turn_normed(j):
                pe.wait_ge(normed_ok, j + 1)
                pe.transpose(ab[1][:, 0:P], normed[:], ident).then_inc(ab_full, 1)

            def project_bkq(j):
                pe.wait_ge(normedT_ok, j + 1)
                pe.wait_ge(res_ok, j + 1)
                project(j, "b", 0)
                project(j, "k", 1)
                pe.wait_ge(bexp_ok, j + 1)
                project(j, "q", 0)

            def project_rk_v(j):
                pe.wait_ge(shifted_ok, 3 * j + 1)
                project(j, "rk", 1)
                pe.wait_ge(shifted_ok, 3 * j + 2)
                project(j, "v", 0)

            def project_rv(j):
                pe.wait_ge(shifted_ok, 3 * j + 3)
                project(j, "rv", 1)

            def turn_keys(j):
                for n in range(3):
                    pe.wait_ge(soft_ok, 3 * j + n + 1)
                    if n < 2:
                        pe.wait_ge(values_ok, 2 * j + n + 1)
                    else:
                        pe.wait_ge(turned_ok, 3 * j + 1)
                    for c in range(H // 2):
                        last = pe.transpose(ab[n % 2][:, c * P:(c + 1) * P], soft[:, n, c * P:(c + 1) * P], ident)
                    last.then_inc(ab_full, 1)

            def grams(j):
                for u in range(UNITS):
                    if u < 2:
                        pe.wait_ge(turned_ok, 3 * j + 2)
                        if not (isinstance(j, int) and j == 0):
                            pe.wait_ge(power_ok, 16 * j - 1 + u)
                    else:
                        pe.wait_ge(turned_ok, 3 * j + 3)
                        pe.wait_ge(power0_ok, 4 * j + u - 1)
                    for n in range(4):
                        h = 4 * (u % 2) + n
                        rows = slice((h % 2) * D, (h % 2) * D + D)
                        if u < 2:
                            last = pe.matmul(head_cols(u % 2, 256)[:, n % 2, n // 2, :], kqT[rows, h // 2, 0, :],
                                             kqT[rows, h // 2, :, :].rearrange("p a c -> p (a c)"),
                                             start=True, stop=True)
                        else:
                            last = pe.matmul(head_cols(u % 2, P)[:, n % 2, n // 2, :], rkT[rows, h // 2, :],
                                             rkT[rows, h // 2, :], start=True, stop=True)
                    last.then_inc(pxp_full, 1)

            def product(i, level, u):
                q_ok = qdve_ok if u < 2 else qact_ok
                pe.wait_ge(q_ok, 8 * i + 2 * level + u % 2 + 1)
                if level == 0:
                    pe.wait_ge(x0_ok, 4 * i + u + 1)
                    if u < 2:
                        pe.wait_ge(power0_ok, 4 * i + u + 3)
                    else:
                        pe.wait_ge(power_ok, 16 * i + u - 1)
                else:
                    pe.wait_ge(power_ok, 16 * i + 4 * level + u - 1)
                out = head_cols(u % 2, 192)
                for n in range(4):
                    o = out[:, n // 2, n % 2, :]
                    if level < 3:
                        last = pe.matmul(o, Q[u][:, n, :], PX[u][:, n, :], start=True, stop=True)
                    else:
                        pe.matmul(o[:, P:192], Q[u][:, n, :], PX[u][:, n, P:192], start=True, stop=True)
                        last = pe.matmul(o[:, 0:P], PX[u][:, n, 0:P], Q[u][:, n, :], start=True, stop=True)
                last.then_inc(pxp_full, 1)

            def turn_power(i, level, u):
                if level == -1:
                    pe.wait_ge(power0_ok, 4 * i + u + 1)
                else:
                    pe.wait_ge(power_ok, 16 * i + 4 * level + u + 1)
                if u >= 2:
                    pe.wait_ge(qdve_ok, 8 * i + 2 * (level + 1) + u - 1)
                elif level >= 0:
                    pe.wait_ge(qact_ok, 8 * i + 2 * level + u + 1)
                elif not (isinstance(i, int) and i == 0):
                    pe.wait_ge(z_ok, 2 * (i - 1) + u + 1)
                for n in range(4):
                    last = pe.transpose(tbp[u % 2][:, n * P:(n + 1) * P], PX[u][:, n, 0:P], ident)
                last.then_inc(tbp_full, 1)

            def horner(i, k, u):
                if k == 0:
                    pe.wait_ge(power_ok, 16 * i + 12 + u + 1)
                    if u < 2:
                        pe.wait_ge(qact_ok, 8 * i + 6 + u + 1)
                    else:
                        pe.wait_ge(w_ok, 12 * i + u - 1)
                else:
                    pe.wait_ge(w_ok, 12 * i + 4 * (k - 1) + u + 1)
                    pe.wait_ge(w_ok, 12 * i + 4 * k + u - 1)
                for n in range(4):
                    rhs = PX[u][:, n, P:192] if k == 0 else W[:, u, n, :]
                    last = pe.matmul(tbp[u % 2][:, n * D:(n + 1) * D], Q[u][:, n, :], rhs, start=True, stop=True)
                last.then_inc(tbp_full, 1)

            def read_out(i):
                for u in range(2):
                    pe.wait_ge(w_ok, 12 * i + 11 + u)
                    for n in range(4):
                        last = pe.matmul(tbp[u][:, n * D:(n + 1) * D], AT[:, 4 * u + n, :], W[:, u, n, :],
                                         start=True, stop=True)
                    last.then_inc(tbp_full, 1)

            def round_(i, level):
                product(i, level, 0)
                product(i, level, 1)
                turn_power(i, level, 0)
                product(i, level, 2)
                turn_power(i, level, 1)
                product(i, level, 3)
                turn_power(i, level, 2)
                turn_power(i, level, 3)

            def prologue():
                pe.wait_ge(consts_in, 16 * 5)
                frame_products(0)
                turn_normed(0)
                project_bkq(0)
                project_rk_v(0)
                project_rv(0)
                turn_keys(0)
                frame_products(1)
                turn_normed(1)
                grams(0)

            def body(i, rest, ln):
                for u in range(UNITS):
                    turn_power(i, -1, u)
                if rest is not None:
                    project_bkq(rest)
                round_(i, 0)
                if rest is not None:
                    project_rk_v(rest)
                round_(i, 1)
                if rest is not None:
                    project_rv(rest)
                round_(i, 2)
                if rest is not None:
                    turn_keys(rest)
                for u in range(UNITS):
                    product(i, 3, u)
                if ln is not None:
                    frame_products(ln)
                for u in range(UNITS):
                    horner(i, 0, u)
                for u in range(UNITS):
                    horner(i, 1, u)
                if ln is not None:
                    turn_normed(ln)
                for u in range(UNITS):
                    horner(i, 2, u)
                read_out(i)
                if rest is not None:
                    grams(rest)

            schedule(pe, prologue, body)

        @block.vector
        def _(dve):
            def norm_stats(j, n, src):
                dve.bn_stats(stats[:, n, :], src).then_inc(stats_ok, 1)
                dve.wait_ge(stats_ok, 2 * j + n + 1)
                dve.sem_inc(held, 1)
                dve.bn_aggr(meanvar[:, n, :], stats[:, n, :]).then_inc(meanvar_ok, 1)
                dve.wait_ge(meanvar_ok, 2 * j + n + 1)
                dve.tensor_scalar(vareps[:, n:n + 1], meanvar[:, n, 1:2], EPS, None, ALU.add).then_inc(vareps_ok, 1)

            def norm1_stats(j):
                dve.wait_ge(ab_full, 11 * j + 1)
                norm_stats(j, 0, ab[0][:, 0:IN])

            def norm1(j):
                dve.wait_ge(rstd_ok, 2 * j + 1)
                dve.tensor_scalar(x1[:], ab[0][:, 0:IN], meanvar[:, 0, 0:1], rstd[:, 0:1], ALU.subtract, ALU.mult)\
                    .then_inc(x1_ok, 1)
                dve.wait_ge(x1_ok, j + 1)
                if not (isinstance(j, int) and j == 0):
                    dve.wait_ge(res_out, 16 * j)
                dve.tensor_tensor(res[:], ab[0][:, 0:IN], x1[:], ALU.add).then_inc(res_ok, 1)
                norm_stats(j, 1, x1[:])

            def norm2(j):
                dve.wait_ge(rstd_ok, 2 * j + 2)
                dve.tensor_scalar(normed[:], x1[:], meanvar[:, 1, 0:1], rstd[:, 1:2], ALU.subtract, ALU.mult)\
                    .then_inc(normed_ok, 1)

            def rates(j):
                dve.wait_ge(bexp_ok, j + 1)
                dve.tensor_scalar(bexp1[:], bexp[:], 1.0, None, ALU.add).then_inc(bexp1_ok, 1)
                dve.wait_ge(bexp1_ok, j + 1)
                dve.reciprocal(rate[:], bexp1[:]).then_inc(rate_ok, 1)

            def shift(j, n, slot, use):
                src = ab[slot][:, 0:HD].rearrange("p (h d) -> p h d", h=H)
                dve.wait_ge(ab_full, 11 * j + use)
                dve.tensor_reduce(rowmax[:, n, :], src, AX_X, ALU.max).then_inc(rowmax_ok, 1)
                dve.wait_ge(rowmax_ok, 3 * j + n + 1)
                if not (isinstance(j, int) and j == 0):
                    dve.wait_ge(soft_ok, 3 * (j - 1) + n + 1)
                dve.tensor_tensor(expd[:, n, :].rearrange("p (h d) -> p h d", h=H), src,
                                  rowmax[:, n, :].unsqueeze(2).to_broadcast([P, H, D]), ALU.subtract)\
                    .then_inc(shifted_ok, 1)

            def scale_values(j):
                for n in range(2):
                    dve.wait_ge(ab_full, 11 * j + 7 + n)
                    if n == 0:
                        dve.wait_ge(rate_ok, j + 1)
                        if not (isinstance(j, int) and j == 0):
                            dve.wait_ge(x0_ok, 4 * j)
                    dve.tensor_tensor(values[:, n, :].rearrange("p (h d) -> p h d", h=H),
                                      ab[n][:, 0:HD].rearrange("p (h d) -> p h d", h=H),
                                      rate[:, n * H:(n + 1) * H].unsqueeze(2).to_broadcast([P, H, D]), ALU.mult)\
                        .then_inc(values_ok, 1)

            def sums(j, n):
                dve.wait_ge(exp_ok, 3 * j + n + 1)
                dve.tensor_reduce(rowsum[:, n, :], expd[:, n, :].rearrange("p (h d) -> p h d", h=H), AX_X, ALU.add)\
                    .then_inc(rowsum_ok, 1)
                dve.wait_ge(rowsum_ok, 3 * j + n + 1)
                dve.reciprocal(rowinv[:, n, :], rowsum[:, n, :]).then_inc(rowinv_ok, 1)

            def mask_grams(j):
                for u in range(UNITS):
                    dve.wait_ge(pxp_full, 20 * j + u + 1)
                    g = head_cols(u % 2, 256 if u < 2 else P)
                    if u < 2:
                        dve.tensor_tensor(AT[:, 4 * u:4 * u + 4, :].rearrange("p (j b) c -> p b j c", b=2), g[:, :, :, P:256],
                                          mask_causal.unsqueeze(1).unsqueeze(1).to_broadcast([P, 2, 2, P]), ALU.mult)
                    for n in range(4):
                        c = (u // 2) * H + 4 * (u % 2) + n
                        last = dve.scalar_tensor_tensor(out=PX[u][:, n, 0:P], in0=g[:, n % 2, n // 2, 0:P],
                                                        scalar=rate[:, c:c + 1], in1=mask_strict,
                                                        op0=ALU.mult, op1=ALU.mult)
                    last.then_inc(power0_ok, 1)

            def add_x(i, level, u):
                dve.wait_ge(pxp_full, 20 * i + 4 + 4 * level + u + 1)
                x = heads(PX[u][:, :, P:192])
                dve.tensor_tensor(x, head_cols(u % 2, 192)[:, :, :, P:192], x, ALU.add).then_inc(added_ok, 1)

            def copy_q(i, level, u):
                dve.wait_ge(tbp_full, 30 * i + 4 * (level + 1) + u + 1)
                dve.tensor_copy(Q[u][:].rearrange("p n c -> p (n c)"), tbp[u % 2][:]).then_inc(qdve_ok, 1)

            def add_w(i, k, u):
                dve.wait_ge(tbp_full, 30 * i + 16 + 4 * k + u + 1)
                if k == 0 and u == 2 and not (isinstance(i, int) and i == 0):
                    dve.wait_ge(u_out, 32 * i)
                dve.tensor_tensor(W[:, u, :, :], tbp[u % 2][:, 0:4 * D].rearrange("p (n d) -> p n d", n=4),
                                  PX[u][:, :, P:192], ALU.add).then_inc(w_ok, 1)

            def round_(i, level):
                add_x(i, level, 0)
                add_x(i, level, 1)
                copy_q(i, level, 0)
                add_x(i, level, 2)
                copy_q(i, level, 1)
                add_x(i, level, 3)

            def prologue():
                dve.memset(minus_half[:], -0.5).then_inc(half_set, 1)
                dve.wait_ge(consts_in, 16 * 5)
                norm1_stats(0)
                norm1(0)
                norm2(0)
                rates(0)
                shift(0, 0, 1, 4)
                shift(0, 1, 0, 5)
                shift(0, 2, 1, 6)
                scale_values(0)
                for n in range(3):
                    sums(0, n)
                norm1_stats(1)
                norm1(1)
                norm2(1)
                mask_grams(0)

            def body(i, rest, ln):
                copy_q(i, -1, 0)
                copy_q(i, -1, 1)
                if rest is not None:
                    rates(rest)
                    shift(rest, 0, 1, 4)
                round_(i, 0)
                if rest is not None:
                    shift(rest, 1, 0, 5)
                    shift(rest, 2, 1, 6)
                round_(i, 1)
                if rest is not None:
                    scale_values(rest)
                    for n in range(3):
                        sums(rest, n)
                round_(i, 2)
                for u in range(UNITS):
                    add_x(i, 3, u)
                if ln is not None:
                    norm1_stats(ln)
                for u in range(UNITS):
                    add_w(i, 0, u)
                if ln is not None:
                    norm1(ln)
                for u in range(UNITS):
                    add_w(i, 1, u)
                if ln is not None:
                    norm2(ln)
                for u in range(UNITS):
                    add_w(i, 2, u)
                if rest is not None:
                    mask_grams(rest)

            schedule(dve, prologue, body)

        @block.scalar
        def _(act):
            def scale_normedT(j):
                act.wait_ge(ab_full, 11 * j + 2)
                act.activation(normedT[:], ab[1][:, 0:P], ACT.Identity, bias=beta[:], scale=gamma[:])\
                    .then_inc(normedT_ok, 1)

            def exp_rates(j):
                act.wait_ge(ab_full, 11 * j + 3)
                act.activation(bexp[:], ab[0][:, 0:2 * H], ACT.Exp, scale=-1.0).then_inc(bexp_ok, 1)

            def exp_rows(j, n):
                act.wait_ge(shifted_ok, 3 * j + n + 1)
                act.activation(expd[:, n, :], expd[:, n, :], ACT.Exp).then_inc(exp_ok, 1)

            def copy_turned(j):
                for n in range(3):
                    act.wait_ge(ab_full, 11 * j + 9 + n)
                    dst = kqT[:, :, n, :] if n < 2 else rkT[:]
                    act.copy(dst, ab[n % 2][:].rearrange("p (c t) -> p c t", c=H // 2)).then_inc(turned_ok, 1)

            def copy_power(i, level, u):
                act.wait_ge(added_ok, 16 * i + 4 * level + u + 1)
                dst = PX[u][:, :, 0:P] if level < 3 else Q[u][:]
                act.copy(heads(dst), head_cols(u % 2, 192)[:, :, :, 0:P]).then_inc(power_ok, 1)

            def copy_q(i, level, u):
                act.wait_ge(tbp_full, 30 * i + 4 * (level + 1) + u + 1)
                act.copy(Q[u][:].rearrange("p n c -> p (n c)"), tbp[u % 2][:]).then_inc(qact_ok, 1)

            def copy_z(i):
                if not (isinstance(i, int) and i == 0):
                    act.wait_ge(z_out, 32 * i)
                for u in range(2):
                    act.wait_ge(tbp_full, 30 * i + 28 + u + 1)
                    act.copy(zrow[:, u * 4 * D:(u + 1) * 4 * D], tbp[u][:, 0:4 * D]).then_inc(z_ok, 1)

            def round_(i, level):
                for u in range(UNITS):
                    copy_power(i, level, u)
                copy_q(i, level, 2)
                copy_q(i, level, 3)

            def prologue():
                act.wait_ge(consts_in, 16 * 5)
                scale_normedT(0)
                exp_rates(0)
                for n in range(3):
                    exp_rows(0, n)
                copy_turned(0)
                scale_normedT(1)

            def body(i, rest, ln):
                copy_q(i, -1, 2)
                copy_q(i, -1, 3)
                if rest is not None:
                    exp_rates(rest)
                    exp_rows(rest, 0)
                round_(i, 0)
                if rest is not None:
                    exp_rows(rest, 1)
                    exp_rows(rest, 2)
                round_(i, 1)
                round_(i, 2)
                if rest is not None:
                    copy_turned(rest)
                for u in range(UNITS):
                    copy_power(i, 3, u)
                if ln is not None:
                    scale_normedT(ln)
                copy_z(i)

            schedule(act, prologue, body)

        @block.gpsimd
        def _(pool):
            def rstds(j):
                for n in range(2):
                    pool.wait_ge(vareps_ok, 2 * j + n + 1)
                    pool.tensor_tensor(rstd[:, n:n + 1], vareps[:, n:n + 1], minus_half[:], ALU.pow)\
                        .then_inc(rstd_ok, 1)

            def normalise(j):
                if not (isinstance(j, int) and j == 0):
                    pool.wait_ge(turned_ok, 3 * j)
                    pool.wait_ge(rk_out, 32 * j)
                for n in range(3):
                    pool.wait_ge(rowinv_ok, 3 * j + n + 1)
                    pool.tensor_tensor(soft[:, n, :].rearrange("p (h d) -> p h d", h=H),
                                       expd[:, n, :].rearrange("p (h d) -> p h d", h=H),
                                       rowinv[:, n, :].unsqueeze(2).to_broadcast([P, H, D]), ALU.mult)\
                        .then_inc(soft_ok, 1)

            def start_x(j):
                pool.wait_ge(values_ok, 2 * j + 2)
                if not (isinstance(j, int) and j == 0):
                    pool.wait_ge(w_ok, 12 * j)
                pool.sem_inc(held, 1)
                for u in range(UNITS):
                    c = (u % 2) * 4 * D
                    pool.tensor_copy(PX[u][:, :, P:192], values[:, u // 2, c:c + 4 * D]
                                     .rearrange("p (n d) -> p n d", n=4)).then_inc(x0_ok, 1)

            def prologue():
                pool.wait_ge(half_set, 1)
                rstds(0)
                normalise(0)
                rstds(1)
                start_x(0)

            def body(i, rest, ln):
                if rest is not None:
                    normalise(rest)
                if ln is not None:
                    rstds(ln)
                if rest is not None:
                    start_x(rest)

            schedule(pool, prologue, body)


def recurrence(nc, rk_d, u_d, z_d, h_d):
    with ExitStack() as ctx:
        def sb(name, shape):
            return ctx.enter_context(nc.sbuf_tensor(name, shape, F32))

        def sem(name):
            return ctx.enter_context(nc.semaphore(name))

        CH = 4
        TS = S // CH
        K = [sb(f"K{g}", [P, S, D]) for g in range(2)]
        U = [sb(f"U{g}", [P, S, D]) for g in range(2)]
        Z = [sb(f"Z{g}", [P, S, D]) for g in range(2)]
        prod = [sb(f"prod{g}", [P, S, D]) for g in range(2)]
        expo = [sb(f"expo{g}", [P, D]) for g in range(2)]
        shifted = [sb(f"shifted{g}", [P, D]) for g in range(2)]
        scores = [sb(f"scores{g}", [P, S]) for g in range(2)]
        read = [sb(f"read{g}", [P, D]) for g in range(2)]
        small = [sb(f"small{g}", [P, 3]) for g in range(2)]

        held = sem("held")
        loaded = [sem(f"loaded{c}") for c in range(CH)]
        stored = sem("stored")
        start_ok = [sem(f"start_ok{g}") for g in range(2)]
        kprod_pool = [sem(f"kprod_pool{g}") for g in range(2)]
        kprod_dve = [sem(f"kprod_dve{g}") for g in range(2)]
        score_ok = [sem(f"score_ok{g}") for g in range(2)]
        uprod_pool = [sem(f"uprod_pool{g}") for g in range(2)]
        uprod_dve = [sem(f"uprod_dve{g}") for g in range(2)]
        read_ok = [sem(f"read_ok{g}") for g in range(2)]
        h_ok = [sem(f"h_ok{g}") for g in range(2)]
        max_ok = [sem(f"max_ok{g}") for g in range(2)]
        shift_ok = [sem(f"shift_ok{g}") for g in range(2)]
        exp_ok = [sem(f"exp_ok{g}") for g in range(2)]
        inv_ok = [sem(f"inv_ok{g}") for g in range(2)]

        def pool_rows(t):
            return 0 if t < 8 else (9 * (t + 1)) // 16

        POOL_STEPS = sum(pool_rows(t) > 0 for t in range(S))
        DVE_FIRST = S - POOL_STEPS

        def chains(dram, pair, g, c):
            return dram.rearrange("(x g b) h t d -> g x (b h) (t d)", g=2, b=GROUP)[
                g, bass.ds(pair, 1), :, c * TS * D:(c + 1) * TS * D].rearrange("x p f -> (x p) f")

        def rows(t3, c):
            return t3[:, c * TS:(c + 1) * TS, :].rearrange("p t d -> p (t d)")

        block = ctx.enter_context(nc.Block())

        @block.sync
        def _(sp):
            def pair(x):
                first = isinstance(x, int) and x == 0
                for c in range(CH):
                    if not first and c == 0:
                        for g in range(2):
                            sp.wait_ge(read_ok[g], S * x)
                            sp.sem_inc(held, 1)
                        sp.wait_ge(stored, 32 * CH * x)
                        sp.sem_inc(held, 1)
                    for g in range(2):
                        for t, d in ((K, rk_d), (U, u_d), (Z, z_d)):
                            sp.dma_start(rows(t[g], c), chains(d, x, g, c)).then_inc(loaded[c], 16)
                for c in range(CH):
                    for g in range(2):
                        sp.wait_ge(h_ok[g], S * x + (c + 1) * TS)
                        sp.sem_inc(held, 1)
                        if c == CH - 1:
                            sp.wait_ge(shift_ok[g], S * x + S)
                            sp.sem_inc(held, 1)
                        sp.dma_start(chains(h_d, x, g, c), rows(Z[g], c)).then_inc(stored, 16)

            pair(0)
            with sp.Fori(1, PAIRS) as x:
                pair(x)
            sp.wait_ge(stored, 32 * CH * PAIRS)

        @block.gpsimd
        def _(pool):
            def pair(x):
                for t in range(DVE_FIRST, S):
                    n = pool_rows(t)
                    done = POOL_STEPS * x + t - DVE_FIRST
                    if t % TS == 0 or t == DVE_FIRST:
                        pool.wait_ge(loaded[t // TS], 96 * (x + 1))
                    for g in range(2):
                        pool.wait_ge(exp_ok[g], S * x + t)
                        pool.wait_ge(read_ok[g], S * x + t)
                        pool.tensor_tensor(prod[g][:, 0:n, :], K[g][:, 0:n, :],
                                           expo[g][:].unsqueeze(1).to_broadcast([P, n, D]), ALU.mult)\
                            .then_inc(kprod_pool[g], 1)
                    for g in range(2):
                        pool.wait_ge(score_ok[g], S * x + t + 1)
                        pool.tensor_tensor(prod[g][:, 0:n, :], U[g][:, 0:n, :],
                                           scores[g][:, 0:n].unsqueeze(2).to_broadcast([P, n, D]), ALU.mult)\
                            .then_inc(uprod_pool[g], 1)

            pair(0)
            with pool.Fori(1, PAIRS) as x:
                pair(x)

        @block.vector
        def _(dve):
            def pair(x):
                for g in range(2):
                    if not (isinstance(x, int) and x == 0):
                        dve.wait_ge(exp_ok[g], S * x)
                    dve.memset(expo[g][:], 1.0)
                    dve.memset(small[g][:, 2:3], 1.0 / D).then_inc(start_ok[g], 1)
                for t in range(S):
                    n = t + 1
                    m = pool_rows(t)
                    done = POOL_STEPS * x + t - DVE_FIRST + 1
                    if t % TS == 0:
                        dve.wait_ge(loaded[t // TS], 96 * (x + 1))
                    for g in range(2):
                        if t == 0:
                            dve.wait_ge(start_ok[g], x + 1)
                        else:
                            dve.wait_ge(exp_ok[g], S * x + t)
                            dve.reciprocal(small[g][:, 2:3], small[g][:, 1:2]).then_inc(inv_ok[g], 1)
                        dve.tensor_tensor(prod[g][:, m:n, :], K[g][:, m:n, :],
                                          expo[g][:].unsqueeze(1).to_broadcast([P, n - m, D]), ALU.mult)\
                            .then_inc(kprod_dve[g], 1)
                        dve.wait_ge(kprod_dve[g], S * x + t + 1)
                        if m:
                            dve.wait_ge(kprod_pool[g], done)
                        dve.tensor_reduce(scores[g][:, 0:n], prod[g][:, 0:n, :], AX_X, ALU.add)\
                            .then_inc(score_ok[g], 1)
                    for g in range(2):
                        dve.wait_ge(score_ok[g], S * x + t + 1)
                        dve.tensor_tensor(prod[g][:, m:n, :], U[g][:, m:n, :],
                                          scores[g][:, m:n].unsqueeze(2).to_broadcast([P, n - m, D]), ALU.mult)\
                            .then_inc(uprod_dve[g], 1)
                        dve.wait_ge(uprod_dve[g], S * x + t + 1)
                        if m:
                            dve.wait_ge(uprod_pool[g], done)
                        dve.tensor_reduce(read[g][:], prod[g][:, 0:n, :].rearrange("p s d -> p d s"), AX_X, ALU.add)\
                            .then_inc(read_ok[g], 1)
                        dve.wait_ge(read_ok[g], S * x + t + 1)
                        if t:
                            dve.wait_ge(inv_ok[g], (S - 1) * x + t)
                        dve.scalar_tensor_tensor(out=Z[g][:, t, :], in0=read[g][:], scalar=small[g][:, 2:3],
                                                 in1=Z[g][:, t, :], op0=ALU.mult, op1=ALU.add).then_inc(h_ok[g], 1)
                        dve.wait_ge(h_ok[g], S * x + t + 1)
                        dve.tensor_reduce(small[g][:, 0:1], Z[g][:, t, :], AX_X, ALU.max).then_inc(max_ok[g], 1)
                        dve.wait_ge(max_ok[g], S * x + t + 1)
                        dve.tensor_scalar(shifted[g][:], Z[g][:, t, :], small[g][:, 0:1], None, ALU.subtract)\
                            .then_inc(shift_ok[g], 1)

            pair(0)
            with dve.Fori(1, PAIRS) as x:
                pair(x)

        @block.scalar
        def _(act):
            def pair(x):
                for t in range(S):
                    for g in range(2):
                        act.wait_ge(shift_ok[g], S * x + t + 1)
                        act.activation(expo[g][:], shifted[g][:], ACT.Exp, accum_out=small[g][:, 1:2])\
                            .then_inc(exp_ok[g], 1)

            pair(0)
            with act.Fori(1, PAIRS) as x:
                pair(x)


def feed_forward(nc, h_d, res_d, wout_d, gatew_d, gateb_d, w1_d, b1_d, w2_d, b2_d, ident_d, out):
    with ExitStack() as ctx:
        def sb(name, shape):
            return ctx.enter_context(nc.sbuf_tensor(name, shape, F32))

        def ps(name, shape):
            return ctx.enter_context(nc.psum_tensor(name, shape, F32))

        def sem(name):
            return ctx.enter_context(nc.semaphore(name))

        T = BATCH * P
        N = TILES // BATCH
        ident = sb("ident3", [P, P])
        wout = sb("wout", [P, HD // P, IN])
        gatew = sb("gatew", [P, NE])
        gateb = sb("gateb", [P, NE])
        w1 = sb("w1", [P, EXPERTS, F])
        b1 = sb("b1", [P, EXPERTS * FC])
        w2 = sb("w2", [P, EXPERTS, FC, IN])
        b2 = sb("b2", [EXPERTS, IN])
        minus_half = sb("minus_half3", [P, BATCH])
        hs = sb("hs", [P, BATCH, HD])
        hsT = sb("hsT", [P, 2, HD // P, P])
        res = sb("res3", [P, BATCH, IN])
        acc = sb("acc", [P, BATCH, IN])
        stats = sb("stats3", [P, BATCH, 6])
        meanvar = sb("meanvar3", [P, BATCH, 2])
        vareps = sb("vareps3", [P, BATCH])
        rstd = sb("rstd3", [P, BATCH])
        x2 = sb("x2", [P, BATCH, IN])
        x2T = sb("x2T", [P, T])
        logit = sb("logit", [P, BATCH, NE])
        lmax = sb("lmax", [P, BATCH])
        lsum = sb("lsum", [P, BATCH])
        linv = sb("linv", [P, BATCH])
        lexp = sb("lexp", [P, BATCH, NE])
        prob = sb("prob", [P, BATCH, NE])
        top = sb("top", [P, BATCH, 8])
        above = sb("above", [P, BATCH, NE])
        equal = sb("equal", [P, BATCH, NE])
        rank = [sb(f"rank{n}", [P, BATCH, NE]) for n in range(3)]
        nabove = sb("nabove", [P, BATCH])
        room = sb("room", [P, BATCH, NE])
        chosen = sb("chosen", [P, BATCH, NE])
        cw = sb("cw", [P, BATCH, EXPERTS])
        cwT = sb("cwT", [EXPERTS, BATCH, P])
        hid = [sb(f"hid{n}", [P, FC, T]) for n in range(2)]

        tp = [ps(f"tp{n}", [P, 512]) for n in range(2)]
        op = ps("op", [P, 512])
        up = [ps(f"up{n}", [P, 512]) for n in range(3)]
        dn = [ps(f"dn{n}", [P, 512]) for n in range(2)]

        held = sem("held3")
        weights_in = sem("weights_in")
        consts_ok = sem("consts_ok")
        hs_in = sem("hs_in")
        res_in = sem("res_in")
        hsp_full = sem("hsp_full")
        hsT_ok = sem("hsT_ok")
        op_full = sem("op_full")
        stream_ok = sem("stream_ok")
        stats_ok = sem("stats_ok3")
        meanvar_ok = sem("meanvar_ok3")
        vareps_ok = sem("vareps_ok3")
        rstd_ok = sem("rstd_ok3")
        x2_ok = sem("x2_ok")
        x2p_full = sem("x2p_full")
        x2T_ok = sem("x2T_ok")
        logit_full = sem("logit_full")
        router = sem("router")
        lexp_ok = sem("lexp_ok")
        cw_ok = sem("cw_ok")
        cwp_full = sem("cwp_full")
        cwT_ok = sem("cwT_ok")
        bias_full = sem("bias_full")
        bias_ok = sem("bias_ok")
        up_full = sem("up_full")
        hid_ok = sem("hid_ok")
        dn_full = sem("dn_full")
        dn_read = sem("dn_read")
        out_out = sem("out_out")
        ROUTER = 14

        def schedule(eng, body):
            body(0)
            with eng.Fori(1, N - 1) as i:
                body(i)
            body(N - 1)

        block = ctx.enter_context(nc.Block())
        weights = ((ident[:], ident_d), (wout[:], wout_d), (gatew[:], gatew_d), (gateb[:], gateb_d),
                   (b1[:], b1_d), (b2[:], b2_d), (w1[:], w1_d), (w2[:], w2_d))

        @block.sync
        def _(sp):
            def load(i):
                if not (isinstance(i, int) and i == 0):
                    sp.wait_ge(hsT_ok, BATCH * i)
                    sp.sem_inc(held, 1)
                    sp.wait_ge(stream_ok, BATCH * i)
                    sp.sem_inc(held, 1)
                for k in range(BATCH):
                    for w in range(2):
                        src = h_d.rearrange("(x k w) h t d -> k w x t h d", k=BATCH, w=2)[
                            k, w, bass.ds(i, 1), :, :, :].rearrange("x t h d -> (x t) h d")
                        sp.dma_start(hs[w * S:(w + 1) * S, k, :].rearrange("p (h d) -> p h d", h=H), src)\
                            .then_inc(hs_in, 16)
                sp.dma_start(res[:], res_d[bass.ds(i * T, T), :].rearrange("(k p) d -> p k d", k=BATCH))\
                    .then_inc(res_in, 16)

            def store(i):
                last = isinstance(i, int) and i == N - 1
                m = REAL_TILES - BATCH * (N - 1) if last else BATCH
                sp.wait_ge(dn_read, EXPERTS * (i + 1))
                sp.sem_inc(held, 1)
                for w in range(2):
                    dst = out.rearrange("t (c w) d -> w t c d", w=2)[w, :, bass.ds(i * BATCH, m), :]
                    sp.dma_start(dst, acc[w * S:(w + 1) * S, 0:m, :]).then_inc(out_out, 16)

            for n, (t, d) in enumerate(weights):
                sp.dma_start(t, d).then_inc(weights_in, 16)
                if n == 3:
                    load(0)
            load(1)
            store(0)
            with sp.Fori(1, N - 1) as i:
                load(i + 1)
                store(i)
            store(N - 1)
            sp.wait_ge(out_out, 32 * N)

        @block.tensor
        def _(pe):
            def body(i):
                first = isinstance(i, int) and i == 0
                for k in range(BATCH):
                    if k == 0:
                        pe.wait_ge(hs_in, 32 * BATCH * (i + 1))
                    if k >= 2:
                        pe.wait_ge(hsT_ok, BATCH * i + k - 1)
                    elif not first:
                        if k == 0:
                            pe.wait_ge(x2T_ok, i)
                        else:
                            pe.wait_ge(cwT_ok, i)
                    for c in range(HD // P):
                        last = pe.transpose(tp[k % 2][:, c * P:(c + 1) * P], hs[:, k, c * P:(c + 1) * P], ident[:])
                    last.then_inc(hsp_full, 1)
                    if k:
                        project(i, k - 1)
                project(i, BATCH - 1)
                for k in range(BATCH):
                    pe.wait_ge(x2_ok, BATCH * i + k + 1)
                    last = pe.transpose(tp[0][:, k * P:(k + 1) * P], x2[:, k, :], ident[:])
                last.then_inc(x2p_full, 1)
                pe.wait_ge(x2T_ok, i + 1)
                for k in range(BATCH):
                    last = pe.matmul(op[:, k * NE:(k + 1) * NE], x2T[:, k * P:(k + 1) * P], gatew[:],
                                     start=True, stop=True)
                last.then_inc(logit_full, 1)
                for e in range(EXPERTS):
                    expert_up(i, e)
                    if e == 0:
                        pe.wait_ge(cw_ok, i + 1)
                        for k in range(BATCH):
                            last = pe.transpose(tp[1][0:EXPERTS, k * P:(k + 1) * P], cw[:, k, :], ident[:])
                        last.then_inc(cwp_full, 1)
                        pe.wait_ge(cwT_ok, i + 1)
                        for k in range(BATCH):
                            last = pe.matmul(op[:, k * IN:(k + 1) * IN], cwT[:, k, :], b2[:], start=True, stop=True)
                        last.then_inc(bias_full, 1)
                    if e:
                        expert_down(i, e - 1)
                expert_down(i, EXPERTS - 1)

            def project(i, k):
                pe.wait_ge(hsT_ok, BATCH * i + k + 1)
                if k:
                    pe.wait_ge(stream_ok, BATCH * i + k)
                elif not (isinstance(i, int) and i == 0):
                    pe.wait_ge(bias_ok, i)
                for c in range(HD // P):
                    last = pe.matmul(op[:, 0:IN], hsT[:, k % 2, c, :], wout[:, c, :],
                                     start=(c == 0), stop=(c == HD // P - 1))
                last.then_inc(op_full, 1)

            def expert_up(i, e):
                for f in range(FC):
                    n = e * FC + f
                    slot = n % 3
                    if n >= 3:
                        pe.wait_ge(hid_ok, EXPERTS * FC * i + n - 2)
                    elif not (isinstance(i, int) and i == 0):
                        pe.wait_ge(hid_ok, EXPERTS * FC * i)
                    pe.matmul(up[slot][:], w1[:, e, f * P:(f + 1) * P], x2T[:], start=True, stop=True)\
                        .then_inc(up_full, 1)

            def expert_down(i, e):
                pe.wait_ge(hid_ok, EXPERTS * FC * i + (e + 1) * FC)
                if e >= 2:
                    pe.wait_ge(dn_read, EXPERTS * i + e - 1)
                elif not (isinstance(i, int) and i == 0):
                    pe.wait_ge(dn_read, EXPERTS * i + e - 1)
                for k in range(BATCH):
                    for f in range(FC):
                        last = pe.matmul(dn[e % 2][:, k * IN:(k + 1) * IN], hid[e % 2][:, f, k * P:(k + 1) * P],
                                         w2[:, e, f, :], start=(f == 0), stop=(f == FC - 1))
                last.then_inc(dn_full, 1)

            pe.wait_ge(weights_in, 16 * len(weights))
            schedule(pe, body)

        @block.scalar
        def _(act):
            def body(i):
                for k in range(BATCH):
                    act.wait_ge(hsp_full, BATCH * i + k + 1)
                    if k >= 2:
                        act.wait_ge(op_full, BATCH * i + k - 1)
                    act.copy(hsT[:, k % 2, :, :].rearrange("p c t -> p (c t)"), tp[k % 2][:]).then_inc(hsT_ok, 1)
                act.wait_ge(x2p_full, i + 1)
                act.copy(x2T[:], tp[0][:]).then_inc(x2T_ok, 1)
                act.wait_ge(router, ROUTER * i + 3)
                act.activation(lexp[:].rearrange("p k e -> p (k e)"), logit[:].rearrange("p k e -> p (k e)"),
                               ACT.Exp).then_inc(lexp_ok, 1)
                for e in range(EXPERTS):
                    for f in range(FC):
                        n = e * FC + f
                        act.wait_ge(up_full, EXPERTS * FC * i + n + 1)
                        if f == 0 and e >= 2:
                            act.wait_ge(dn_full, EXPERTS * i + e - 1)
                        act.activation(hid[e % 2][:, f, :], up[n % 3][:], ACT.Gelu, bias=b1[:, n:n + 1])\
                            .then_inc(hid_ok, 1)

            act.wait_ge(weights_in, 16 * len(weights))
            schedule(act, body)

        @block.gpsimd
        def _(pool):
            def body(i):
                pool.wait_ge(vareps_ok, i + 1)
                pool.tensor_tensor(rstd[:], vareps[:], minus_half[:], ALU.pow).then_inc(rstd_ok, 1)

            pool.wait_ge(consts_ok, 2)
            schedule(pool, body)

        @block.vector
        def _(dve):
            def body(i):
                first = isinstance(i, int) and i == 0
                dve.wait_ge(res_in, 16 * (i + 1))
                if not first:
                    dve.wait_ge(out_out, 32 * i)
                for k in range(BATCH):
                    dve.wait_ge(op_full, BATCH * i + k + 1)
                    dve.tensor_tensor(acc[:, k, :], op[:, 0:IN], res[:, k, :], ALU.add).then_inc(stream_ok, 1)
                    dve.wait_ge(stream_ok, BATCH * i + k + 1)
                    dve.bn_stats(stats[:, k, :], acc[:, k, :]).then_inc(stats_ok, 1)
                    dve.wait_ge(stats_ok, BATCH * i + k + 1)
                    dve.sem_inc(held, 1)
                    dve.bn_aggr(meanvar[:, k, :], stats[:, k, :]).then_inc(meanvar_ok, 1)
                dve.wait_ge(meanvar_ok, BATCH * i + BATCH)
                dve.tensor_scalar(vareps[:], meanvar[:, :, 1], EPS, None, ALU.add).then_inc(vareps_ok, 1)
                dve.wait_ge(rstd_ok, i + 1)
                for k in range(BATCH):
                    dve.tensor_scalar(x2[:, k, :], acc[:, k, :], meanvar[:, k, 0:1], rstd[:, k:k + 1],
                                      ALU.subtract, ALU.mult).then_inc(x2_ok, 1)
                dve.wait_ge(logit_full, i + 1)
                route(i)
                dve.wait_ge(bias_full, i + 1)
                dve.tensor_tensor(acc[:].rearrange("p k d -> p (k d)"), op[:],
                                  acc[:].rearrange("p k d -> p (k d)"), ALU.add).then_inc(bias_ok, 1)
                dve.wait_ge(bias_ok, i + 1)
                for e in range(EXPERTS):
                    dve.wait_ge(dn_full, EXPERTS * i + e + 1)
                    if e:
                        dve.wait_ge(dn_read, EXPERTS * i + e)
                    for k in range(BATCH):
                        last = dve.scalar_tensor_tensor(out=acc[:, k, :], in0=dn[e % 2][:, k * IN:(k + 1) * IN],
                                                        scalar=cw[:, k, e:e + 1], in1=acc[:, k, :],
                                                        op0=ALU.mult, op1=ALU.add)
                    last.then_inc(dn_read, 1)

            def route(i):
                def wide(a):
                    return a.unsqueeze(2).to_broadcast([P, BATCH, NE])

                r = ROUTER * i
                dve.tensor_tensor(logit[:], op[:, 0:BATCH * NE].rearrange("p (k e) -> p k e", k=BATCH),
                                  gateb[:].unsqueeze(1).to_broadcast([P, BATCH, NE]), ALU.add).then_inc(router, 1)
                dve.wait_ge(router, r + 1)
                dve.tensor_reduce(lmax[:], logit[:], AX_X, ALU.max).then_inc(router, 1)
                dve.wait_ge(router, r + 2)
                dve.tensor_tensor(logit[:], logit[:], wide(lmax[:]), ALU.subtract).then_inc(router, 1)
                dve.wait_ge(lexp_ok, i + 1)
                dve.tensor_reduce(lsum[:], lexp[:], AX_X, ALU.add).then_inc(router, 1)
                dve.wait_ge(router, r + 4)
                dve.reciprocal(linv[:], lsum[:]).then_inc(router, 1)
                dve.wait_ge(router, r + 5)
                dve.tensor_tensor(prob[:], lexp[:], wide(linv[:]), ALU.mult).then_inc(router, 1)
                dve.wait_ge(router, r + 6)
                dve.sem_inc(held, 1)
                for k in range(BATCH):
                    last = dve.max(top[:, k, :], prob[:, k, :])
                last.then_inc(router, 1)
                dve.wait_ge(router, r + 7)
                dve.tensor_tensor(above[:], prob[:], wide(top[:, :, 1]), ALU.is_gt)
                dve.tensor_tensor(equal[:], prob[:], wide(top[:, :, 1]), ALU.is_equal).then_inc(router, 1)
                dve.wait_ge(router, r + 8)
                dve.tensor_reduce(nabove[:], above[:], AX_X, ALU.add)
                src = equal
                for n, step in enumerate((1, 2, 4)):
                    dve.tensor_copy(rank[n][:, :, 0:step], src[:, :, 0:step])
                    dve.tensor_tensor(rank[n][:, :, step:NE], src[:, :, step:NE], src[:, :, 0:NE - step],
                                      ALU.add).then_inc(router, 1)
                    dve.wait_ge(router, r + 9 + n)
                    src = rank[n]
                dve.tensor_tensor(room[:], rank[2][:], wide(nabove[:]), ALU.add).then_inc(router, 1)
                dve.wait_ge(router, r + 12)
                dve.scalar_tensor_tensor(out=chosen[:].rearrange("p k e -> p (k e)"),
                                         in0=room[:].rearrange("p k e -> p (k e)"), scalar=2.0,
                                         in1=equal[:].rearrange("p k e -> p (k e)"),
                                         op0=ALU.is_le, op1=ALU.mult).then_inc(router, 1)
                dve.wait_ge(router, r + 13)
                dve.tensor_tensor(chosen[:], chosen[:], above[:], ALU.add).then_inc(router, 1)
                dve.wait_ge(router, r + 14)
                dve.tensor_tensor(cw[:, :, 0:NE], chosen[:], prob[:], ALU.mult).then_inc(cw_ok, 1)
                dve.wait_ge(cwp_full, i + 1)
                dve.tensor_copy(cwT[:].rearrange("e k p -> e (k p)"), tp[1][0:EXPERTS, :]).then_inc(cwT_ok, 1)

            dve.memset(minus_half[:], -0.5).then_inc(consts_ok, 1)
            dve.memset(cw[:], 1.0).then_inc(consts_ok, 1)
            dve.wait_ge(weights_in, 16 * len(weights))
            dve.wait_ge(consts_ok, 2)
            schedule(dve, body)


def audio_tower(nc, frames, mdct, wslow, gamma, beta, masks, wout, gatew, gateb, w1, b1, w2, b2, ident, out):
    chain_shape = [FRAMES, H, S, D]
    res_d = nc.dram_tensor("res_scratch", [TILES * P, IN], F32, kind="Internal").ap()
    rk_d = nc.dram_tensor("rk_scratch", chain_shape, F32, kind="Internal").ap()
    u_d = nc.dram_tensor("u_scratch", chain_shape, F32, kind="Internal").ap()
    z_d = nc.dram_tensor("z_scratch", chain_shape, F32, kind="Internal").ap()
    h_d = nc.dram_tensor("h_scratch", chain_shape, F32, kind="Internal").ap()
    delta_rule_tiles(nc, frames, mdct, wslow, gamma, beta, masks, res_d, rk_d, u_d, z_d)
    recurrence(nc, rk_d, u_d, z_d, h_d)
    feed_forward(nc, h_d, res_d, wout, gatew, gateb, w1, b1, w2, b2, ident, out)


def mdct_matrix():
    length = 2 * HOP
    half = length // 2
    f32 = np.float32
    n = np.arange(length, dtype=f32) + f32(0.5)
    k = f32(np.pi / half) * n[:half]
    n = n + f32(half / 2)
    z = np.sqrt(f32(2.0 / half * 2.0))
    m = z * np.cos(n[:, None] * k[None, :])
    w = np.sin(f32(np.pi) * (np.arange(length, dtype=f32) + f32(0.5)) / f32(length))
    return (w[:, None] * m).astype(f32)


def mask_tables():
    t = np.arange(P)
    same = (t[:, None] // S) == (t[None, :] // S)
    ident = np.eye(P)
    strict = -(same & (t[None, :] < t[:, None])).astype(np.float64)
    causal = (same & (t[:, None] <= t[None, :])).astype(np.float64)
    return np.ascontiguousarray(np.stack([ident, strict, causal], 1).astype(np.float32))


def kernel(x, L0_attn_W_slow, L0_attn_W_out, L0_attn_ln_gamma, L0_attn_ln_beta, L0_ffn_gate_w, L0_ffn_gate_b,
           L0_ffn_sw1, L0_ffn_sb1, L0_ffn_sw2, L0_ffn_sb2, L0_ffn_rw1, L0_ffn_rb1, L0_ffn_rw2, L0_ffn_rb2):
    import concourse.bacc as bacc
    from concourse.bass_utils import run_bass_kernel_spmd

    arr = np.asarray
    x = arr(x)
    blocks = FRAMES + 1
    xp = np.zeros((S, blocks * HOP), x.dtype)
    xp[:, HOP:HOP + LEN] = x
    frames = xp.reshape(S, blocks, HOP).transpose(2, 1, 0).reshape(HOP, blocks * S)
    mdct = mdct_matrix().reshape(2, HOP, IN).transpose(1, 0, 2)
    ws = arr(L0_attn_W_slow).reshape(H, 5 * D + 2, IN)
    part = [ws[:, n * D:(n + 1) * D].reshape(HD, IN) for n in (1, 0, 3, 2, 4)]
    wslow = np.concatenate(part + [ws[:, 5 * D], ws[:, 5 * D + 1]], 0).T
    wout = arr(L0_attn_W_out).T.reshape(HD // P, P, IN).transpose(1, 0, 2)
    w1 = np.concatenate([arr(L0_ffn_rw1), arr(L0_ffn_sw1)], 0).transpose(2, 0, 1)
    b1 = np.concatenate([arr(L0_ffn_rb1), arr(L0_ffn_sb1)], 0).reshape(EXPERTS * FC, P).T
    w2 = np.concatenate([arr(L0_ffn_rw2), arr(L0_ffn_sw2)], 0).reshape(EXPERTS, IN, FC, P).transpose(3, 0, 2, 1)
    b2 = np.concatenate([arr(L0_ffn_rb2), arr(L0_ffn_sb2)], 0)
    gateb = np.broadcast_to(arr(L0_ffn_gate_b)[None, :], (P, NE))
    arrays = {
        "frames": frames, "mdct": mdct, "wslow": wslow, "gamma": arr(L0_attn_ln_gamma).reshape(IN, 1),
        "beta": arr(L0_attn_ln_beta).reshape(IN, 1), "masks": mask_tables(), "wout": wout,
        "gatew": arr(L0_ffn_gate_w).T, "gateb": gateb, "w1": w1, "b1": b1, "w2": w2, "b2": b2,
        "ident": np.eye(P, dtype=np.float32),
    }
    nc = bacc.Bacc("TRN2", target_bir_lowering=False, num_devices=1)
    named, args = {}, []
    for name, a in arrays.items():
        a = np.ascontiguousarray(a)
        named[f"in_{name}"] = a
        args.append(nc.dram_tensor(f"in_{name}", a.shape, mybir.dt.from_np(a.dtype), kind="ExternalInput").ap())
    args.append(nc.dram_tensor("out_0", (S, NF, IN), F32, kind="ExternalOutput").ap())
    audio_tower(nc, *args)
    r = run_bass_kernel_spmd(nc, [named], core_ids=[0])
    return r.results[0]["out_0"]
```

```python
from contextlib import ExitStack

import concourse.bass as bass
import numpy as np
from concourse import mybir

F32 = mybir.dt.float32
ALU = mybir.AluOpType
ACT = mybir.ActivationFunctionType
AX_X = mybir.AxisListType.X

P = 128
S, NF = 64, 158
LEN = 20000
HOP = 128
IN = 128
H, D = 8, 64
HD = H * D
NE, NSH, F = 8, 2, 512
EXPERTS = NE + NSH
FC = F // P
TILES = 80
REAL_TILES = NF // 2
FRAMES = 2 * TILES
UNITS = 4
GROUP = 16
PAIRS = FRAMES // GROUP // 2
PT = GROUP
POOL_SHARE = 12
HEAD_STEPS = 8

TURN0, ROUND, KEYS, LAST, TEMP, NORMED, READOUT, RING_USES = 0, 4, 28, 31, 35, 37, 38, 39
OWN_USES = RING_USES - 4
M_USE = (0, 1, 3, 5)
T_USE = (2, 4, 6, 7)

KEY, SCORE, VALUE, STATE = range(4)
PARTS = [(kind, t, g) for t in range(S) for kind in (KEY, SCORE, VALUE, STATE) for g in range(2)]


def part_weight(kind, t):
    return (1.0, 1.0, 1.0, 6.0)[kind] + (t + 1) * ((0.35, 1.0, 0.35, 1.0)[kind] if t >= 8 else 1.0) * 0.6


PART_START = np.cumsum([0.0] + [part_weight(kind, t) for kind, t, _ in PARTS])
TILE_0_END = PART_START[8 * HEAD_STEPS]


def position(k, f):
    if k == 0:
        return TILE_0_END * max(0.0, (f - LOAD_PART) / (1 - LOAD_PART))
    return TILE_0_END + (PART_START[-1] - TILE_0_END) * (k - 1 + f) / (PT - 1)


def parts_between(k, f, until):
    if k is None:
        return []
    a, b = position(k, f), position(k, until)
    return [p for p, start in zip(PARTS, PART_START) if a - 1e-6 <= start < b - 1e-6]


LOAD_PART = 0.25
STEPS_DONE = [sum(1 for p, start in zip(PARTS, PART_START) if p[0] == STATE and p[2] == 1
                  and start < position(k, 1.0) - 1e-6) for k in range(PT)]

BATCH = 4
EPS = 1e-5

COL = {"k": 0, "q": HD, "rk": 2 * HD, "v": 3 * HD, "rv": 4 * HD, "b": 5 * HD}
PROJ = 5 * HD + 2 * H


def tiles_and_recurrence(nc, frames_d, mdct_d, wslow_d, gamma_d, beta_d, masks_d, res_d, rk_d, u_d, z_d, h_d):
    with ExitStack() as ctx:
        def sb(name, shape):
            return ctx.enter_context(nc.sbuf_tensor(name, shape, F32))

        def ps(name, shape):
            return ctx.enter_context(nc.psum_tensor(name, shape, F32))

        def sem(name):
            return ctx.enter_context(nc.semaphore(name))

        wslow = sb("wslow", [P, PROJ])
        mdct = sb("mdct", [P, 2, IN])
        gamma = sb("gamma", [P, 1])
        beta = sb("beta", [P, 1])
        masks = sb("masks", [P, 3, P])
        ident, mask_strict, mask_causal = masks[:, 0, :], masks[:, 1, :], masks[:, 2, :]
        minus_half = sb("minus_half", [P, 1])
        frames = sb("frames", [P, 3 * S])
        stats = sb("stats", [P, 2, 6])
        meanvar = sb("meanvar", [P, 2, 2])
        vareps = sb("vareps", [P, 2])
        rstd = sb("rstd", [P, 2])
        x1 = sb("x1", [P, IN])
        res = sb("res", [P, IN])
        normed = sb("normed", [P, IN])
        normedT = sb("normedT", [P, P])
        bexp = sb("bexp", [P, 2 * H])
        bexp1 = sb("bexp1", [P, 2 * H])
        rate = sb("rate", [P, 2 * H])
        rowmax = sb("rowmax", [P, 3, H])
        rowsum = sb("rowsum", [P, 3, H])
        rowinv = sb("rowinv", [P, 3, H])
        expd = sb("expd", [P, 3, HD])
        soft = sb("soft", [P, 3, HD])
        values = sb("values", [P, 2, HD])
        kqT = sb("kqT", [P, H // 2, 2, P])
        rkT = sb("rkT", [P, H // 2, P])
        PW = [sb(f"PW{u}", [P, 4, P]) for u in range(UNITS)]
        Q = [sb(f"Q{u}", [P, 4, P]) for u in range(UNITS)]
        X = [sb(f"X{n}", [P, H, D]) for n in range(2)]
        T16 = [sb(f"T16{n}", [P, H, D]) for n in range(2)]
        AT = sb("AT", [P, H, P])
        zrow = sb("zrow", [P, HD])

        K = [sb(f"K{g}", [P, S, D]) for g in range(2)]
        U = [sb(f"U{g}", [P, S, D]) for g in range(2)]
        Z = [sb(f"Z{g}", [P, S, D]) for g in range(2)]
        prod = [sb(f"prod{g}", [P, S, D]) for g in range(2)]
        expo = [sb(f"expo{g}", [P, D]) for g in range(2)]
        shifted = [sb(f"shifted{g}", [P, D]) for g in range(2)]
        scores = [sb(f"scores{g}", [P, S]) for g in range(2)]
        read = [sb(f"read{g}", [P, D]) for g in range(2)]
        hmax = [sb(f"hmax{g}", [P, 1]) for g in range(2)]
        esum = [sb(f"esum{g}", [P, 1]) for g in range(2)]
        einv = [sb(f"einv{g}", [P, 1]) for g in range(2)]

        ab = [ps(f"ab{n}", [P, 512]) for n in range(3)]
        ring = [ps(f"ring{n}", [P, 512]) for n in range(3)]
        xps = [ps(f"xps{n}", [P, H, D]) for n in range(2)]

        held = sem("held")
        consts_in = sem("consts_in")
        half_set = sem("half_set")
        frames_in = sem("frames_in")
        mdct_full = sem("mdct_full")
        proj_full = sem("proj_full")
        gram_full = sem("gram_full")
        normed_full = sem("normed_full")
        keys_full = sem("keys_full")
        stats_ok = sem("stats_ok")
        meanvar_ok = sem("meanvar_ok")
        vareps_ok = sem("vareps_ok")
        rstd_ok = sem("rstd_ok")
        x1_ok = sem("x1_ok")
        res_ok = sem("res_ok")
        normed_ok = sem("normed_ok")
        normedT_ok = sem("normedT_ok")
        bexp_ok = sem("bexp_ok")
        bexp1_ok = sem("bexp1_ok")
        rate_ok = sem("rate_ok")
        rowmax_ok = sem("rowmax_ok")
        shifted_ok = sem("shifted_ok")
        exp_ok = sem("exp_ok")
        rowsum_ok = sem("rowsum_ok")
        rowinv_ok = sem("rowinv_ok")
        soft_ok = sem("soft_ok")
        values_ok = sem("values_ok")
        turned_ok = sem("turned_ok")
        masked_ok = sem("masked_ok")
        ring_full = sem("ring_full")
        ring_read = sem("ring_read")
        x_full = sem("x_full")
        x_ok = sem("x_ok")
        res_out = sem("res_out")
        rk_out = sem("rk_out")
        u_out = sem("u_out")
        z_out = sem("z_out")
        loaded = [sem(f"loaded{c}") for c in range(2)]
        h_out = sem("h_out")

        def two(name):
            return [sem(f"{name}{g}") for g in range(2)]

        start_ok = two("start_ok")
        kprod_pool = two("kprod_pool")
        uprod_pool = two("uprod_pool")
        kprod_ok = two("kprod_ok")
        score_ok = two("score_ok")
        uprod_ok = two("uprod_ok")
        read_ok = two("read_ok")
        h_ok = two("h_ok")
        hmax_ok = two("hmax_ok")
        hshift_ok = two("hshift_ok")
        hexp_ok = two("hexp_ok")
        einv_ok = two("einv_ok")

        def pool_rows(t):
            return 0 if t < POOL_FIRST else ((t + 1) * POOL_SHARE) // 16

        POOL_FIRST = 8
        POOL_STEPS = S - POOL_FIRST

        def own(use):
            return use - 3 * (use > KEYS) - (use > NORMED)

        def exists(i, use):
            if not isinstance(i, int):
                return True
            ahead = 1 if KEYS <= use < KEYS + 3 else 2 if use == NORMED else 0
            return 0 <= i + ahead < TILES

        def ring_taker(i, use):
            use -= 3
            while True:
                if use < 0:
                    i, use = i - 1, use + RING_USES
                if isinstance(i, int) and i < -2:
                    return None
                if exists(i, use):
                    break
                use -= 3
            if KEYS <= use < KEYS + 3:
                return turned_ok, 3 * (i + 1) + use - KEYS + 1
            if use == NORMED:
                return normedT_ok, i + 2 + 1
            return ring_read, OWN_USES * i + own(use) + 1

        def schedule(eng, prologue, body, between, alone):
            prologue()
            body(0, 1, 2, None, None)
            with eng.Fori(1, PT) as i:
                body(i, i + 1, i + 2, None, None)
            between(0)
            with eng.Fori(0, PAIRS - 2) as x:
                for k in range(PT):
                    i = (x + 1) * PT + k
                    body(i, i + 1, i + 2, x, k)
                between(x + 1)
            for k in range(PT):
                i = TILES - PT + k
                body(i, i + 1 if i + 1 < TILES else None, i + 2 if i + 2 < TILES else None, PAIRS - 2, k)
            between(PAIRS - 1)
            for k in range(PT):
                alone(PAIRS - 1, k)

        block = ctx.enter_context(nc.Block())

        @block.sync
        def _(sp):
            def load_frames(j):
                if not (isinstance(j, int) and j == 0):
                    sp.wait_ge(mdct_full, j)
                    sp.sem_inc(held, 1)
                sp.dma_start(frames[:], frames_d[:, bass.ds(j * 2 * S, 3 * S)]).then_inc(frames_in, 16)

            def per_chain(dram, j, w):
                return dram.rearrange("(j w) h t d -> w j t h d", w=2)[w, bass.ds(j, 1), :, :, :]\
                    .rearrange("j t h d -> (j t) h d")

            def store_rk(j):
                sp.wait_ge(soft_ok, 3 * j + 3)
                sp.sem_inc(held, 1)
                for w in range(2):
                    sp.dma_start(per_chain(rk_d, j, w), soft[w * S:(w + 1) * S, 2, :]
                                 .rearrange("p (h d) -> p h d", h=H)).then_inc(rk_out, 16)

            def store_res(j):
                sp.wait_ge(res_ok, j + 1)
                sp.sem_inc(held, 1)
                sp.dma_start(res_d[bass.ds(j * P, P), :], res[:]).then_inc(res_out, 16)

            def prologue():
                for t, d in ((mdct[:], mdct_d), (masks[:], masks_d), (gamma[:], gamma_d), (beta[:], beta_d),
                             (wslow[:], wslow_d)):
                    sp.dma_start(t, d).then_inc(consts_in, 16)
                load_frames(0)
                store_res(0)
                load_frames(1)
                store_rk(0)
                store_res(1)

            def chains(dram, x, g, t, n):
                return dram.rearrange("(x g b) h t d -> g x (b h) (t d)", g=2, b=GROUP)[
                    g, bass.ds(x, 1), :, t * D:(t + n) * D].rearrange("x p f -> (x p) f")

            def load_pair(x):
                for s in (rk_out, u_out, z_out):
                    sp.wait_ge(s, 32 * PT * (x + 1))
                    sp.sem_inc(held, 1)
                if not (isinstance(x, int) and x == 0):
                    for g in range(2):
                        sp.wait_ge(read_ok[g], S * x)
                        sp.sem_inc(held, 1)
                    sp.wait_ge(h_out, 32 * PT * x)
                    sp.sem_inc(held, 1)
                for c, (t, n) in enumerate(((0, HEAD_STEPS), (HEAD_STEPS, S - HEAD_STEPS))):
                    for g in range(2):
                        for sbuf, dram in ((K, rk_d), (U, u_d), (Z, z_d)):
                            sp.dma_start(sbuf[g][:, t:t + n, :].rearrange("p t d -> p (t d)"),
                                         chains(dram, x, g, t, n)).then_inc(loaded[c], 16)

            def store_h(x, k):
                done, before = STEPS_DONE[k], STEPS_DONE[k - 1] if k else 0
                for g in range(2):
                    sp.wait_ge(h_ok[g], S * x + done)
                    sp.sem_inc(held, 1)
                    if done < S:
                        sp.wait_ge(hshift_ok[g], (S - 1) * x + done)
                        sp.sem_inc(held, 1)
                    sp.dma_start(chains(h_d, x, g, before, done - before),
                                 Z[g][:, before:done, :].rearrange("p t d -> p (t d)")).then_inc(h_out, 16)

            def body(i, rest, ln, x, k):
                if ln is not None:
                    load_frames(ln)
                if rest is not None:
                    store_rk(rest)
                if ln is not None:
                    store_res(ln)
                sp.wait_ge(x_ok, 12 * i + 12)
                sp.sem_inc(held, 1)
                for w in range(2):
                    sp.dma_start(per_chain(u_d, i, w), X[1][w * S:(w + 1) * S, :, :]).then_inc(u_out, 16)
                sp.wait_ge(ring_read, OWN_USES * (i + 1))
                sp.sem_inc(held, 1)
                for w in range(2):
                    sp.dma_start(per_chain(z_d, i, w), zrow[w * S:(w + 1) * S, :]
                                 .rearrange("p (h d) -> p h d", h=H)).then_inc(z_out, 16)
                if k is not None:
                    store_h(x, k)

            schedule(sp, prologue, body, load_pair, store_h)
            sp.wait_ge(res_out, 16 * TILES)
            sp.wait_ge(rk_out, 32 * TILES)
            sp.wait_ge(u_out, 32 * TILES)
            sp.wait_ge(z_out, 32 * TILES)
            sp.wait_ge(h_out, 32 * PT * PAIRS)

        @block.tensor
        def _(pe):
            def project(j, name, slot):
                c = COL[name]
                n = 2 * H if name == "b" else HD
                pe.matmul(ab[slot][:, 0:n], normedT[:], wslow[:, c:c + n], start=True, stop=True)\
                    .then_inc(proj_full, 1)

            def frame_products(j):
                pe.wait_ge(frames_in, 16 * (j + 1))
                if not (isinstance(j, int) and j == 0):
                    pe.wait_ge(shifted_ok, 3 * j)
                pe.matmul(ab[1][:, 0:IN], frames[:, 0:P], mdct[:, 0, :], start=True, stop=False)
                pe.matmul(ab[1][:, 0:IN], frames[:, S:S + P], mdct[:, 1, :], start=False, stop=True)\
                    .then_inc(mdct_full, 1)

            def turn_normed(j):
                pe.wait_ge(normed_ok, j + 1)
                bank = take_ring(j - 2, NORMED)
                pe.transpose(bank[:, 0:P], normed[:], ident).then_inc(normed_full, 1)

            def project_bkq(j):
                pe.wait_ge(normedT_ok, j + 1)
                if isinstance(j, int) and j == 0:
                    pe.wait_ge(res_ok, 1)
                else:
                    pe.wait_ge(masked_ok, 6 * (j - 1) + 4)
                project(j, "b", 1)
                project(j, "k", 2)
                project(j, "q", 0)

            def project_rk_v(j):
                pe.wait_ge(bexp_ok, j + 1)
                project(j, "rk", 1)
                pe.wait_ge(shifted_ok, 3 * j + 1)
                project(j, "v", 2)

            def project_rv(j):
                pe.wait_ge(shifted_ok, 3 * j + 2)
                project(j, "rv", 0)

            def turn_keys(j):
                for n in range(3):
                    pe.wait_ge(soft_ok, 3 * j + n + 1)
                    bank = take_ring(j - 1, KEYS + n)
                    for c in range(H // 2):
                        last = pe.transpose(bank[:, c * P:(c + 1) * P], soft[:, n, c * P:(c + 1) * P], ident)
                    last.then_inc(keys_full, 1)

            def take_ring(i, use):
                before = ring_taker(i, use)
                if before:
                    pe.wait_ge(*before)
                return ring[use % 3]

            def gram(slot, lhs, rhs, odd):
                rows = slice(odd * D, odd * D + D)
                for c in range(H // 2):
                    last = pe.matmul(ab[slot][:, c * P:(c + 1) * P], lhs[rows, c, :], rhs[rows, c, :],
                                     start=True, stop=True)
                last.then_inc(gram_full, 1)

            def causal_grams(j, odd):
                if odd == 0:
                    if isinstance(j, int) and j == TILES - 1:
                        pe.wait_ge(masked_ok, 6 * j + 2)
                    else:
                        pe.wait_ge(values_ok, 2 * (j + 1) + 1)
                else:
                    if isinstance(j, int) and j == TILES - 1:
                        pe.wait_ge(masked_ok, 6 * j + 3)
                    else:
                        pe.wait_ge(values_ok, 2 * (j + 1) + 2)
                gram((2, 0)[odd], kqT[:, :, 0, :], kqT[:, :, 1, :], odd)

            def strict_grams(j, system):
                first = isinstance(j, int) and j == 0
                pe.wait_ge(turned_ok, 3 * j + (1, 3)[system])
                if system == 0:
                    if first:
                        pe.wait_ge(res_ok, 2)
                        pe.wait_ge(values_ok, 1)
                    else:
                        if not (isinstance(j, int) and j == TILES - 1):
                            pe.wait_ge(res_ok, j + 2)
                        pe.wait_ge(masked_ok, 6 * (j - 1) + 5)
                    src = kqT[:, :, 0, :]
                    gram(1, src, src, 0)
                    gram(2, src, src, 1)
                else:
                    if first:
                        pe.wait_ge(values_ok, 2)
                    else:
                        pe.wait_ge(masked_ok, 6 * (j - 1) + 6)
                    gram(0, rkT, rkT, 0)
                    pe.wait_ge(masked_ok, 6 * j + 1)
                    gram(1, rkT, rkT, 1)

            def start_x(j):
                pe.wait_ge(values_ok, 2 * j + 2)
                if not (isinstance(j, int) and j == 0):
                    pe.wait_ge(x_ok, 12 * j)
                for n in range(2):
                    pe.matmul(xps[n][:].rearrange("p h d -> p (h d)"), ident, values[:, n, :], start=True, stop=False,
                              skip_group_check=True)

            def add_power(u, n, rhs, last):
                h = 4 * (u % 2) + n
                return pe.matmul(xps[u // 2][:, h, :], Q[u][:, n, :], rhs, start=False, stop=last,
                                 skip_group_check=True)

            def product(i, level, u):
                use = ROUND + 8 * level + M_USE[u] if level < 3 else LAST + u
                q_use = TURN0 + u if level == 0 else ROUND + 8 * (level - 1) + T_USE[u]
                pe.wait_ge(ring_read, OWN_USES * i + own(q_use) + 1)
                if level:
                    pe.wait_ge(x_ok, 12 * i + 2 * (level - 1) + u // 2 + 1)
                bank = take_ring(i, use)
                for n in range(4):
                    h = 4 * (u % 2) + n
                    o = bank[:, n * P:(n + 1) * P]
                    rhs = X[u // 2][:, h, :] if level else values[:, u // 2, h * D:(h + 1) * D]
                    mm = add_power(u, n, rhs, False)
                    if level < 3:
                        sq = pe.matmul(o, Q[u][:, n, :], PW[u][:, n, :], start=True, stop=True)
                    else:
                        sq = pe.matmul(o, PW[u][:, n, :], Q[u][:, n, :], start=True, stop=True)
                    if n == 3:
                        sq.then_inc(ring_full, 1)
                        if u % 2:
                            mm.then_inc(x_full, 1)

            def turn_power(i, level, u):
                if level == -1:
                    pe.wait_ge(masked_ok, 6 * i + 2 * (u // 2) + 2)
                    use = TURN0 + u
                else:
                    pe.wait_ge(ring_read, OWN_USES * i + own(ROUND + 8 * level + M_USE[u]) + 1)
                    use = ROUND + 8 * level + T_USE[u]
                bank = take_ring(i, use)
                for n in range(4):
                    last = pe.transpose(bank[:, n * P:(n + 1) * P], PW[u][:, n, :], ident)
                last.then_inc(ring_full, 1)

            def add_16th(i, s, rhs, last):
                for u in (2 * s, 2 * s + 1):
                    for n in range(4):
                        mm = add_power(u, n, rhs[:, 4 * (u % 2) + n, :], last)
                mm.then_inc(x_full, 1)

            def finish_x(i, stage, s):
                if stage == 4:
                    pe.wait_ge(ring_read, OWN_USES * i + own(LAST + 2 * s + 1) + 1)
                    pe.wait_ge(x_ok, 12 * i + 6 + s + 1)
                    add_16th(i, s, X[s], False)
                elif stage == 5:
                    pe.wait_ge(x_ok, 12 * i + 8 + s + 1)
                    bank = take_ring(i, TEMP + s)
                    for h in range(H):
                        mm = pe.matmul(bank[:, h * D:(h + 1) * D], Q[2 * s + h // 4][:, h % 4, :], X[s][:, h, :],
                                       start=True, stop=True)
                    mm.then_inc(ring_full, 1)
                else:
                    pe.wait_ge(ring_read, OWN_USES * i + own(TEMP + s) + 1)
                    add_16th(i, s, T16[s], True)

            def read_out(i):
                pe.wait_ge(x_ok, 12 * i + 11)
                pe.wait_ge(masked_ok, 6 * i + 6)
                bank = take_ring(i, READOUT)
                for h in range(H):
                    last = pe.matmul(bank[:, h * D:(h + 1) * D], AT[:, h, :], X[0][:, h, :], start=True, stop=True)
                last.then_inc(ring_full, 1)

            def round_(i, level):
                product(i, level, 0)
                product(i, level, 1)
                turn_power(i, level, 0)
                product(i, level, 2)
                turn_power(i, level, 1)
                product(i, level, 3)
                turn_power(i, level, 2)
                turn_power(i, level, 3)

            def prologue():
                pe.wait_ge(consts_in, 16 * 5)
                frame_products(0)
                turn_normed(0)
                project_bkq(0)
                project_rk_v(0)
                project_rv(0)
                turn_keys(0)
                frame_products(1)
                turn_normed(1)
                strict_grams(0, 0)
                strict_grams(0, 1)
                start_x(0)

            def body(i, rest, ln, x, k):
                for u in range(UNITS):
                    turn_power(i, -1, u)
                if rest is not None:
                    project_bkq(rest)
                round_(i, 0)
                if rest is not None:
                    project_rk_v(rest)
                round_(i, 1)
                if rest is not None:
                    project_rv(rest)
                if ln is not None:
                    frame_products(ln)
                causal_grams(i, 0)
                round_(i, 2)
                causal_grams(i, 1)
                if rest is not None:
                    turn_keys(rest)
                for u in range(UNITS):
                    product(i, 3, u)
                for n in range(2):
                    finish_x(i, 4, n)
                if rest is not None:
                    strict_grams(rest, 0)
                for n in range(2):
                    finish_x(i, 5, n)
                if rest is not None:
                    strict_grams(rest, 1)
                if ln is not None:
                    turn_normed(ln)
                for n in range(2):
                    finish_x(i, 6, n)
                read_out(i)
                if rest is not None:
                    start_x(rest)

            schedule(pe, prologue, body, lambda x: None, lambda x, k: None)

        @block.vector
        def _(dve):
            def norm_stats(j, n, src):
                dve.bn_stats(stats[:, n, :], src).then_inc(stats_ok, 1)
                dve.wait_ge(stats_ok, 2 * j + n + 1)
                dve.sem_inc(held, 1)
                dve.bn_aggr(meanvar[:, n, :], stats[:, n, :]).then_inc(meanvar_ok, 1)
                dve.wait_ge(meanvar_ok, 2 * j + n + 1)
                dve.tensor_scalar(vareps[:, n:n + 1], meanvar[:, n, 1:2], EPS, None, ALU.add).then_inc(vareps_ok, 1)

            def norm1_stats(j):
                dve.wait_ge(mdct_full, j + 1)
                norm_stats(j, 0, ab[1][:, 0:IN])

            def norm1(j):
                dve.wait_ge(rstd_ok, 2 * j + 1)
                dve.tensor_scalar(x1[:], ab[1][:, 0:IN], meanvar[:, 0, 0:1], rstd[:, 0:1], ALU.subtract, ALU.mult)\
                    .then_inc(x1_ok, 1)
                dve.wait_ge(x1_ok, j + 1)
                if not (isinstance(j, int) and j == 0):
                    dve.wait_ge(res_out, 16 * j)
                dve.tensor_tensor(res[:], ab[1][:, 0:IN], x1[:], ALU.add).then_inc(res_ok, 1)
                norm_stats(j, 1, x1[:])

            def norm2(j):
                dve.wait_ge(rstd_ok, 2 * j + 2)
                dve.tensor_scalar(normed[:], x1[:], meanvar[:, 1, 0:1], rstd[:, 1:2], ALU.subtract, ALU.mult)\
                    .then_inc(normed_ok, 1)

            def rates(j):
                dve.wait_ge(bexp_ok, j + 1)
                dve.tensor_scalar(bexp1[:], bexp[:], 1.0, None, ALU.add).then_inc(bexp1_ok, 1)
                dve.wait_ge(bexp1_ok, j + 1)
                dve.reciprocal(rate[:], bexp1[:]).then_inc(rate_ok, 1)

            def shift(j, n):
                src = ab[(2, 0, 1)[n]][:, 0:HD].rearrange("p (h d) -> p h d", h=H)
                dve.wait_ge(proj_full, 6 * j + (2, 3, 4)[n])
                dve.tensor_reduce(rowmax[:, n, :], src, AX_X, ALU.max).then_inc(rowmax_ok, 1)
                dve.wait_ge(rowmax_ok, 3 * j + n + 1)
                if not (isinstance(j, int) and j == 0):
                    dve.wait_ge(soft_ok, 3 * (j - 1) + n + 1)
                dve.tensor_tensor(expd[:, n, :].rearrange("p (h d) -> p h d", h=H), src,
                                  rowmax[:, n, :].unsqueeze(2).to_broadcast([P, H, D]), ALU.subtract)\
                    .then_inc(shifted_ok, 1)

            def scale_values(j, n):
                dve.wait_ge(proj_full, 6 * j + 5 + n)
                if n == 0:
                    dve.wait_ge(rate_ok, j + 1)
                    if not (isinstance(j, int) and j == 0):
                        dve.wait_ge(x_full, 12 * j - 10)
                dve.tensor_tensor(values[:, n, :].rearrange("p (h d) -> p h d", h=H),
                                  ab[(2, 0)[n]][:, 0:HD].rearrange("p (h d) -> p h d", h=H),
                                  rate[:, n * H:(n + 1) * H].unsqueeze(2).to_broadcast([P, H, D]), ALU.mult)\
                    .then_inc(values_ok, 1)

            def sums(j, n):
                dve.wait_ge(exp_ok, 3 * j + n + 1)
                dve.tensor_reduce(rowsum[:, n, :], expd[:, n, :].rearrange("p (h d) -> p h d", h=H), AX_X, ALU.add)\
                    .then_inc(rowsum_ok, 1)
                dve.wait_ge(rowsum_ok, 3 * j + n + 1)
                dve.reciprocal(rowinv[:, n, :], rowsum[:, n, :]).then_inc(rowinv_ok, 1)

            def mask_strict_grams(j, use):
                system, odd = use // 2, use % 2
                bank = ab[(1, 2, 0, 1)[use]]
                dve.wait_ge(gram_full, 6 * j + use + 1)
                for c in range(H // 2):
                    h = 2 * c + odd
                    last = dve.scalar_tensor_tensor(out=PW[2 * system + h // 4][:, h % 4, :],
                                                    in0=bank[:, c * P:(c + 1) * P],
                                                    scalar=rate[:, system * H + h:system * H + h + 1],
                                                    in1=mask_strict, op0=ALU.mult, op1=ALU.mult)
                last.then_inc(masked_ok, 1)

            def mask_causal_grams(j, odd):
                dve.wait_ge(gram_full, 6 * j + 4 + odd + 1)
                if not (isinstance(j, int) and j == 0):
                    dve.wait_ge(ring_full, OWN_USES * j)
                dve.tensor_tensor(AT[:].rearrange("p (n b) c -> p b n c", b=2)[:, odd, :, :],
                                  ab[(2, 0)[odd]][:].rearrange("p (n c) -> p n c", c=P),
                                  mask_causal.unsqueeze(1).to_broadcast([P, H // 2, P]), ALU.mult)\
                    .then_inc(masked_ok, 1)

            def key_products(x, t, g):
                n, m = t + 1, pool_rows(t)
                if t in (0, HEAD_STEPS):
                    dve.wait_ge(loaded[t // HEAD_STEPS], 96 * (x + 1))
                if t == 0:
                    dve.memset(expo[g][:], 1.0)
                    dve.memset(einv[g][:], 1.0 / D).then_inc(start_ok[g], 1)
                    dve.wait_ge(start_ok[g], x + 1)
                else:
                    dve.wait_ge(hexp_ok[g], (S - 1) * x + t)
                    dve.reciprocal(einv[g][:], esum[g][:]).then_inc(einv_ok[g], 1)
                dve.tensor_tensor(prod[g][:, m:n, :], K[g][:, m:n, :],
                                  expo[g][:].unsqueeze(1).to_broadcast([P, n - m, D]), ALU.mult)\
                    .then_inc(kprod_ok[g], 1)

            def key_scores(x, t, g):
                n, m = t + 1, pool_rows(t)
                dve.wait_ge(kprod_ok[g], S * x + t + 1)
                if m:
                    dve.wait_ge(kprod_pool[g], POOL_STEPS * x + t - POOL_FIRST + 1)
                dve.tensor_reduce(scores[g][:, 0:n], prod[g][:, 0:n, :], AX_X, ALU.add).then_inc(score_ok[g], 1)

            def value_products(x, t, g):
                n, m = t + 1, pool_rows(t)
                dve.wait_ge(score_ok[g], S * x + t + 1)
                dve.tensor_tensor(prod[g][:, m:n, :], U[g][:, m:n, :], scores[g][:, m:n].unsqueeze(2)
                                  .to_broadcast([P, n - m, D]), ALU.mult).then_inc(uprod_ok[g], 1)

            def state(x, t, g):
                n, m = t + 1, pool_rows(t)
                dve.wait_ge(uprod_ok[g], S * x + t + 1)
                if m:
                    dve.wait_ge(uprod_pool[g], POOL_STEPS * x + t - POOL_FIRST + 1)
                dve.tensor_reduce(read[g][:], prod[g][:, 0:n, :].rearrange("p s d -> p d s"), AX_X, ALU.add)\
                    .then_inc(read_ok[g], 1)
                dve.wait_ge(read_ok[g], S * x + t + 1)
                if t:
                    dve.wait_ge(einv_ok[g], (S - 1) * x + t)
                dve.scalar_tensor_tensor(out=Z[g][:, t, :], in0=read[g][:], scalar=einv[g][:], in1=Z[g][:, t, :],
                                         op0=ALU.mult, op1=ALU.add).then_inc(h_ok[g], 1)
                if t < S - 1:
                    dve.wait_ge(h_ok[g], S * x + t + 1)
                    dve.tensor_reduce(hmax[g][:], Z[g][:, t, :], AX_X, ALU.max).then_inc(hmax_ok[g], 1)
                    dve.wait_ge(hmax_ok[g], (S - 1) * x + t + 1)
                    dve.tensor_scalar(shifted[g][:], Z[g][:, t, :], hmax[g][:], None, ALU.subtract)\
                        .then_inc(hshift_ok[g], 1)

            def recur(x, k, f, until):
                for kind, t, g in parts_between(k, f, until):
                    (key_products, key_scores, value_products, state)[kind](x, t, g)

            def prologue():
                dve.memset(minus_half[:], -0.5).then_inc(half_set, 1)
                dve.wait_ge(consts_in, 16 * 5)
                norm1_stats(0)
                norm1(0)
                norm2(0)
                rates(0)
                for n in range(3):
                    shift(0, n)
                for n in range(2):
                    scale_values(0, n)
                for n in range(3):
                    sums(0, n)
                norm1_stats(1)
                norm1(1)
                norm2(1)
                for use in range(4):
                    mask_strict_grams(0, use)

            def body(i, rest, ln, x, k):
                recur(x, k, 0.00, 0.12)
                if rest is not None:
                    rates(rest)
                recur(x, k, 0.12, 0.14)
                if rest is not None:
                    shift(rest, 0)
                recur(x, k, 0.14, 0.18)
                if rest is not None:
                    shift(rest, 1)
                recur(x, k, 0.18, 0.32)
                if rest is not None:
                    shift(rest, 2)
                recur(x, k, 0.32, 0.36)
                if rest is not None:
                    scale_values(rest, 0)
                recur(x, k, 0.36, 0.40)
                if rest is not None:
                    sums(rest, 0)
                recur(x, k, 0.40, 0.42)
                if rest is not None:
                    sums(rest, 1)
                recur(x, k, 0.42, 0.46)
                if rest is not None:
                    sums(rest, 2)
                recur(x, k, 0.46, 0.52)
                if rest is not None:
                    scale_values(rest, 1)
                recur(x, k, 0.52, 0.54)
                if ln is not None:
                    norm1_stats(ln)
                recur(x, k, 0.54, 0.58)
                if ln is not None:
                    norm1(ln)
                recur(x, k, 0.58, 0.60)
                mask_causal_grams(i, 0)
                recur(x, k, 0.60, 0.62)
                if ln is not None:
                    norm2(ln)
                recur(x, k, 0.62, 0.68)
                mask_causal_grams(i, 1)
                recur(x, k, 0.68, 0.86)
                if rest is not None:
                    mask_strict_grams(rest, 0)
                recur(x, k, 0.86, 0.88)
                if rest is not None:
                    mask_strict_grams(rest, 1)
                recur(x, k, 0.88, 0.92)
                if rest is not None:
                    mask_strict_grams(rest, 2)
                recur(x, k, 0.92, 0.95)
                if rest is not None:
                    mask_strict_grams(rest, 3)
                recur(x, k, 0.95, 1.00)

            def alone(x, k):
                recur(x, k, 0.0, 1.0)

            schedule(dve, prologue, body, lambda x: None, alone)

        @block.scalar
        def _(act):
            def scale_normedT(j):
                act.wait_ge(normed_full, j + 1)
                if not (isinstance(j, int) and j == 0):
                    act.wait_ge(proj_full, 6 * j)
                act.activation(normedT[:], ring[NORMED % 3][:, 0:P], ACT.Identity, bias=beta[:], scale=gamma[:])\
                    .then_inc(normedT_ok, 1)

            def exp_rates(j):
                act.wait_ge(proj_full, 6 * j + 1)
                act.activation(bexp[:], ab[1][:, 0:2 * H], ACT.Exp, scale=-1.0).then_inc(bexp_ok, 1)

            def exp_rows(j, n):
                act.wait_ge(shifted_ok, 3 * j + n + 1)
                act.activation(expd[:, n, :], expd[:, n, :], ACT.Exp).then_inc(exp_ok, 1)

            def copy_turned(j):
                if not (isinstance(j, int) and j == 0):
                    act.wait_ge(gram_full, 6 * j)
                for n in range(3):
                    act.wait_ge(keys_full, 3 * j + n + 1)
                    dst = kqT[:, :, n, :] if n < 2 else rkT[:]
                    act.copy(dst, ring[(KEYS + n) % 3][:].rearrange("p (c t) -> p c t", c=H // 2))\
                        .then_inc(turned_ok, 1)

            def copy_power(i, level, u):
                use = ROUND + 8 * level + M_USE[u] if level < 3 else LAST + u
                act.wait_ge(ring_full, OWN_USES * i + own(use) + 1)
                dst = PW[u] if level < 3 else Q[u]
                act.copy(dst[:].rearrange("p n c -> p (n c)"), ring[use % 3][:]).then_inc(ring_read, 1)

            def copy_q(i, level, u):
                use = TURN0 + u if level == -1 else ROUND + 8 * level + T_USE[u]
                act.wait_ge(ring_full, OWN_USES * i + own(use) + 1)
                act.copy(Q[u][:].rearrange("p n c -> p (n c)"), ring[use % 3][:]).then_inc(ring_read, 1)

            def copy_x(i, stage, s):
                act.wait_ge(x_full, 12 * i + 2 * stage + s + 1)
                if s == 1 and stage == 0 and not (isinstance(i, int) and i == 0):
                    act.wait_ge(u_out, 32 * i)
                act.copy(X[s][:], xps[s][:]).then_inc(x_ok, 1)

            def copy_temp(i, s):
                act.wait_ge(ring_full, OWN_USES * i + own(TEMP + s) + 1)
                act.copy(T16[s][:].rearrange("p h d -> p (h d)"), ring[(TEMP + s) % 3][:]).then_inc(ring_read, 1)

            def copy_z(i):
                if not (isinstance(i, int) and i == 0):
                    act.wait_ge(z_out, 32 * i)
                act.wait_ge(ring_full, OWN_USES * (i + 1))
                act.copy(zrow[:], ring[READOUT % 3][:]).then_inc(ring_read, 1)

            def exp_state(x, t, g):
                act.wait_ge(hshift_ok[g], (S - 1) * x + t + 1)
                act.activation(expo[g][:], shifted[g][:], ACT.Exp, accum_out=esum[g][:]).then_inc(hexp_ok[g], 1)

            def recur(x, k, f, until):
                for kind, t, g in parts_between(k, f, until):
                    if kind == STATE and t < S - 1:
                        exp_state(x, t, g)

            def prologue():
                act.wait_ge(consts_in, 16 * 5)
                scale_normedT(0)
                exp_rates(0)
                for n in range(3):
                    exp_rows(0, n)
                copy_turned(0)
                scale_normedT(1)

            def round_(i, level, x, k, f, until):
                def meanwhile(n):
                    recur(x, k, f + (until - f) * n / 10, f + (until - f) * (n + 1) / 10)

                copy_power(i, level, 0)
                meanwhile(0)
                copy_power(i, level, 1)
                meanwhile(1)
                copy_x(i, level, 0)
                meanwhile(2)
                copy_q(i, level, 0)
                meanwhile(3)
                copy_power(i, level, 2)
                meanwhile(4)
                copy_q(i, level, 1)
                meanwhile(5)
                copy_power(i, level, 3)
                meanwhile(6)
                copy_x(i, level, 1)
                meanwhile(7)
                copy_q(i, level, 2)
                meanwhile(8)
                copy_q(i, level, 3)
                meanwhile(9)

            def body(i, rest, ln, x, k):
                copy_q(i, -1, 0)
                recur(x, k, 0.000, 0.023)
                copy_q(i, -1, 1)
                recur(x, k, 0.023, 0.047)
                copy_q(i, -1, 2)
                recur(x, k, 0.047, 0.070)
                copy_q(i, -1, 3)
                recur(x, k, 0.070, 0.093)
                if rest is not None:
                    exp_rates(rest)
                recur(x, k, 0.093, 0.117)
                if rest is not None:
                    exp_rows(rest, 0)
                recur(x, k, 0.117, 0.140)
                round_(i, 0, x, k, 0.140, 0.280)
                if rest is not None:
                    exp_rows(rest, 1)
                recur(x, k, 0.280, 0.300)
                if rest is not None:
                    exp_rows(rest, 2)
                recur(x, k, 0.300, 0.320)
                round_(i, 1, x, k, 0.320, 0.460)
                round_(i, 2, x, k, 0.460, 0.620)
                if rest is not None:
                    copy_turned(rest)
                recur(x, k, 0.620, 0.646)
                copy_power(i, 3, 0)
                recur(x, k, 0.646, 0.671)
                copy_power(i, 3, 1)
                recur(x, k, 0.671, 0.697)
                copy_x(i, 3, 0)
                recur(x, k, 0.697, 0.723)
                copy_power(i, 3, 2)
                recur(x, k, 0.723, 0.749)
                copy_power(i, 3, 3)
                recur(x, k, 0.749, 0.774)
                copy_x(i, 3, 1)
                recur(x, k, 0.774, 0.800)
                copy_x(i, 4, 0)
                recur(x, k, 0.800, 0.825)
                copy_x(i, 4, 1)
                recur(x, k, 0.825, 0.850)
                copy_temp(i, 0)
                recur(x, k, 0.850, 0.875)
                copy_temp(i, 1)
                recur(x, k, 0.875, 0.900)
                if ln is not None:
                    scale_normedT(ln)
                recur(x, k, 0.900, 0.925)
                copy_x(i, 5, 0)
                recur(x, k, 0.925, 0.950)
                copy_x(i, 5, 1)
                recur(x, k, 0.950, 0.975)
                copy_z(i)
                recur(x, k, 0.975, 1.000)

            def alone(x, k):
                recur(x, k, 0.0, 1.0)

            schedule(act, prologue, body, lambda x: None, alone)

        @block.gpsimd
        def _(pool):
            def rstd_of(j, n):
                pool.wait_ge(vareps_ok, 2 * j + n + 1)
                pool.tensor_tensor(rstd[:, n:n + 1], vareps[:, n:n + 1], minus_half[:], ALU.pow).then_inc(rstd_ok, 1)

            def normalise(j, n):
                if n == 0 and not (isinstance(j, int) and j == 0):
                    pool.wait_ge(turned_ok, 3 * j)
                    pool.wait_ge(rk_out, 32 * j)
                pool.wait_ge(rowinv_ok, 3 * j + n + 1)
                pool.tensor_tensor(soft[:, n, :].rearrange("p (h d) -> p h d", h=H),
                                   expd[:, n, :].rearrange("p (h d) -> p h d", h=H),
                                   rowinv[:, n, :].unsqueeze(2).to_broadcast([P, H, D]), ALU.mult)\
                    .then_inc(soft_ok, 1)

            def key_products(x, t, g):
                m = pool_rows(t)
                if t == POOL_FIRST:
                    pool.wait_ge(loaded[1], 96 * (x + 1))
                pool.wait_ge(hexp_ok[g], (S - 1) * x + t)
                pool.tensor_tensor(prod[g][:, 0:m, :], K[g][:, 0:m, :],
                                   expo[g][:].unsqueeze(1).to_broadcast([P, m, D]), ALU.mult)\
                    .then_inc(kprod_pool[g], 1)

            def value_products(x, t, g):
                m = pool_rows(t)
                pool.wait_ge(score_ok[g], S * x + t + 1)
                pool.tensor_tensor(prod[g][:, 0:m, :], U[g][:, 0:m, :], scores[g][:, 0:m].unsqueeze(2)
                                   .to_broadcast([P, m, D]), ALU.mult).then_inc(uprod_pool[g], 1)

            def recur(x, k, f, until):
                for kind, t, g in parts_between(k, f, until):
                    if kind in (KEY, VALUE) and pool_rows(t):
                        (key_products if kind == KEY else value_products)(x, t, g)

            def prologue():
                pool.wait_ge(half_set, 1)
                rstd_of(0, 0)
                rstd_of(0, 1)
                for n in range(3):
                    normalise(0, n)
                rstd_of(1, 0)
                rstd_of(1, 1)

            def body(i, rest, ln, x, k):
                recur(x, k, 0.00, 0.42)
                if rest is not None:
                    normalise(rest, 0)
                recur(x, k, 0.42, 0.46)
                if rest is not None:
                    normalise(rest, 1)
                recur(x, k, 0.46, 0.50)
                if rest is not None:
                    normalise(rest, 2)
                recur(x, k, 0.50, 0.56)
                if ln is not None:
                    rstd_of(ln, 0)
                recur(x, k, 0.56, 0.60)
                if ln is not None:
                    rstd_of(ln, 1)
                recur(x, k, 0.60, 1.00)

            def alone(x, k):
                recur(x, k, 0.0, 1.0)

            schedule(pool, prologue, body, lambda x: None, alone)


def feed_forward(nc, h_d, res_d, wout_d, gatew_d, gateb_d, w1_d, b1_d, w2_d, b2_d, ident_d, out):
    with ExitStack() as ctx:
        def sb(name, shape):
            return ctx.enter_context(nc.sbuf_tensor(name, shape, F32))

        def ps(name, shape):
            return ctx.enter_context(nc.psum_tensor(name, shape, F32))

        def sem(name):
            return ctx.enter_context(nc.semaphore(name))

        T = BATCH * P
        N = TILES // BATCH
        ident = sb("ident3", [P, P])
        wout = sb("wout", [P, HD // P, IN])
        gatew = sb("gatew", [P, NE])
        gateb = sb("gateb", [P, NE])
        w1 = sb("w1", [P, EXPERTS, F])
        b1 = sb("b1", [P, EXPERTS * FC])
        w2 = sb("w2", [P, EXPERTS, FC, IN])
        b2 = sb("b2", [EXPERTS, IN])
        minus_half = sb("minus_half3", [P, BATCH])
        hs = sb("hs", [P, BATCH, HD])
        hsT = sb("hsT", [P, 2, HD // P, P])
        res = sb("res3", [P, BATCH, IN])
        acc = sb("acc", [P, BATCH, IN])
        stats = sb("stats3", [P, BATCH, 6])
        meanvar = sb("meanvar3", [P, BATCH, 2])
        vareps = sb("vareps3", [P, BATCH])
        rstd = sb("rstd3", [P, BATCH])
        x2 = sb("x2", [P, BATCH, IN])
        x2T = sb("x2T", [P, T])
        logit = sb("logit", [P, BATCH, NE])
        lmax = sb("lmax", [P, BATCH])
        lsum = sb("lsum", [P, BATCH])
        linv = sb("linv", [P, BATCH])
        lexp = sb("lexp", [P, BATCH, NE])
        prob = sb("prob", [P, BATCH, NE])
        top = sb("top", [P, BATCH, 8])
        above = sb("above", [P, BATCH, NE])
        equal = sb("equal", [P, BATCH, NE])
        rank = [sb(f"rank{n}", [P, BATCH, NE]) for n in range(3)]
        nabove = sb("nabove", [P, BATCH])
        room = sb("room", [P, BATCH, NE])
        chosen = sb("chosen", [P, BATCH, NE])
        cw = sb("cw", [P, BATCH, EXPERTS])
        cwT = sb("cwT", [EXPERTS, BATCH, P])
        hid = [sb(f"hid{n}", [P, FC, T]) for n in range(2)]

        tp = [ps(f"tp{n}", [P, 512]) for n in range(2)]
        op = ps("op", [P, 512])
        up = [ps(f"up{n}", [P, 512]) for n in range(3)]
        dn = [ps(f"dn{n}", [P, 512]) for n in range(2)]

        held = sem("held3")
        weights_in = sem("weights_in")
        consts_ok = sem("consts_ok")
        hs_in = sem("hs_in")
        res_in = sem("res_in")
        hsp_full = sem("hsp_full")
        hsT_ok = sem("hsT_ok")
        op_full = sem("op_full")
        stream_ok = sem("stream_ok")
        stats_ok = sem("stats_ok3")
        meanvar_ok = sem("meanvar_ok3")
        vareps_ok = sem("vareps_ok3")
        rstd_ok = sem("rstd_ok3")
        x2_ok = sem("x2_ok")
        x2p_full = sem("x2p_full")
        x2T_ok = sem("x2T_ok")
        logit_full = sem("logit_full")
        router = sem("router")
        lexp_ok = sem("lexp_ok")
        cw_ok = sem("cw_ok")
        cwp_full = sem("cwp_full")
        cwT_ok = sem("cwT_ok")
        bias_full = sem("bias_full")
        bias_ok = sem("bias_ok")
        up_full = sem("up_full")
        hid_ok = sem("hid_ok")
        dn_full = sem("dn_full")
        dn_read = sem("dn_read")
        out_out = sem("out_out")
        ROUTER = 14

        def schedule(eng, body):
            body(0)
            with eng.Fori(1, N - 1) as i:
                body(i)
            body(N - 1)

        block = ctx.enter_context(nc.Block())
        weights = ((ident[:], ident_d), (wout[:], wout_d), (gatew[:], gatew_d), (gateb[:], gateb_d),
                   (b1[:], b1_d), (b2[:], b2_d), (w1[:], w1_d), (w2[:], w2_d))

        @block.sync
        def _(sp):
            def load(i):
                if not (isinstance(i, int) and i == 0):
                    sp.wait_ge(hsT_ok, BATCH * i)
                    sp.sem_inc(held, 1)
                    sp.wait_ge(stream_ok, BATCH * i)
                    sp.sem_inc(held, 1)
                for k in range(BATCH):
                    for w in range(2):
                        src = h_d.rearrange("(x k w) h t d -> k w x t h d", k=BATCH, w=2)[
                            k, w, bass.ds(i, 1), :, :, :].rearrange("x t h d -> (x t) h d")
                        sp.dma_start(hs[w * S:(w + 1) * S, k, :].rearrange("p (h d) -> p h d", h=H), src)\
                            .then_inc(hs_in, 16)
                sp.dma_start(res[:], res_d[bass.ds(i * T, T), :].rearrange("(k p) d -> p k d", k=BATCH))\
                    .then_inc(res_in, 16)

            def store(i):
                last = isinstance(i, int) and i == N - 1
                m = REAL_TILES - BATCH * (N - 1) if last else BATCH
                sp.wait_ge(dn_read, EXPERTS * (i + 1))
                sp.sem_inc(held, 1)
                for w in range(2):
                    dst = out.rearrange("t (c w) d -> w t c d", w=2)[w, :, bass.ds(i * BATCH, m), :]
                    sp.dma_start(dst, acc[w * S:(w + 1) * S, 0:m, :]).then_inc(out_out, 16)

            for n, (t, d) in enumerate(weights):
                sp.dma_start(t, d).then_inc(weights_in, 16)
                if n == 3:
                    load(0)
            load(1)
            store(0)
            with sp.Fori(1, N - 1) as i:
                load(i + 1)
                store(i)
            store(N - 1)
            sp.wait_ge(out_out, 32 * N)

        @block.tensor
        def _(pe):
            def body(i):
                first = isinstance(i, int) and i == 0
                for k in range(BATCH):
                    if k == 0:
                        pe.wait_ge(hs_in, 32 * BATCH * (i + 1))
                    if k >= 2:
                        pe.wait_ge(hsT_ok, BATCH * i + k - 1)
                    elif not first:
                        if k == 0:
                            pe.wait_ge(x2T_ok, i)
                        else:
                            pe.wait_ge(cwT_ok, i)
                    for c in range(HD // P):
                        last = pe.transpose(tp[k % 2][:, c * P:(c + 1) * P], hs[:, k, c * P:(c + 1) * P], ident[:])
                    last.then_inc(hsp_full, 1)
                    if k:
                        project(i, k - 1)
                project(i, BATCH - 1)
                for k in range(BATCH):
                    pe.wait_ge(x2_ok, BATCH * i + k + 1)
                    last = pe.transpose(tp[0][:, k * P:(k + 1) * P], x2[:, k, :], ident[:])
                last.then_inc(x2p_full, 1)
                pe.wait_ge(x2T_ok, i + 1)
                for k in range(BATCH):
                    last = pe.matmul(op[:, k * NE:(k + 1) * NE], x2T[:, k * P:(k + 1) * P], gatew[:],
                                     start=True, stop=True)
                last.then_inc(logit_full, 1)
                for e in range(EXPERTS):
                    expert_up(i, e)
                    if e == 0:
                        pe.wait_ge(cw_ok, i + 1)
                        for k in range(BATCH):
                            last = pe.transpose(tp[1][0:EXPERTS, k * P:(k + 1) * P], cw[:, k, :], ident[:])
                        last.then_inc(cwp_full, 1)
                        pe.wait_ge(cwT_ok, i + 1)
                        for k in range(BATCH):
                            last = pe.matmul(op[:, k * IN:(k + 1) * IN], cwT[:, k, :], b2[:], start=True, stop=True)
                        last.then_inc(bias_full, 1)
                    if e:
                        expert_down(i, e - 1)
                expert_down(i, EXPERTS - 1)

            def project(i, k):
                pe.wait_ge(hsT_ok, BATCH * i + k + 1)
                if k:
                    pe.wait_ge(stream_ok, BATCH * i + k)
                elif not (isinstance(i, int) and i == 0):
                    pe.wait_ge(bias_ok, i)
                for c in range(HD // P):
                    last = pe.matmul(op[:, 0:IN], hsT[:, k % 2, c, :], wout[:, c, :],
                                     start=(c == 0), stop=(c == HD // P - 1))
                last.then_inc(op_full, 1)

            def expert_up(i, e):
                for f in range(FC):
                    n = e * FC + f
                    slot = n % 3
                    if n >= 3:
                        pe.wait_ge(hid_ok, EXPERTS * FC * i + n - 2)
                    elif not (isinstance(i, int) and i == 0):
                        pe.wait_ge(hid_ok, EXPERTS * FC * i)
                    pe.matmul(up[slot][:], w1[:, e, f * P:(f + 1) * P], x2T[:], start=True, stop=True)\
                        .then_inc(up_full, 1)

            def expert_down(i, e):
                pe.wait_ge(hid_ok, EXPERTS * FC * i + (e + 1) * FC)
                if e >= 2:
                    pe.wait_ge(dn_read, EXPERTS * i + e - 1)
                elif not (isinstance(i, int) and i == 0):
                    pe.wait_ge(dn_read, EXPERTS * i + e - 1)
                for k in range(BATCH):
                    for f in range(FC):
                        last = pe.matmul(dn[e % 2][:, k * IN:(k + 1) * IN], hid[e % 2][:, f, k * P:(k + 1) * P],
                                         w2[:, e, f, :], start=(f == 0), stop=(f == FC - 1))
                last.then_inc(dn_full, 1)

            pe.wait_ge(weights_in, 16 * len(weights))
            schedule(pe, body)

        @block.scalar
        def _(act):
            def body(i):
                for k in range(BATCH):
                    act.wait_ge(hsp_full, BATCH * i + k + 1)
                    if k >= 2:
                        act.wait_ge(op_full, BATCH * i + k - 1)
                    act.copy(hsT[:, k % 2, :, :].rearrange("p c t -> p (c t)"), tp[k % 2][:]).then_inc(hsT_ok, 1)
                act.wait_ge(x2p_full, i + 1)
                act.copy(x2T[:], tp[0][:]).then_inc(x2T_ok, 1)
                act.wait_ge(router, ROUTER * i + 3)
                act.activation(lexp[:].rearrange("p k e -> p (k e)"), logit[:].rearrange("p k e -> p (k e)"),
                               ACT.Exp).then_inc(lexp_ok, 1)
                for e in range(EXPERTS):
                    for f in range(FC):
                        n = e * FC + f
                        act.wait_ge(up_full, EXPERTS * FC * i + n + 1)
                        if f == 0 and e >= 2:
                            act.wait_ge(dn_full, EXPERTS * i + e - 1)
                        act.activation(hid[e % 2][:, f, :], up[n % 3][:], ACT.Gelu, bias=b1[:, n:n + 1])\
                            .then_inc(hid_ok, 1)

            act.wait_ge(weights_in, 16 * len(weights))
            schedule(act, body)

        @block.gpsimd
        def _(pool):
            def body(i):
                pool.wait_ge(vareps_ok, i + 1)
                pool.tensor_tensor(rstd[:], vareps[:], minus_half[:], ALU.pow).then_inc(rstd_ok, 1)

            pool.wait_ge(consts_ok, 2)
            schedule(pool, body)

        @block.vector
        def _(dve):
            def body(i):
                first = isinstance(i, int) and i == 0
                dve.wait_ge(res_in, 16 * (i + 1))
                if not first:
                    dve.wait_ge(out_out, 32 * i)
                for k in range(BATCH):
                    dve.wait_ge(op_full, BATCH * i + k + 1)
                    dve.tensor_tensor(acc[:, k, :], op[:, 0:IN], res[:, k, :], ALU.add).then_inc(stream_ok, 1)
                    dve.wait_ge(stream_ok, BATCH * i + k + 1)
                    dve.bn_stats(stats[:, k, :], acc[:, k, :]).then_inc(stats_ok, 1)
                    dve.wait_ge(stats_ok, BATCH * i + k + 1)
                    dve.sem_inc(held, 1)
                    dve.bn_aggr(meanvar[:, k, :], stats[:, k, :]).then_inc(meanvar_ok, 1)
                dve.wait_ge(meanvar_ok, BATCH * i + BATCH)
                dve.tensor_scalar(vareps[:], meanvar[:, :, 1], EPS, None, ALU.add).then_inc(vareps_ok, 1)
                dve.wait_ge(rstd_ok, i + 1)
                for k in range(BATCH):
                    dve.tensor_scalar(x2[:, k, :], acc[:, k, :], meanvar[:, k, 0:1], rstd[:, k:k + 1],
                                      ALU.subtract, ALU.mult).then_inc(x2_ok, 1)
                dve.wait_ge(logit_full, i + 1)
                route(i)
                dve.wait_ge(bias_full, i + 1)
                dve.tensor_tensor(acc[:].rearrange("p k d -> p (k d)"), op[:],
                                  acc[:].rearrange("p k d -> p (k d)"), ALU.add).then_inc(bias_ok, 1)
                dve.wait_ge(bias_ok, i + 1)
                for e in range(EXPERTS):
                    dve.wait_ge(dn_full, EXPERTS * i + e + 1)
                    if e:
                        dve.wait_ge(dn_read, EXPERTS * i + e)
                    for k in range(BATCH):
                        last = dve.scalar_tensor_tensor(out=acc[:, k, :], in0=dn[e % 2][:, k * IN:(k + 1) * IN],
                                                        scalar=cw[:, k, e:e + 1], in1=acc[:, k, :],
                                                        op0=ALU.mult, op1=ALU.add)
                    last.then_inc(dn_read, 1)

            def route(i):
                def wide(a):
                    return a.unsqueeze(2).to_broadcast([P, BATCH, NE])

                r = ROUTER * i
                dve.tensor_tensor(logit[:], op[:, 0:BATCH * NE].rearrange("p (k e) -> p k e", k=BATCH),
                                  gateb[:].unsqueeze(1).to_broadcast([P, BATCH, NE]), ALU.add).then_inc(router, 1)
                dve.wait_ge(router, r + 1)
                dve.tensor_reduce(lmax[:], logit[:], AX_X, ALU.max).then_inc(router, 1)
                dve.wait_ge(router, r + 2)
                dve.tensor_tensor(logit[:], logit[:], wide(lmax[:]), ALU.subtract).then_inc(router, 1)
                dve.wait_ge(lexp_ok, i + 1)
                dve.tensor_reduce(lsum[:], lexp[:], AX_X, ALU.add).then_inc(router, 1)
                dve.wait_ge(router, r + 4)
                dve.reciprocal(linv[:], lsum[:]).then_inc(router, 1)
                dve.wait_ge(router, r + 5)
                dve.tensor_tensor(prob[:], lexp[:], wide(linv[:]), ALU.mult).then_inc(router, 1)
                dve.wait_ge(router, r + 6)
                dve.sem_inc(held, 1)
                for k in range(BATCH):
                    last = dve.max(top[:, k, :], prob[:, k, :])
                last.then_inc(router, 1)
                dve.wait_ge(router, r + 7)
                dve.tensor_tensor(above[:], prob[:], wide(top[:, :, 1]), ALU.is_gt)
                dve.tensor_tensor(equal[:], prob[:], wide(top[:, :, 1]), ALU.is_equal).then_inc(router, 1)
                dve.wait_ge(router, r + 8)
                dve.tensor_reduce(nabove[:], above[:], AX_X, ALU.add)
                src = equal
                for n, step in enumerate((1, 2, 4)):
                    dve.tensor_copy(rank[n][:, :, 0:step], src[:, :, 0:step])
                    dve.tensor_tensor(rank[n][:, :, step:NE], src[:, :, step:NE], src[:, :, 0:NE - step],
                                      ALU.add).then_inc(router, 1)
                    dve.wait_ge(router, r + 9 + n)
                    src = rank[n]
                dve.tensor_tensor(room[:], rank[2][:], wide(nabove[:]), ALU.add).then_inc(router, 1)
                dve.wait_ge(router, r + 12)
                dve.scalar_tensor_tensor(out=chosen[:].rearrange("p k e -> p (k e)"),
                                         in0=room[:].rearrange("p k e -> p (k e)"), scalar=2.0,
                                         in1=equal[:].rearrange("p k e -> p (k e)"),
                                         op0=ALU.is_le, op1=ALU.mult).then_inc(router, 1)
                dve.wait_ge(router, r + 13)
                dve.tensor_tensor(chosen[:], chosen[:], above[:], ALU.add).then_inc(router, 1)
                dve.wait_ge(router, r + 14)
                dve.tensor_tensor(cw[:, :, 0:NE], chosen[:], prob[:], ALU.mult).then_inc(cw_ok, 1)
                dve.wait_ge(cwp_full, i + 1)
                dve.tensor_copy(cwT[:].rearrange("e k p -> e (k p)"), tp[1][0:EXPERTS, :]).then_inc(cwT_ok, 1)

            dve.memset(minus_half[:], -0.5).then_inc(consts_ok, 1)
            dve.memset(cw[:], 1.0).then_inc(consts_ok, 1)
            dve.wait_ge(weights_in, 16 * len(weights))
            dve.wait_ge(consts_ok, 2)
            schedule(dve, body)


def audio_tower(nc, frames, mdct, wslow, gamma, beta, masks, wout, gatew, gateb, w1, b1, w2, b2, ident, out):
    chain_shape = [FRAMES, H, S, D]
    res_d = nc.dram_tensor("res_scratch", [TILES * P, IN], F32, kind="Internal").ap()
    rk_d = nc.dram_tensor("rk_scratch", chain_shape, F32, kind="Internal").ap()
    u_d = nc.dram_tensor("u_scratch", chain_shape, F32, kind="Internal").ap()
    z_d = nc.dram_tensor("z_scratch", chain_shape, F32, kind="Internal").ap()
    h_d = nc.dram_tensor("h_scratch", chain_shape, F32, kind="Internal").ap()
    tiles_and_recurrence(nc, frames, mdct, wslow, gamma, beta, masks, res_d, rk_d, u_d, z_d, h_d)
    feed_forward(nc, h_d, res_d, wout, gatew, gateb, w1, b1, w2, b2, ident, out)


def mdct_matrix():
    length = 2 * HOP
    half = length // 2
    f32 = np.float32
    n = np.arange(length, dtype=f32) + f32(0.5)
    k = f32(np.pi / half) * n[:half]
    n = n + f32(half / 2)
    z = np.sqrt(f32(2.0 / half * 2.0))
    m = z * np.cos(n[:, None] * k[None, :])
    w = np.sin(f32(np.pi) * (np.arange(length, dtype=f32) + f32(0.5)) / f32(length))
    return (w[:, None] * m).astype(f32)


def mask_tables():
    t = np.arange(P)
    same = (t[:, None] // S) == (t[None, :] // S)
    ident = np.eye(P)
    strict = -(same & (t[None, :] < t[:, None])).astype(np.float64)
    causal = (same & (t[:, None] <= t[None, :])).astype(np.float64)
    return np.ascontiguousarray(np.stack([ident, strict, causal], 1).astype(np.float32))


def kernel(x, L0_attn_W_slow, L0_attn_W_out, L0_attn_ln_gamma, L0_attn_ln_beta, L0_ffn_gate_w, L0_ffn_gate_b,
           L0_ffn_sw1, L0_ffn_sb1, L0_ffn_sw2, L0_ffn_sb2, L0_ffn_rw1, L0_ffn_rb1, L0_ffn_rw2, L0_ffn_rb2):
    import concourse.bacc as bacc
    from concourse.bass_utils import run_bass_kernel_spmd

    arr = np.asarray
    x = arr(x)
    blocks = FRAMES + 1
    xp = np.zeros((S, blocks * HOP), x.dtype)
    xp[:, HOP:HOP + LEN] = x
    frames = xp.reshape(S, blocks, HOP).transpose(2, 1, 0).reshape(HOP, blocks * S)
    mdct = mdct_matrix().reshape(2, HOP, IN).transpose(1, 0, 2)
    ws = arr(L0_attn_W_slow).reshape(H, 5 * D + 2, IN)
    part = [ws[:, n * D:(n + 1) * D].reshape(HD, IN) for n in (1, 0, 3, 2, 4)]
    wslow = np.concatenate(part + [ws[:, 5 * D], ws[:, 5 * D + 1]], 0).T
    wout = arr(L0_attn_W_out).T.reshape(HD // P, P, IN).transpose(1, 0, 2)
    w1 = np.concatenate([arr(L0_ffn_rw1), arr(L0_ffn_sw1)], 0).transpose(2, 0, 1)
    b1 = np.concatenate([arr(L0_ffn_rb1), arr(L0_ffn_sb1)], 0).reshape(EXPERTS * FC, P).T
    w2 = np.concatenate([arr(L0_ffn_rw2), arr(L0_ffn_sw2)], 0).reshape(EXPERTS, IN, FC, P).transpose(3, 0, 2, 1)
    b2 = np.concatenate([arr(L0_ffn_rb2), arr(L0_ffn_sb2)], 0)
    gateb = np.broadcast_to(arr(L0_ffn_gate_b)[None, :], (P, NE))
    arrays = {
        "frames": frames, "mdct": mdct, "wslow": wslow, "gamma": arr(L0_attn_ln_gamma).reshape(IN, 1),
        "beta": arr(L0_attn_ln_beta).reshape(IN, 1), "masks": mask_tables(), "wout": wout,
        "gatew": arr(L0_ffn_gate_w).T, "gateb": gateb, "w1": w1, "b1": b1, "w2": w2, "b2": b2,
        "ident": np.eye(P, dtype=np.float32),
    }
    nc = bacc.Bacc("TRN2", target_bir_lowering=False, num_devices=1)
    named, args = {}, []
    for name, a in arrays.items():
        a = np.ascontiguousarray(a)
        named[f"in_{name}"] = a
        args.append(nc.dram_tensor(f"in_{name}", a.shape, mybir.dt.from_np(a.dtype), kind="ExternalInput").ap())
    args.append(nc.dram_tensor("out_0", (S, NF, IN), F32, kind="ExternalOutput").ap())
    audio_tower(nc, *args)
    r = run_bass_kernel_spmd(nc, [named], core_ids=[0])
    return r.results[0]["out_0"]
```

```python
from contextlib import ExitStack

import concourse.bass as bass
import numpy as np
from concourse import mybir

F32 = mybir.dt.float32
ALU = mybir.AluOpType
ACT = mybir.ActivationFunctionType
AX_X = mybir.AxisListType.X

P = 128
S, NF = 64, 158
LEN = 20000
HOP = 128
IN = 128
H, D = 8, 64
HD = H * D
NE, NSH, F = 8, 2, 512
EXPERTS = NE + NSH
FC = F // P
TILES = 80
REAL_TILES = NF // 2
FRAMES = 2 * TILES
UNITS = 4
GROUP = 16
PAIRS = FRAMES // GROUP // 2
PT = GROUP
POOL_SHARE = 12
POOL_FIRST = 8
POOL_STEPS = S - POOL_FIRST
HEAD_STEPS = 8

TURN0, ROUND, KEYS, LAST, TEMP, NORMED, READOUT, RING_USES = 0, 4, 28, 31, 35, 37, 38, 39
OWN_USES = RING_USES - 4
M_USE = (0, 1, 3, 5)
T_USE = (2, 4, 6, 7)

KEY, SCORE, VALUE, STATE = range(4)
PARTS = [(kind, t, g) for t in range(S) for kind in (KEY, SCORE, VALUE, STATE) for g in range(2)]


def part_weight(kind, t):
    return (1.0, 1.0, 1.0, 6.0)[kind] + (t + 1) * ((0.35, 1.0, 0.35, 1.0)[kind] if t >= 8 else 1.0) * 0.6


PART_START = np.cumsum([0.0] + [part_weight(kind, t) for kind, t, _ in PARTS])
TILE_0_END = PART_START[8 * HEAD_STEPS]


def position(k, f):
    if k == 0:
        return TILE_0_END * max(0.0, (f - LOAD_PART) / (1 - LOAD_PART))
    return TILE_0_END + (PART_START[-1] - TILE_0_END) * (k - 1 + f) / (PT - 1)


def parts_in(a, b):
    return [p for p, start in zip(PARTS, PART_START) if a - 1e-6 <= start < b - 1e-6]


def steps_done(a):
    return sum(1 for kind, _, g in parts_in(0.0, a) if kind == STATE and g == 1)


def beside_tile(k, f, until):
    return [] if k is None else parts_in(position(k, f), position(k, until))


def batch_position(i, f):
    return TILE_0_END + (PART_START[-1] - TILE_0_END) * max(0.0, i + f) / BESIDE


def beside_batch(i, f, until):
    return parts_in(batch_position(i, f), batch_position(i, until))


FIRST_STEPS = parts_in(0.0, TILE_0_END)
LOAD_PART = 0.25
BATCH = 2
BESIDE = 16
EPS = 1e-5

COL = {"k": 0, "q": HD, "rk": 2 * HD, "v": 3 * HD, "rv": 4 * HD, "b": 5 * HD}
PROJ = 5 * HD + 2 * H


def pool_rows(t):
    return 0 if t < POOL_FIRST else ((t + 1) * POOL_SHARE) // 16


class Recurrence:

    def __init__(self, nc, ctx, rk_d, u_d, z_d, h_d):
        self.rk_d, self.u_d, self.z_d, self.h_d = rk_d, u_d, z_d, h_d

        def sb(name, shape):
            return ctx.enter_context(nc.sbuf_tensor(name, shape, F32))

        def sem(name):
            return ctx.enter_context(nc.semaphore(name))

        def two(name):
            return [sem(f"{name}{g}") for g in range(2)]

        self.K = [sb(f"K{g}", [P, S, D]) for g in range(2)]
        self.U = [sb(f"U{g}", [P, S, D]) for g in range(2)]
        self.Z = [sb(f"Z{g}", [P, S, D]) for g in range(2)]
        self.prod = [sb(f"prod{g}", [P, S, D]) for g in range(2)]
        self.expo = [sb(f"expo{g}", [P, D]) for g in range(2)]
        self.shifted = [sb(f"shifted{g}", [P, D]) for g in range(2)]
        self.scores = [sb(f"scores{g}", [P, S]) for g in range(2)]
        self.read = [sb(f"read{g}", [P, D]) for g in range(2)]
        self.hmax = [sb(f"hmax{g}", [P, 1]) for g in range(2)]
        self.esum = [sb(f"esum{g}", [P, 1]) for g in range(2)]
        self.einv = [sb(f"einv{g}", [P, 1]) for g in range(2)]
        self.held = sem("held_recurrence")
        self.loaded = [sem(f"loaded{c}") for c in range(2)]
        self.h_out = sem("h_out")
        self.start_ok = two("start_ok")
        self.kprod_pool = two("kprod_pool")
        self.uprod_pool = two("uprod_pool")
        self.kprod_ok = two("kprod_ok")
        self.score_ok = two("score_ok")
        self.uprod_ok = two("uprod_ok")
        self.read_ok = two("read_ok")
        self.h_ok = two("h_ok")
        self.hmax_ok = two("hmax_ok")
        self.hshift_ok = two("hshift_ok")
        self.hexp_ok = two("hexp_ok")
        self.einv_ok = two("einv_ok")

    @staticmethod
    def chains(dram, x, g, t, n):
        return dram.rearrange("(x g b) h t d -> g x (b h) (t d)", g=2, b=GROUP)[
            g, bass.ds(x, 1), :, t * D:(t + n) * D].rearrange("x p f -> (x p) f")

    def load(self, sp, x):
        if not (isinstance(x, int) and x == 0):
            for g in range(2):
                sp.wait_ge(self.read_ok[g], S * x)
                sp.sem_inc(self.held, 1)
            sp.wait_ge(self.h_out, 32 * PT * x)
            sp.sem_inc(self.held, 1)
        self.load_steps(sp, x, 0)
        if not (isinstance(x, int) and x == PAIRS - 1):
            self.load_steps(sp, x, 1)

    def load_steps(self, sp, x, c):
        t, n = ((0, HEAD_STEPS), (HEAD_STEPS, S - HEAD_STEPS))[c]
        for g in range(2):
            for sbuf, dram in ((self.K, self.rk_d), (self.U, self.u_d), (self.Z, self.z_d)):
                sp.dma_start(sbuf[g][:, t:t + n, :].rearrange("p t d -> p (t d)"),
                             self.chains(dram, x, g, t, n)).then_inc(self.loaded[c], 16)

    def store_h(self, sp, x, before, done):
        for g in range(2):
            sp.wait_ge(self.h_ok[g], S * x + done)
            sp.sem_inc(self.held, 1)
            if done < S:
                sp.wait_ge(self.hshift_ok[g], (S - 1) * x + done)
                sp.sem_inc(self.held, 1)
            sp.dma_start(self.chains(self.h_d, x, g, before, done - before),
                         self.Z[g][:, before:done, :].rearrange("p t d -> p (t d)")).then_inc(self.h_out, 16)

    def key_products(self, dve, x, t, g):
        n, m = t + 1, pool_rows(t)
        if t in (0, HEAD_STEPS):
            dve.wait_ge(self.loaded[t // HEAD_STEPS], 96 * (x + 1))
        if t == 0:
            dve.memset(self.expo[g][:], 1.0)
            dve.memset(self.einv[g][:], 1.0 / D).then_inc(self.start_ok[g], 1)
            dve.wait_ge(self.start_ok[g], x + 1)
        else:
            dve.wait_ge(self.hexp_ok[g], (S - 1) * x + t)
            dve.reciprocal(self.einv[g][:], self.esum[g][:]).then_inc(self.einv_ok[g], 1)
        dve.tensor_tensor(self.prod[g][:, m:n, :], self.K[g][:, m:n, :],
                          self.expo[g][:].unsqueeze(1).to_broadcast([P, n - m, D]), ALU.mult)\
            .then_inc(self.kprod_ok[g], 1)

    def key_scores(self, dve, x, t, g):
        n, m = t + 1, pool_rows(t)
        dve.wait_ge(self.kprod_ok[g], S * x + t + 1)
        if m:
            dve.wait_ge(self.kprod_pool[g], POOL_STEPS * x + t - POOL_FIRST + 1)
        dve.tensor_reduce(self.scores[g][:, 0:n], self.prod[g][:, 0:n, :], AX_X, ALU.add).then_inc(self.score_ok[g], 1)

    def value_products(self, dve, x, t, g):
        n, m = t + 1, pool_rows(t)
        dve.wait_ge(self.score_ok[g], S * x + t + 1)
        dve.tensor_tensor(self.prod[g][:, m:n, :], self.U[g][:, m:n, :], self.scores[g][:, m:n].unsqueeze(2)
                          .to_broadcast([P, n - m, D]), ALU.mult).then_inc(self.uprod_ok[g], 1)

    def state(self, dve, x, t, g):
        n, m = t + 1, pool_rows(t)
        dve.wait_ge(self.uprod_ok[g], S * x + t + 1)
        if m:
            dve.wait_ge(self.uprod_pool[g], POOL_STEPS * x + t - POOL_FIRST + 1)
        dve.tensor_reduce(self.read[g][:], self.prod[g][:, 0:n, :].rearrange("p s d -> p d s"), AX_X, ALU.add)\
            .then_inc(self.read_ok[g], 1)
        dve.wait_ge(self.read_ok[g], S * x + t + 1)
        if t:
            dve.wait_ge(self.einv_ok[g], (S - 1) * x + t)
        dve.scalar_tensor_tensor(out=self.Z[g][:, t, :], in0=self.read[g][:], scalar=self.einv[g][:], in1=self.Z[g][:, t, :],
                                 op0=ALU.mult, op1=ALU.add).then_inc(self.h_ok[g], 1)
        if t < S - 1:
            dve.wait_ge(self.h_ok[g], S * x + t + 1)
            dve.tensor_reduce(self.hmax[g][:], self.Z[g][:, t, :], AX_X, ALU.max).then_inc(self.hmax_ok[g], 1)
            dve.wait_ge(self.hmax_ok[g], (S - 1) * x + t + 1)
            dve.tensor_scalar(self.shifted[g][:], self.Z[g][:, t, :], self.hmax[g][:], None, ALU.subtract)\
                .then_inc(self.hshift_ok[g], 1)

    def on_dve(self, dve, x, parts):
        for kind, t, g in parts:
            (self.key_products, self.key_scores, self.value_products, self.state)[kind](dve, x, t, g)

    def exp_state(self, act, x, t, g):
        act.wait_ge(self.hshift_ok[g], (S - 1) * x + t + 1)
        act.activation(self.expo[g][:], self.shifted[g][:], ACT.Exp, accum_out=self.esum[g][:]).then_inc(self.hexp_ok[g], 1)

    def on_act(self, act, x, parts):
        for kind, t, g in parts:
            if kind == STATE and t < S - 1:
                self.exp_state(act, x, t, g)

    def key_products_pool(self, pool, x, t, g):
        m = pool_rows(t)
        if t == POOL_FIRST:
            pool.wait_ge(self.loaded[1], 96 * (x + 1))
        pool.wait_ge(self.hexp_ok[g], (S - 1) * x + t)
        pool.tensor_tensor(self.prod[g][:, 0:m, :], self.K[g][:, 0:m, :],
                           self.expo[g][:].unsqueeze(1).to_broadcast([P, m, D]), ALU.mult)\
            .then_inc(self.kprod_pool[g], 1)

    def value_products_pool(self, pool, x, t, g):
        m = pool_rows(t)
        pool.wait_ge(self.score_ok[g], S * x + t + 1)
        pool.tensor_tensor(self.prod[g][:, 0:m, :], self.U[g][:, 0:m, :], self.scores[g][:, 0:m].unsqueeze(2)
                           .to_broadcast([P, m, D]), ALU.mult).then_inc(self.uprod_pool[g], 1)

    def on_pool(self, pool, x, parts):
        for kind, t, g in parts:
            if kind in (KEY, VALUE) and pool_rows(t):
                (self.key_products_pool if kind == KEY else self.value_products_pool)(pool, x, t, g)


def tiles_and_recurrence(nc, recurrence, frames_d, mdct_d, wslow_d, gamma_d, beta_d, masks_d, res_d, rk_d, u_d, z_d):
    with ExitStack() as ctx:
        def sb(name, shape):
            return ctx.enter_context(nc.sbuf_tensor(name, shape, F32))

        def ps(name, shape):
            return ctx.enter_context(nc.psum_tensor(name, shape, F32))

        def sem(name):
            return ctx.enter_context(nc.semaphore(name))

        wslow = sb("wslow", [P, PROJ])
        mdct = sb("mdct", [P, 2, IN])
        gamma = sb("gamma", [P, 1])
        beta = sb("beta", [P, 1])
        masks = sb("masks", [P, 3, P])
        ident, mask_strict, mask_causal = masks[:, 0, :], masks[:, 1, :], masks[:, 2, :]
        minus_half = sb("minus_half", [P, 1])
        frames = sb("frames", [P, 3 * S])
        stats = sb("stats", [P, 2, 6])
        meanvar = sb("meanvar", [P, 2, 2])
        vareps = sb("vareps", [P, 2])
        rstd = sb("rstd", [P, 2])
        x1 = sb("x1", [P, IN])
        res = sb("res", [P, IN])
        normed = sb("normed", [P, IN])
        normedT = sb("normedT", [P, P])
        bexp = sb("bexp", [P, 2 * H])
        bexp1 = sb("bexp1", [P, 2 * H])
        rate = sb("rate", [P, 2 * H])
        rowmax = sb("rowmax", [P, 3, H])
        rowsum = sb("rowsum", [P, 3, H])
        rowinv = sb("rowinv", [P, 3, H])
        expd = sb("expd", [P, 3, HD])
        soft = sb("soft", [P, 3, HD])
        values = sb("values", [P, 2, HD])
        kqT = sb("kqT", [P, H // 2, 2, P])
        rkT = sb("rkT", [P, H // 2, P])
        PW = [sb(f"PW{u}", [P, 4, P]) for u in range(UNITS)]
        Q = [sb(f"Q{u}", [P, 4, P]) for u in range(UNITS)]
        X = [sb(f"X{n}", [P, H, D]) for n in range(2)]
        T16 = [sb(f"T16{n}", [P, H, D]) for n in range(2)]
        AT = sb("AT", [P, H, P])
        zrow = sb("zrow", [P, HD])

        ab = [ps(f"ab{n}", [P, 512]) for n in range(3)]
        ring = [ps(f"ring{n}", [P, 512]) for n in range(3)]
        xps = [ps(f"xps{n}", [P, H, D]) for n in range(2)]

        held = sem("held")
        consts_in = sem("consts_in")
        half_set = sem("half_set")
        frames_in = sem("frames_in")
        mdct_full = sem("mdct_full")
        proj_full = sem("proj_full")
        gram_full = sem("gram_full")
        normed_full = sem("normed_full")
        keys_full = sem("keys_full")
        stats_ok = sem("stats_ok")
        meanvar_ok = sem("meanvar_ok")
        vareps_ok = sem("vareps_ok")
        rstd_ok = sem("rstd_ok")
        x1_ok = sem("x1_ok")
        res_ok = sem("res_ok")
        normed_ok = sem("normed_ok")
        normedT_ok = sem("normedT_ok")
        bexp_ok = sem("bexp_ok")
        bexp1_ok = sem("bexp1_ok")
        rate_ok = sem("rate_ok")
        rowmax_ok = sem("rowmax_ok")
        shifted_ok = sem("shifted_ok")
        exp_ok = sem("exp_ok")
        rowsum_ok = sem("rowsum_ok")
        rowinv_ok = sem("rowinv_ok")
        soft_ok = sem("soft_ok")
        values_ok = sem("values_ok")
        turned_ok = sem("turned_ok")
        masked_ok = sem("masked_ok")
        ring_full = sem("ring_full")
        ring_read = sem("ring_read")
        x_full = sem("x_full")
        x_ok = sem("x_ok")
        res_out = sem("res_out")
        rk_out = sem("rk_out")
        u_out = sem("u_out")
        z_out = sem("z_out")
        def own(use):
            return use - 3 * (use > KEYS) - (use > NORMED)

        def exists(i, use):
            if not isinstance(i, int):
                return True
            ahead = 1 if KEYS <= use < KEYS + 3 else 2 if use == NORMED else 0
            return 0 <= i + ahead < TILES

        def ring_taker(i, use):
            use -= 3
            while True:
                if use < 0:
                    i, use = i - 1, use + RING_USES
                if isinstance(i, int) and i < -2:
                    return None
                if exists(i, use):
                    break
                use -= 3
            if KEYS <= use < KEYS + 3:
                return turned_ok, 3 * (i + 1) + use - KEYS + 1
            if use == NORMED:
                return normedT_ok, i + 2 + 1
            return ring_read, OWN_USES * i + own(use) + 1

        def schedule(eng, prologue, body, between):
            prologue()
            body(0, 1, 2, None, None)
            with eng.Fori(1, PT) as i:
                body(i, i + 1, i + 2, None, None)
            between(0)
            with eng.Fori(0, PAIRS - 2) as x:
                for k in range(PT):
                    i = (x + 1) * PT + k
                    body(i, i + 1, i + 2, x, k)
                between(x + 1)
            for k in range(PT):
                i = TILES - PT + k
                body(i, i + 1 if i + 1 < TILES else None, i + 2 if i + 2 < TILES else None, PAIRS - 2, k)
            between(PAIRS - 1)

        block = ctx.enter_context(nc.Block())

        @block.sync
        def _(sp):
            def load_frames(j):
                if not (isinstance(j, int) and j == 0):
                    sp.wait_ge(mdct_full, j)
                    sp.sem_inc(held, 1)
                sp.dma_start(frames[:], frames_d[:, bass.ds(j * 2 * S, 3 * S)]).then_inc(frames_in, 16)

            def per_chain(dram, j, w):
                return dram.rearrange("(j w) h t d -> w j t h d", w=2)[w, bass.ds(j, 1), :, :, :]\
                    .rearrange("j t h d -> (j t) h d")

            def store_rk(j):
                sp.wait_ge(soft_ok, 3 * j + 3)
                sp.sem_inc(held, 1)
                for w in range(2):
                    sp.dma_start(per_chain(rk_d, j, w), soft[w * S:(w + 1) * S, 2, :]
                                 .rearrange("p (h d) -> p h d", h=H)).then_inc(rk_out, 16)

            def store_res(j):
                sp.wait_ge(res_ok, j + 1)
                sp.sem_inc(held, 1)
                sp.dma_start(res_d[bass.ds(j * P, P), :], res[:]).then_inc(res_out, 16)

            def prologue():
                for t, d in ((mdct[:], mdct_d), (masks[:], masks_d), (gamma[:], gamma_d), (beta[:], beta_d),
                             (wslow[:], wslow_d)):
                    sp.dma_start(t, d).then_inc(consts_in, 16)
                load_frames(0)
                store_res(0)
                load_frames(1)
                store_rk(0)
                store_res(1)

            def body(i, rest, ln, x, k):
                if ln is not None:
                    load_frames(ln)
                if rest is not None:
                    store_rk(rest)
                if ln is not None:
                    store_res(ln)
                sp.wait_ge(x_ok, 12 * i + 12)
                sp.sem_inc(held, 1)
                for w in range(2):
                    sp.dma_start(per_chain(u_d, i, w), X[1][w * S:(w + 1) * S, :, :]).then_inc(u_out, 16)
                sp.wait_ge(ring_read, OWN_USES * (i + 1))
                sp.sem_inc(held, 1)
                for w in range(2):
                    sp.dma_start(per_chain(z_d, i, w), zrow[w * S:(w + 1) * S, :]
                                 .rearrange("p (h d) -> p h d", h=H)).then_inc(z_out, 16)
                if k is not None:
                    recurrence.store_h(sp, x, steps_done(position(k, 0.0)), steps_done(position(k, 1.0)))

            def load_pair(x):
                for s in (rk_out, u_out, z_out):
                    sp.wait_ge(s, 32 * PT * (x + 1))
                    sp.sem_inc(held, 1)
                recurrence.load(sp, x)

            schedule(sp, prologue, body, load_pair)
            sp.wait_ge(res_out, 16 * TILES)
            sp.wait_ge(rk_out, 32 * TILES)
            sp.wait_ge(u_out, 32 * TILES)
            sp.wait_ge(z_out, 32 * TILES)

        @block.tensor
        def _(pe):
            def project(j, name, slot):
                c = COL[name]
                n = 2 * H if name == "b" else HD
                pe.matmul(ab[slot][:, 0:n], normedT[:], wslow[:, c:c + n], start=True, stop=True)\
                    .then_inc(proj_full, 1)

            def frame_products(j):
                pe.wait_ge(frames_in, 16 * (j + 1))
                if not (isinstance(j, int) and j == 0):
                    pe.wait_ge(shifted_ok, 3 * j)
                pe.matmul(ab[1][:, 0:IN], frames[:, 0:P], mdct[:, 0, :], start=True, stop=False)
                pe.matmul(ab[1][:, 0:IN], frames[:, S:S + P], mdct[:, 1, :], start=False, stop=True)\
                    .then_inc(mdct_full, 1)

            def turn_normed(j):
                pe.wait_ge(normed_ok, j + 1)
                bank = take_ring(j - 2, NORMED)
                pe.transpose(bank[:, 0:P], normed[:], ident).then_inc(normed_full, 1)

            def project_bkq(j):
                pe.wait_ge(normedT_ok, j + 1)
                if isinstance(j, int) and j == 0:
                    pe.wait_ge(res_ok, 1)
                else:
                    pe.wait_ge(masked_ok, 6 * (j - 1) + 4)
                project(j, "b", 1)
                project(j, "k", 2)
                project(j, "q", 0)

            def project_rk_v(j):
                pe.wait_ge(bexp_ok, j + 1)
                project(j, "rk", 1)
                pe.wait_ge(shifted_ok, 3 * j + 1)
                project(j, "v", 2)

            def project_rv(j):
                pe.wait_ge(shifted_ok, 3 * j + 2)
                project(j, "rv", 0)

            def turn_keys(j):
                for n in range(3):
                    pe.wait_ge(soft_ok, 3 * j + n + 1)
                    bank = take_ring(j - 1, KEYS + n)
                    for c in range(H // 2):
                        last = pe.transpose(bank[:, c * P:(c + 1) * P], soft[:, n, c * P:(c + 1) * P], ident)
                    last.then_inc(keys_full, 1)

            def take_ring(i, use):
                before = ring_taker(i, use)
                if before:
                    pe.wait_ge(*before)
                return ring[use % 3]

            def gram(slot, lhs, rhs, odd):
                rows = slice(odd * D, odd * D + D)
                for c in range(H // 2):
                    last = pe.matmul(ab[slot][:, c * P:(c + 1) * P], lhs[rows, c, :], rhs[rows, c, :],
                                     start=True, stop=True)
                last.then_inc(gram_full, 1)

            def causal_grams(j, odd):
                if odd == 0:
                    if isinstance(j, int) and j == TILES - 1:
                        pe.wait_ge(masked_ok, 6 * j + 2)
                    else:
                        pe.wait_ge(values_ok, 2 * (j + 1) + 1)
                else:
                    if isinstance(j, int) and j == TILES - 1:
                        pe.wait_ge(masked_ok, 6 * j + 3)
                    else:
                        pe.wait_ge(values_ok, 2 * (j + 1) + 2)
                gram((2, 0)[odd], kqT[:, :, 0, :], kqT[:, :, 1, :], odd)

            def strict_grams(j, system):
                first = isinstance(j, int) and j == 0
                pe.wait_ge(turned_ok, 3 * j + (1, 3)[system])
                if system == 0:
                    if first:
                        pe.wait_ge(res_ok, 2)
                        pe.wait_ge(values_ok, 1)
                    else:
                        if not (isinstance(j, int) and j == TILES - 1):
                            pe.wait_ge(res_ok, j + 2)
                        pe.wait_ge(masked_ok, 6 * (j - 1) + 5)
                    src = kqT[:, :, 0, :]
                    gram(1, src, src, 0)
                    gram(2, src, src, 1)
                else:
                    if first:
                        pe.wait_ge(values_ok, 2)
                    else:
                        pe.wait_ge(masked_ok, 6 * (j - 1) + 6)
                    gram(0, rkT, rkT, 0)
                    pe.wait_ge(masked_ok, 6 * j + 1)
                    gram(1, rkT, rkT, 1)

            def start_x(j):
                pe.wait_ge(values_ok, 2 * j + 2)
                if not (isinstance(j, int) and j == 0):
                    pe.wait_ge(x_ok, 12 * j)
                for n in range(2):
                    pe.matmul(xps[n][:].rearrange("p h d -> p (h d)"), ident, values[:, n, :], start=True, stop=False,
                              skip_group_check=True)

            def add_power(u, n, rhs, last):
                h = 4 * (u % 2) + n
                return pe.matmul(xps[u // 2][:, h, :], Q[u][:, n, :], rhs, start=False, stop=last,
                                 skip_group_check=True)

            def product(i, level, u):
                use = ROUND + 8 * level + M_USE[u] if level < 3 else LAST + u
                q_use = TURN0 + u if level == 0 else ROUND + 8 * (level - 1) + T_USE[u]
                pe.wait_ge(ring_read, OWN_USES * i + own(q_use) + 1)
                if level:
                    pe.wait_ge(x_ok, 12 * i + 2 * (level - 1) + u // 2 + 1)
                bank = take_ring(i, use)
                for n in range(4):
                    h = 4 * (u % 2) + n
                    o = bank[:, n * P:(n + 1) * P]
                    rhs = X[u // 2][:, h, :] if level else values[:, u // 2, h * D:(h + 1) * D]
                    mm = add_power(u, n, rhs, False)
                    if level < 3:
                        sq = pe.matmul(o, Q[u][:, n, :], PW[u][:, n, :], start=True, stop=True)
                    else:
                        sq = pe.matmul(o, PW[u][:, n, :], Q[u][:, n, :], start=True, stop=True)
                    if n == 3:
                        sq.then_inc(ring_full, 1)
                        if u % 2:
                            mm.then_inc(x_full, 1)

            def turn_power(i, level, u):
                if level == -1:
                    pe.wait_ge(masked_ok, 6 * i + 2 * (u // 2) + 2)
                    use = TURN0 + u
                else:
                    pe.wait_ge(ring_read, OWN_USES * i + own(ROUND + 8 * level + M_USE[u]) + 1)
                    use = ROUND + 8 * level + T_USE[u]
                bank = take_ring(i, use)
                for n in range(4):
                    last = pe.transpose(bank[:, n * P:(n + 1) * P], PW[u][:, n, :], ident)
                last.then_inc(ring_full, 1)

            def add_16th(i, s, rhs, last):
                for u in (2 * s, 2 * s + 1):
                    for n in range(4):
                        mm = add_power(u, n, rhs[:, 4 * (u % 2) + n, :], last)
                mm.then_inc(x_full, 1)

            def finish_x(i, stage, s):
                if stage == 4:
                    pe.wait_ge(ring_read, OWN_USES * i + own(LAST + 2 * s + 1) + 1)
                    pe.wait_ge(x_ok, 12 * i + 6 + s + 1)
                    add_16th(i, s, X[s], False)
                elif stage == 5:
                    pe.wait_ge(x_ok, 12 * i + 8 + s + 1)
                    bank = take_ring(i, TEMP + s)
                    for h in range(H):
                        mm = pe.matmul(bank[:, h * D:(h + 1) * D], Q[2 * s + h // 4][:, h % 4, :], X[s][:, h, :],
                                       start=True, stop=True)
                    mm.then_inc(ring_full, 1)
                else:
                    pe.wait_ge(ring_read, OWN_USES * i + own(TEMP + s) + 1)
                    add_16th(i, s, T16[s], True)

            def read_out(i):
                pe.wait_ge(x_ok, 12 * i + 11)
                pe.wait_ge(masked_ok, 6 * i + 6)
                bank = take_ring(i, READOUT)
                for h in range(H):
                    last = pe.matmul(bank[:, h * D:(h + 1) * D], AT[:, h, :], X[0][:, h, :], start=True, stop=True)
                last.then_inc(ring_full, 1)

            def round_(i, level):
                product(i, level, 0)
                product(i, level, 1)
                turn_power(i, level, 0)
                product(i, level, 2)
                turn_power(i, level, 1)
                product(i, level, 3)
                turn_power(i, level, 2)
                turn_power(i, level, 3)

            def prologue():
                pe.wait_ge(consts_in, 16 * 5)
                frame_products(0)
                turn_normed(0)
                project_bkq(0)
                project_rk_v(0)
                project_rv(0)
                turn_keys(0)
                frame_products(1)
                turn_normed(1)
                strict_grams(0, 0)
                strict_grams(0, 1)
                start_x(0)

            def body(i, rest, ln, x, k):
                for u in range(UNITS):
                    turn_power(i, -1, u)
                if rest is not None:
                    project_bkq(rest)
                round_(i, 0)
                if rest is not None:
                    project_rk_v(rest)
                round_(i, 1)
                if rest is not None:
                    project_rv(rest)
                if ln is not None:
                    frame_products(ln)
                causal_grams(i, 0)
                round_(i, 2)
                causal_grams(i, 1)
                if rest is not None:
                    turn_keys(rest)
                for u in range(UNITS):
                    product(i, 3, u)
                for n in range(2):
                    finish_x(i, 4, n)
                if rest is not None:
                    strict_grams(rest, 0)
                for n in range(2):
                    finish_x(i, 5, n)
                if rest is not None:
                    strict_grams(rest, 1)
                if ln is not None:
                    turn_normed(ln)
                for n in range(2):
                    finish_x(i, 6, n)
                read_out(i)
                if rest is not None:
                    start_x(rest)

            schedule(pe, prologue, body, lambda x: None)

        @block.vector
        def _(dve):
            def norm_stats(j, n, src):
                dve.bn_stats(stats[:, n, :], src).then_inc(stats_ok, 1)
                dve.wait_ge(stats_ok, 2 * j + n + 1)
                dve.sem_inc(held, 1)
                dve.bn_aggr(meanvar[:, n, :], stats[:, n, :]).then_inc(meanvar_ok, 1)
                dve.wait_ge(meanvar_ok, 2 * j + n + 1)
                dve.tensor_scalar(vareps[:, n:n + 1], meanvar[:, n, 1:2], EPS, None, ALU.add).then_inc(vareps_ok, 1)

            def norm1_stats(j):
                dve.wait_ge(mdct_full, j + 1)
                norm_stats(j, 0, ab[1][:, 0:IN])

            def norm1(j):
                dve.wait_ge(rstd_ok, 2 * j + 1)
                dve.tensor_scalar(x1[:], ab[1][:, 0:IN], meanvar[:, 0, 0:1], rstd[:, 0:1], ALU.subtract, ALU.mult)\
                    .then_inc(x1_ok, 1)
                dve.wait_ge(x1_ok, j + 1)
                if not (isinstance(j, int) and j == 0):
                    dve.wait_ge(res_out, 16 * j)
                dve.tensor_tensor(res[:], ab[1][:, 0:IN], x1[:], ALU.add).then_inc(res_ok, 1)
                norm_stats(j, 1, x1[:])

            def norm2(j):
                dve.wait_ge(rstd_ok, 2 * j + 2)
                dve.tensor_scalar(normed[:], x1[:], meanvar[:, 1, 0:1], rstd[:, 1:2], ALU.subtract, ALU.mult)\
                    .then_inc(normed_ok, 1)

            def rates(j):
                dve.wait_ge(bexp_ok, j + 1)
                dve.tensor_scalar(bexp1[:], bexp[:], 1.0, None, ALU.add).then_inc(bexp1_ok, 1)
                dve.wait_ge(bexp1_ok, j + 1)
                dve.reciprocal(rate[:], bexp1[:]).then_inc(rate_ok, 1)

            def shift(j, n):
                src = ab[(2, 0, 1)[n]][:, 0:HD].rearrange("p (h d) -> p h d", h=H)
                dve.wait_ge(proj_full, 6 * j + (2, 3, 4)[n])
                dve.tensor_reduce(rowmax[:, n, :], src, AX_X, ALU.max).then_inc(rowmax_ok, 1)
                dve.wait_ge(rowmax_ok, 3 * j + n + 1)
                if not (isinstance(j, int) and j == 0):
                    dve.wait_ge(soft_ok, 3 * (j - 1) + n + 1)
                dve.tensor_tensor(expd[:, n, :].rearrange("p (h d) -> p h d", h=H), src,
                                  rowmax[:, n, :].unsqueeze(2).to_broadcast([P, H, D]), ALU.subtract)\
                    .then_inc(shifted_ok, 1)

            def scale_values(j, n):
                dve.wait_ge(proj_full, 6 * j + 5 + n)
                if n == 0:
                    dve.wait_ge(rate_ok, j + 1)
                    if not (isinstance(j, int) and j == 0):
                        dve.wait_ge(x_full, 12 * j - 10)
                dve.tensor_tensor(values[:, n, :].rearrange("p (h d) -> p h d", h=H),
                                  ab[(2, 0)[n]][:, 0:HD].rearrange("p (h d) -> p h d", h=H),
                                  rate[:, n * H:(n + 1) * H].unsqueeze(2).to_broadcast([P, H, D]), ALU.mult)\
                    .then_inc(values_ok, 1)

            def sums(j, n):
                dve.wait_ge(exp_ok, 3 * j + n + 1)
                dve.tensor_reduce(rowsum[:, n, :], expd[:, n, :].rearrange("p (h d) -> p h d", h=H), AX_X, ALU.add)\
                    .then_inc(rowsum_ok, 1)
                dve.wait_ge(rowsum_ok, 3 * j + n + 1)
                dve.reciprocal(rowinv[:, n, :], rowsum[:, n, :]).then_inc(rowinv_ok, 1)

            def mask_strict_grams(j, use):
                system, odd = use // 2, use % 2
                bank = ab[(1, 2, 0, 1)[use]]
                dve.wait_ge(gram_full, 6 * j + use + 1)
                for c in range(H // 2):
                    h = 2 * c + odd
                    last = dve.scalar_tensor_tensor(out=PW[2 * system + h // 4][:, h % 4, :],
                                                    in0=bank[:, c * P:(c + 1) * P],
                                                    scalar=rate[:, system * H + h:system * H + h + 1],
                                                    in1=mask_strict, op0=ALU.mult, op1=ALU.mult)
                last.then_inc(masked_ok, 1)

            def mask_causal_grams(j, odd):
                dve.wait_ge(gram_full, 6 * j + 4 + odd + 1)
                if not (isinstance(j, int) and j == 0):
                    dve.wait_ge(ring_full, OWN_USES * j)
                dve.tensor_tensor(AT[:].rearrange("p (n b) c -> p b n c", b=2)[:, odd, :, :],
                                  ab[(2, 0)[odd]][:].rearrange("p (n c) -> p n c", c=P),
                                  mask_causal.unsqueeze(1).to_broadcast([P, H // 2, P]), ALU.mult)\
                    .then_inc(masked_ok, 1)

            def recur(x, k, f, until):
                recurrence.on_dve(dve, x, beside_tile(k, f, until))

            def prologue():
                dve.memset(minus_half[:], -0.5).then_inc(half_set, 1)
                dve.wait_ge(consts_in, 16 * 5)
                norm1_stats(0)
                norm1(0)
                norm2(0)
                rates(0)
                for n in range(3):
                    shift(0, n)
                for n in range(2):
                    scale_values(0, n)
                for n in range(3):
                    sums(0, n)
                norm1_stats(1)
                norm1(1)
                norm2(1)
                for use in range(4):
                    mask_strict_grams(0, use)

            def body(i, rest, ln, x, k):
                recur(x, k, 0.00, 0.12)
                if rest is not None:
                    rates(rest)
                recur(x, k, 0.12, 0.14)
                if rest is not None:
                    shift(rest, 0)
                recur(x, k, 0.14, 0.18)
                if rest is not None:
                    shift(rest, 1)
                recur(x, k, 0.18, 0.32)
                if rest is not None:
                    shift(rest, 2)
                recur(x, k, 0.32, 0.36)
                if rest is not None:
                    scale_values(rest, 0)
                recur(x, k, 0.36, 0.40)
                if rest is not None:
                    sums(rest, 0)
                recur(x, k, 0.40, 0.42)
                if rest is not None:
                    sums(rest, 1)
                recur(x, k, 0.42, 0.46)
                if rest is not None:
                    sums(rest, 2)
                recur(x, k, 0.46, 0.52)
                if rest is not None:
                    scale_values(rest, 1)
                recur(x, k, 0.52, 0.54)
                if ln is not None:
                    norm1_stats(ln)
                recur(x, k, 0.54, 0.58)
                if ln is not None:
                    norm1(ln)
                recur(x, k, 0.58, 0.60)
                mask_causal_grams(i, 0)
                recur(x, k, 0.60, 0.62)
                if ln is not None:
                    norm2(ln)
                recur(x, k, 0.62, 0.68)
                mask_causal_grams(i, 1)
                recur(x, k, 0.68, 0.86)
                if rest is not None:
                    mask_strict_grams(rest, 0)
                recur(x, k, 0.86, 0.88)
                if rest is not None:
                    mask_strict_grams(rest, 1)
                recur(x, k, 0.88, 0.92)
                if rest is not None:
                    mask_strict_grams(rest, 2)
                recur(x, k, 0.92, 0.95)
                if rest is not None:
                    mask_strict_grams(rest, 3)
                recur(x, k, 0.95, 1.00)

            schedule(dve, prologue, body, lambda x: None)

        @block.scalar
        def _(act):
            def scale_normedT(j):
                act.wait_ge(normed_full, j + 1)
                if not (isinstance(j, int) and j == 0):
                    act.wait_ge(proj_full, 6 * j)
                act.activation(normedT[:], ring[NORMED % 3][:, 0:P], ACT.Identity, bias=beta[:], scale=gamma[:])\
                    .then_inc(normedT_ok, 1)

            def exp_rates(j):
                act.wait_ge(proj_full, 6 * j + 1)
                act.activation(bexp[:], ab[1][:, 0:2 * H], ACT.Exp, scale=-1.0).then_inc(bexp_ok, 1)

            def exp_rows(j, n):
                act.wait_ge(shifted_ok, 3 * j + n + 1)
                act.activation(expd[:, n, :], expd[:, n, :], ACT.Exp).then_inc(exp_ok, 1)

            def copy_turned(j):
                if not (isinstance(j, int) and j == 0):
                    act.wait_ge(gram_full, 6 * j)
                for n in range(3):
                    act.wait_ge(keys_full, 3 * j + n + 1)
                    dst = kqT[:, :, n, :] if n < 2 else rkT[:]
                    act.copy(dst, ring[(KEYS + n) % 3][:].rearrange("p (c t) -> p c t", c=H // 2))\
                        .then_inc(turned_ok, 1)

            def copy_power(i, level, u):
                use = ROUND + 8 * level + M_USE[u] if level < 3 else LAST + u
                act.wait_ge(ring_full, OWN_USES * i + own(use) + 1)
                dst = PW[u] if level < 3 else Q[u]
                act.copy(dst[:].rearrange("p n c -> p (n c)"), ring[use % 3][:]).then_inc(ring_read, 1)

            def copy_q(i, level, u):
                use = TURN0 + u if level == -1 else ROUND + 8 * level + T_USE[u]
                act.wait_ge(ring_full, OWN_USES * i + own(use) + 1)
                act.copy(Q[u][:].rearrange("p n c -> p (n c)"), ring[use % 3][:]).then_inc(ring_read, 1)

            def copy_x(i, stage, s):
                act.wait_ge(x_full, 12 * i + 2 * stage + s + 1)
                if s == 1 and stage == 0 and not (isinstance(i, int) and i == 0):
                    act.wait_ge(u_out, 32 * i)
                act.copy(X[s][:], xps[s][:]).then_inc(x_ok, 1)

            def copy_temp(i, s):
                act.wait_ge(ring_full, OWN_USES * i + own(TEMP + s) + 1)
                act.copy(T16[s][:].rearrange("p h d -> p (h d)"), ring[(TEMP + s) % 3][:]).then_inc(ring_read, 1)

            def copy_z(i):
                if not (isinstance(i, int) and i == 0):
                    act.wait_ge(z_out, 32 * i)
                act.wait_ge(ring_full, OWN_USES * (i + 1))
                act.copy(zrow[:], ring[READOUT % 3][:]).then_inc(ring_read, 1)

            def recur(x, k, f, until):
                recurrence.on_act(act, x, beside_tile(k, f, until))

            def prologue():
                act.wait_ge(consts_in, 16 * 5)
                scale_normedT(0)
                exp_rates(0)
                for n in range(3):
                    exp_rows(0, n)
                copy_turned(0)
                scale_normedT(1)

            def round_(i, level, x, k, f, until):
                def meanwhile(n):
                    recur(x, k, f + (until - f) * n / 10, f + (until - f) * (n + 1) / 10)

                copy_power(i, level, 0)
                meanwhile(0)
                copy_power(i, level, 1)
                meanwhile(1)
                copy_x(i, level, 0)
                meanwhile(2)
                copy_q(i, level, 0)
                meanwhile(3)
                copy_power(i, level, 2)
                meanwhile(4)
                copy_q(i, level, 1)
                meanwhile(5)
                copy_power(i, level, 3)
                meanwhile(6)
                copy_x(i, level, 1)
                meanwhile(7)
                copy_q(i, level, 2)
                meanwhile(8)
                copy_q(i, level, 3)
                meanwhile(9)

            def body(i, rest, ln, x, k):
                copy_q(i, -1, 0)
                recur(x, k, 0.000, 0.023)
                copy_q(i, -1, 1)
                recur(x, k, 0.023, 0.047)
                copy_q(i, -1, 2)
                recur(x, k, 0.047, 0.070)
                copy_q(i, -1, 3)
                recur(x, k, 0.070, 0.093)
                if rest is not None:
                    exp_rates(rest)
                recur(x, k, 0.093, 0.117)
                if rest is not None:
                    exp_rows(rest, 0)
                recur(x, k, 0.117, 0.140)
                round_(i, 0, x, k, 0.140, 0.280)
                if rest is not None:
                    exp_rows(rest, 1)
                recur(x, k, 0.280, 0.300)
                if rest is not None:
                    exp_rows(rest, 2)
                recur(x, k, 0.300, 0.320)
                round_(i, 1, x, k, 0.320, 0.460)
                round_(i, 2, x, k, 0.460, 0.620)
                if rest is not None:
                    copy_turned(rest)
                recur(x, k, 0.620, 0.646)
                copy_power(i, 3, 0)
                recur(x, k, 0.646, 0.671)
                copy_power(i, 3, 1)
                recur(x, k, 0.671, 0.697)
                copy_x(i, 3, 0)
                recur(x, k, 0.697, 0.723)
                copy_power(i, 3, 2)
                recur(x, k, 0.723, 0.749)
                copy_power(i, 3, 3)
                recur(x, k, 0.749, 0.774)
                copy_x(i, 3, 1)
                recur(x, k, 0.774, 0.800)
                copy_x(i, 4, 0)
                recur(x, k, 0.800, 0.825)
                copy_x(i, 4, 1)
                recur(x, k, 0.825, 0.850)
                copy_temp(i, 0)
                recur(x, k, 0.850, 0.875)
                copy_temp(i, 1)
                recur(x, k, 0.875, 0.900)
                if ln is not None:
                    scale_normedT(ln)
                recur(x, k, 0.900, 0.925)
                copy_x(i, 5, 0)
                recur(x, k, 0.925, 0.950)
                copy_x(i, 5, 1)
                recur(x, k, 0.950, 0.975)
                copy_z(i)
                recur(x, k, 0.975, 1.000)

            schedule(act, prologue, body, lambda x: None)

        @block.gpsimd
        def _(pool):
            def rstd_of(j, n):
                pool.wait_ge(vareps_ok, 2 * j + n + 1)
                pool.tensor_tensor(rstd[:, n:n + 1], vareps[:, n:n + 1], minus_half[:], ALU.pow).then_inc(rstd_ok, 1)

            def normalise(j, n):
                if n == 0 and not (isinstance(j, int) and j == 0):
                    pool.wait_ge(turned_ok, 3 * j)
                    pool.wait_ge(rk_out, 32 * j)
                pool.wait_ge(rowinv_ok, 3 * j + n + 1)
                pool.tensor_tensor(soft[:, n, :].rearrange("p (h d) -> p h d", h=H),
                                   expd[:, n, :].rearrange("p (h d) -> p h d", h=H),
                                   rowinv[:, n, :].unsqueeze(2).to_broadcast([P, H, D]), ALU.mult)\
                    .then_inc(soft_ok, 1)

            def recur(x, k, f, until):
                recurrence.on_pool(pool, x, beside_tile(k, f, until))

            def prologue():
                pool.wait_ge(half_set, 1)
                rstd_of(0, 0)
                rstd_of(0, 1)
                for n in range(3):
                    normalise(0, n)
                rstd_of(1, 0)
                rstd_of(1, 1)

            def body(i, rest, ln, x, k):
                recur(x, k, 0.00, 0.42)
                if rest is not None:
                    normalise(rest, 0)
                recur(x, k, 0.42, 0.46)
                if rest is not None:
                    normalise(rest, 1)
                recur(x, k, 0.46, 0.50)
                if rest is not None:
                    normalise(rest, 2)
                recur(x, k, 0.50, 0.56)
                if ln is not None:
                    rstd_of(ln, 0)
                recur(x, k, 0.56, 0.60)
                if ln is not None:
                    rstd_of(ln, 1)
                recur(x, k, 0.60, 1.00)

            schedule(pool, prologue, body, lambda x: None)


def feed_forward(nc, recurrence, res_d, wout_d, gatew_d, gateb_d, w1_d, b1_d, w2_d, b2_d, ident_d, out):
    with ExitStack() as ctx:
        def sb(what, shape):
            return ctx.enter_context(nc.sbuf_tensor(f"ffn_{what}", shape, F32))

        def ps(what, shape):
            return ctx.enter_context(nc.psum_tensor(f"ffn_{what}", shape, F32))

        def sem(what):
            return ctx.enter_context(nc.semaphore(f"ffn_{what}"))

        B = BATCH
        T = B * P
        N = TILES // B
        ident = sb("ident", [P, P])
        wout = sb("wout", [P, HD // P, IN])
        gatew = sb("gatew", [P, NE])
        gateb = sb("gateb", [P, NE])
        w1 = sb("w1", [P, EXPERTS, F])
        b1 = sb("b1", [P, EXPERTS * FC])
        w2 = sb("w2", [P, EXPERTS, FC, IN])
        b2 = sb("b2", [EXPERTS, IN])
        minus_half = sb("minus_half", [P, B])
        hs = sb("hs", [P, B, HD])
        hsT = sb("hsT", [P, 2, HD // P, P])
        res = sb("res", [P, B, IN])
        acc = [sb(f"acc{n}", [P, B, IN]) for n in range(2)]
        stats = sb("stats", [P, B, 6])
        meanvar = sb("meanvar", [P, B, 2])
        vareps = sb("vareps", [P, B])
        rstd = sb("rstd", [P, B])
        x2 = sb("x2", [P, B, IN])
        x2T = [sb(f"x2T{n}", [P, T]) for n in range(2)]
        logit = sb("logit", [P, B, NE])
        lmax = sb("lmax", [P, B])
        lsum = sb("lsum", [P, B])
        linv = sb("linv", [P, B])
        lexp = sb("lexp", [P, B, NE])
        prob = sb("prob", [P, B, NE])
        top = sb("top", [P, B, 8])
        above = sb("above", [P, B, NE])
        equal = sb("equal", [P, B, NE])
        rank = [sb(f"rank{n}", [P, B, NE]) for n in range(3)]
        nabove = sb("nabove", [P, B])
        room = sb("room", [P, B, NE])
        chosen = sb("chosen", [P, B, NE])
        cw = [sb(f"cw{n}", [P, B, EXPERTS]) for n in range(2)]
        cwT = sb("cwT", [EXPERTS, B, P])
        hid = [sb(f"hid{n}", [P, FC, T]) for n in range(2)]

        tp = [ps(f"tp{n}", [P, 512]) for n in range(2)]
        op = ps("op", [P, 512])
        up = [ps(f"up{n}", [P, 512]) for n in range(3)]
        dn = [ps(f"dn{n}", [P, 512]) for n in range(2)]

        held = sem("held")
        weights_in = [sem(f"weights_in{n}") for n in range(2)]
        consts_ok = sem("consts_ok")
        hs_in = sem("hs_in")
        res_in = sem("res_in")
        hsp_full = sem("hsp_full")
        hsT_ok = sem("hsT_ok")
        op_full = sem("op_full")
        stream_ok = sem("stream_ok")
        stats_ok = sem("stats_ok")
        meanvar_ok = sem("meanvar_ok")
        vareps_ok = sem("vareps_ok")
        rstd_ok = sem("rstd_ok")
        x2_ok = sem("x2_ok")
        x2p_full = sem("x2p_full")
        x2T_ok = sem("x2T_ok")
        logit_full = sem("logit_full")
        router = sem("router")
        lexp_ok = sem("lexp_ok")
        cw_ok = sem("cw_ok")
        cwp_full = sem("cwp_full")
        cwT_ok = sem("cwT_ok")
        bias_full = sem("bias_full")
        bias_ok = sem("bias_ok")
        up_full = sem("up_full")
        hid_ok = sem("hid_ok")
        dn_full = sem("dn_full")
        dn_read = sem("dn_read")
        out_out = sem("out_out")
        ROUTER = 14
        AHEAD = 9

        def schedule(eng, prologue, body, recurrence_through=None):
            prologue()
            for i in range(BESIDE):
                body(i, i % 2, True, True)
            if recurrence_through:
                recurrence_through()
            with eng.Fori(BESIDE // 2, N // 2 - 1) as m:
                body(2 * m, 0, True, False)
                body(2 * m + 1, 1, True, False)
            body(N - 2, 0, True, False)
            body(N - 1, 1, False, False)

        def early(i, n):
            return isinstance(i, int) and i < n

        block = ctx.enter_context(nc.Block())
        weights = ((ident[:], ident_d), (wout[:], wout_d), (gatew[:], gatew_d), (gateb[:], gateb_d),
                   (b2[:], b2_d), (b1[:], b1_d), (w1[:], w1_d), (w2[:], w2_d))

        @block.sync
        def _(sp):
            def load(i):
                if not early(i, 1):
                    sp.wait_ge(hsT_ok, B * i)
                    sp.sem_inc(held, 1)
                    sp.wait_ge(stream_ok, B * i)
                    sp.sem_inc(held, 1)
                for k in range(B):
                    for w in range(2):
                        src = recurrence.h_d.rearrange("(x k w) h t d -> k w x t h d", k=B, w=2)[
                            k, w, bass.ds(i, 1), :, :, :].rearrange("x t h d -> (x t) h d")
                        sp.dma_start(hs[w * S:(w + 1) * S, k, :].rearrange("p (h d) -> p h d", h=H), src)\
                            .then_inc(hs_in, 16)
                sp.dma_start(res[:], res_d[bass.ds(i * T, T), :].rearrange("(k p) d -> p k d", k=B))\
                    .then_inc(res_in, 16)

            def store(i, par):
                last = isinstance(i, int) and i == N - 1
                m = B - (TILES - REAL_TILES) if last else B
                sp.wait_ge(dn_read, EXPERTS * (i + 1))
                sp.sem_inc(held, 1)
                for w in range(2):
                    dst = out.rearrange("t (c w) d -> w t c d", w=2)[w, :, bass.ds(i * B, m), :]
                    sp.dma_start(dst, acc[par][w * S:(w + 1) * S, 0:m, :]).then_inc(out_out, 16)

            def prologue():
                for n, (t, d) in enumerate(weights):
                    sp.dma_start(t, d).then_inc(weights_in[n // 5], 16)
                    if n == 1:
                        load(0)
                recurrence.load_steps(sp, PAIRS - 1, 1)
                load(1)

            def body(i, par, follows, beside):
                if not (isinstance(i, int) and i + 2 >= N):
                    load(i + 2)
                if beside:
                    before = steps_done(batch_position(i, 0.0)) if i else 0
                    done = steps_done(batch_position(i, 1.0))
                    recurrence.store_h(sp, PAIRS - 1, before, done)
                store(i, par)

            def stored():
                sp.wait_ge(recurrence.h_out, 32 * (PT * (PAIRS - 1) + BESIDE))
                sp.sem_inc(held, 1)

            schedule(sp, prologue, body, stored)
            sp.wait_ge(out_out, 32 * N)

        @block.tensor
        def _(pe):
            def turn_hs(j, k):
                if k == 0:
                    pe.wait_ge(hs_in, 32 * B * (j + 1))
                if k >= 2:
                    pe.wait_ge(hsT_ok, B * j + k - 1)
                elif not early(j, 1):
                    if k == 0:
                        pe.wait_ge(x2T_ok, j)
                    else:
                        pe.wait_ge(cwT_ok, j)
                for c in range(HD // P):
                    last = pe.transpose(tp[k % 2][:, c * P:(c + 1) * P], hs[:, k, c * P:(c + 1) * P], ident[:])
                last.then_inc(hsp_full, 1)

            def turn_x2(j):
                pe.wait_ge(x2_ok, B * j + B)
                for k in range(B):
                    last = pe.transpose(tp[0][:, k * P:(k + 1) * P], x2[:, k, :], ident[:])
                last.then_inc(x2p_full, 1)

            def logits(j, par):
                pe.wait_ge(x2T_ok, j + 1)
                for k in range(B):
                    last = pe.matmul(op[:, k * NE:(k + 1) * NE], x2T[par][:, k * P:(k + 1) * P], gatew[:],
                                     start=True, stop=True)
                last.then_inc(logit_full, 1)

            def turn_cw(j, par):
                pe.wait_ge(cw_ok, j + 1)
                for k in range(B):
                    last = pe.transpose(tp[1][0:EXPERTS, k * P:(k + 1) * P], cw[par][:, k, :], ident[:])
                last.then_inc(cwp_full, 1)

            def bias_products(j):
                pe.wait_ge(cwT_ok, j + 1)
                for k in range(B):
                    last = pe.matmul(op[:, k * IN:(k + 1) * IN], cwT[:, k, :], b2[:], start=True, stop=True)
                last.then_inc(bias_full, 1)

            def prologue():
                for k in range(B):
                    turn_hs(0, k)
                    project(0, k)
                turn_x2(0)
                logits(0, 0)
                turn_cw(0, 0)
                bias_products(0)
                pe.wait_ge(weights_in[1], 16 * 3)

            def body(i, par, follows, beside):
                for e in range(EXPERTS):
                    expert_up(i, e, par)
                    if e:
                        expert_down(i, e - 1)
                    if follows:
                        if 1 <= e <= B:
                            project(i + 1, e - 1)
                        if e < B:
                            turn_hs(i + 1, e)
                        if e == 7:
                            turn_x2(i + 1)
                        if e == 8:
                            logits(i + 1, 1 - par)
                        if e == 9:
                            turn_cw(i + 1, 1 - par)
                expert_down(i, EXPERTS - 1)
                if follows:
                    bias_products(i + 1)

            def project(i, k):
                pe.wait_ge(hsT_ok, B * i + k + 1)
                if k:
                    pe.wait_ge(stream_ok, B * i + k)
                elif not early(i, 1):
                    pe.wait_ge(bias_ok, i)
                for c in range(HD // P):
                    last = pe.matmul(op[:, 0:IN], hsT[:, k % 2, c, :], wout[:, c, :],
                                     start=(c == 0), stop=(c == HD // P - 1))
                last.then_inc(op_full, 1)

            def expert_up(i, e, par):
                for f in range(FC):
                    n = e * FC + f
                    slot = n % 3
                    if n >= 3:
                        pe.wait_ge(hid_ok, EXPERTS * FC * i + n - 2)
                    elif not early(i, 1):
                        pe.wait_ge(hid_ok, EXPERTS * FC * i)
                    pe.matmul(up[slot][:, 0:T], w1[:, e, f * P:(f + 1) * P], x2T[par][:], start=True, stop=True)\
                        .then_inc(up_full, 1)

            def expert_down(i, e):
                pe.wait_ge(hid_ok, EXPERTS * FC * i + (e + 1) * FC)
                if e >= 2:
                    pe.wait_ge(dn_read, EXPERTS * i + e - 1)
                elif not early(i, 1):
                    pe.wait_ge(dn_read, EXPERTS * i + e - 1)
                for k in range(B):
                    for f in range(FC):
                        last = pe.matmul(dn[e % 2][:, k * IN:(k + 1) * IN], hid[e % 2][:, f, k * P:(k + 1) * P],
                                         w2[:, e, f, :], start=(f == 0), stop=(f == FC - 1))
                last.then_inc(dn_full, 1)

            pe.wait_ge(weights_in[0], 16 * 5)
            schedule(pe, prologue, body)

        @block.scalar
        def _(act):
            def copy_hsT(j, k):
                act.wait_ge(hsp_full, B * j + k + 1)
                if not (early(j, 1) and k < 2):
                    act.wait_ge(op_full, B * j + k - 1)
                act.copy(hsT[:, k % 2, :, :].rearrange("p c t -> p (c t)"), tp[k % 2][:]).then_inc(hsT_ok, 1)

            def copy_x2T(j, par):
                act.wait_ge(x2p_full, j + 1)
                if not early(j, 2):
                    act.wait_ge(up_full, EXPERTS * FC * (j - 1))
                act.copy(x2T[par][:], tp[0][:, 0:T]).then_inc(x2T_ok, 1)

            def exp_logits(j):
                act.wait_ge(router, ROUTER * j + 3)
                act.activation(lexp[:].rearrange("p k e -> p (k e)"), logit[:].rearrange("p k e -> p (k e)"),
                               ACT.Exp).then_inc(lexp_ok, 1)

            def prologue():
                for k in range(B):
                    copy_hsT(0, k)
                copy_x2T(0, 0)
                exp_logits(0)
                recurrence.on_act(act, PAIRS - 1, FIRST_STEPS)
                act.wait_ge(weights_in[1], 16 * 3)

            def body(i, par, follows, beside):
                for e in range(EXPERTS):
                    for f in range(FC):
                        n = e * FC + f
                        act.wait_ge(up_full, EXPERTS * FC * i + n + 1)
                        if f == 0 and e >= 2:
                            act.wait_ge(dn_full, EXPERTS * i + e - 1)
                        elif f == 0 and not early(i, 1):
                            act.wait_ge(dn_full, EXPERTS * i + e - 1)
                        act.activation(hid[e % 2][:, f, :], up[n % 3][:, 0:T], ACT.Gelu, bias=b1[:, n:n + 1])\
                            .then_inc(hid_ok, 1)
                        if beside:
                            recurrence.on_act(act, PAIRS - 1, beside_batch(i, (n - AHEAD) / 40, (n - AHEAD + 1) / 40))
                        if follows and n == 36:
                            exp_logits(i + 1)
                    if follows:
                        if e < B:
                            copy_hsT(i + 1, e)
                        if e == 7:
                            copy_x2T(i + 1, 1 - par)
                if beside and i == BESIDE - 1:
                    recurrence.on_act(act, PAIRS - 1, beside_batch(i, 1 - AHEAD / 40, 1.0))

            act.wait_ge(weights_in[0], 16 * 5)
            schedule(act, prologue, body)

        @block.gpsimd
        def _(pool):
            def rstd_of(j):
                pool.wait_ge(vareps_ok, j + 1)
                pool.tensor_tensor(rstd[:], vareps[:], minus_half[:], ALU.pow).then_inc(rstd_ok, 1)

            def body(i, par, follows, beside):
                if beside:
                    recurrence.on_pool(pool, PAIRS - 1, beside_batch(i, 0.0, 0.2))
                if follows:
                    rstd_of(i + 1)
                if beside:
                    recurrence.on_pool(pool, PAIRS - 1, beside_batch(i, 0.2, 1.0))

            pool.wait_ge(consts_ok, 3)
            schedule(pool, lambda: rstd_of(0), body)

        @block.vector
        def _(dve):
            def stream(j, par, k):
                if k == 0:
                    dve.wait_ge(res_in, 16 * (j + 1))
                    if not early(j, 2):
                        dve.wait_ge(out_out, 32 * (j - 1))
                dve.wait_ge(op_full, B * j + k + 1)
                dve.tensor_tensor(acc[par][:, k, :], op[:, 0:IN], res[:, k, :], ALU.add).then_inc(stream_ok, 1)
                dve.wait_ge(stream_ok, B * j + k + 1)
                dve.bn_stats(stats[:, k, :], acc[par][:, k, :]).then_inc(stats_ok, 1)
                dve.wait_ge(stats_ok, B * j + k + 1)
                dve.sem_inc(held, 1)
                dve.bn_aggr(meanvar[:, k, :], stats[:, k, :]).then_inc(meanvar_ok, 1)
                if k == B - 1:
                    dve.wait_ge(meanvar_ok, B * j + B)
                    dve.tensor_scalar(vareps[:], meanvar[:, :, 1], EPS, None, ALU.add).then_inc(vareps_ok, 1)

            def normalise(j, par):
                dve.wait_ge(rstd_ok, j + 1)
                for k in range(B):
                    dve.tensor_scalar(x2[:, k, :], acc[par][:, k, :], meanvar[:, k, 0:1], rstd[:, k:k + 1],
                                      ALU.subtract, ALU.mult).then_inc(x2_ok, 1)

            def turned_cw(j):
                dve.wait_ge(cwp_full, j + 1)
                dve.tensor_copy(cwT[:].rearrange("e k p -> e (k p)"), tp[1][0:EXPERTS, 0:T]).then_inc(cwT_ok, 1)

            def add_bias(j, par):
                dve.wait_ge(bias_full, j + 1)
                dve.tensor_tensor(acc[par][:].rearrange("p k d -> p (k d)"), op[:, 0:T],
                                  acc[par][:].rearrange("p k d -> p (k d)"), ALU.add).then_inc(bias_ok, 1)

            def add_expert(i, par, e):
                dve.wait_ge(dn_full, EXPERTS * i + e + 1)
                if e:
                    dve.wait_ge(dn_read, EXPERTS * i + e)
                else:
                    dve.wait_ge(bias_ok, i + 1)
                for k in range(B):
                    last = dve.scalar_tensor_tensor(out=acc[par][:, k, :], in0=dn[e % 2][:, k * IN:(k + 1) * IN],
                                                    scalar=cw[par][:, k, e:e + 1], in1=acc[par][:, k, :],
                                                    op0=ALU.mult, op1=ALU.add)
                last.then_inc(dn_read, 1)

            def prologue():
                for k in range(B):
                    stream(0, 0, k)
                normalise(0, 0)
                route(0, 0)
                turned_cw(0)
                add_bias(0, 0)
                recurrence.on_dve(dve, PAIRS - 1, FIRST_STEPS)

            def body(i, par, follows, beside):
                for e in range(EXPERTS):
                    if follows and e == 7:
                        route(i + 1, 1 - par)
                    add_expert(i, par, e)
                    if follows:
                        if e < B:
                            stream(i + 1, 1 - par, e)
                        if e == 5:
                            normalise(i + 1, 1 - par)
                        if e == 7:
                            turned_cw(i + 1)
                        if e == 9:
                            add_bias(i + 1, 1 - par)
                    if beside:
                        recurrence.on_dve(dve, PAIRS - 1, beside_batch(i, e / 10, (e + 1) / 10))

            def route(i, par):
                def wide(a):
                    return a.unsqueeze(2).to_broadcast([P, B, NE])

                r = ROUTER * i
                dve.wait_ge(logit_full, i + 1)
                dve.tensor_tensor(logit[:], op[:, 0:B * NE].rearrange("p (k e) -> p k e", k=B),
                                  gateb[:].unsqueeze(1).to_broadcast([P, B, NE]), ALU.add).then_inc(router, 1)
                dve.wait_ge(router, r + 1)
                dve.tensor_reduce(lmax[:], logit[:], AX_X, ALU.max).then_inc(router, 1)
                dve.wait_ge(router, r + 2)
                dve.tensor_tensor(logit[:], logit[:], wide(lmax[:]), ALU.subtract).then_inc(router, 1)
                dve.wait_ge(lexp_ok, i + 1)
                dve.tensor_reduce(lsum[:], lexp[:], AX_X, ALU.add).then_inc(router, 1)
                dve.wait_ge(router, r + 4)
                dve.reciprocal(linv[:], lsum[:]).then_inc(router, 1)
                dve.wait_ge(router, r + 5)
                dve.tensor_tensor(prob[:], lexp[:], wide(linv[:]), ALU.mult).then_inc(router, 1)
                dve.wait_ge(router, r + 6)
                dve.sem_inc(held, 1)
                for k in range(B):
                    last = dve.max(top[:, k, :], prob[:, k, :])
                last.then_inc(router, 1)
                dve.wait_ge(router, r + 7)
                dve.tensor_tensor(above[:], prob[:], wide(top[:, :, 1]), ALU.is_gt)
                dve.tensor_tensor(equal[:], prob[:], wide(top[:, :, 1]), ALU.is_equal).then_inc(router, 1)
                dve.wait_ge(router, r + 8)
                dve.tensor_reduce(nabove[:], above[:], AX_X, ALU.add)
                src = equal
                for n, step in enumerate((1, 2, 4)):
                    dve.tensor_copy(rank[n][:, :, 0:step], src[:, :, 0:step])
                    dve.tensor_tensor(rank[n][:, :, step:NE], src[:, :, step:NE], src[:, :, 0:NE - step],
                                      ALU.add).then_inc(router, 1)
                    dve.wait_ge(router, r + 9 + n)
                    src = rank[n]
                dve.tensor_tensor(room[:], rank[2][:], wide(nabove[:]), ALU.add).then_inc(router, 1)
                dve.wait_ge(router, r + 12)
                dve.scalar_tensor_tensor(out=chosen[:].rearrange("p k e -> p (k e)"),
                                         in0=room[:].rearrange("p k e -> p (k e)"), scalar=2.0,
                                         in1=equal[:].rearrange("p k e -> p (k e)"),
                                         op0=ALU.is_le, op1=ALU.mult).then_inc(router, 1)
                dve.wait_ge(router, r + 13)
                dve.tensor_tensor(chosen[:], chosen[:], above[:], ALU.add).then_inc(router, 1)
                dve.wait_ge(router, r + 14)
                dve.tensor_tensor(cw[par][:, :, 0:NE], chosen[:], prob[:], ALU.mult).then_inc(cw_ok, 1)

            dve.memset(minus_half[:], -0.5).then_inc(consts_ok, 1)
            for n in range(2):
                dve.memset(cw[n][:], 1.0).then_inc(consts_ok, 1)
            dve.wait_ge(weights_in[0], 16 * 5)
            dve.wait_ge(consts_ok, 3)
            schedule(dve, prologue, body)


def audio_tower(nc, frames, mdct, wslow, gamma, beta, masks, wout, gatew, gateb, w1, b1, w2, b2, ident, out):
    chain_shape = [FRAMES, H, S, D]
    res_d = nc.dram_tensor("res_scratch", [TILES * P, IN], F32, kind="Internal").ap()
    rk_d = nc.dram_tensor("rk_scratch", chain_shape, F32, kind="Internal").ap()
    u_d = nc.dram_tensor("u_scratch", chain_shape, F32, kind="Internal").ap()
    z_d = nc.dram_tensor("z_scratch", chain_shape, F32, kind="Internal").ap()
    h_d = nc.dram_tensor("h_scratch", chain_shape, F32, kind="Internal").ap()
    with ExitStack() as ctx:
        recurrence = Recurrence(nc, ctx, rk_d, u_d, z_d, h_d)
        tiles_and_recurrence(nc, recurrence, frames, mdct, wslow, gamma, beta, masks, res_d, rk_d, u_d, z_d)
        feed_forward(nc, recurrence, res_d, wout, gatew, gateb, w1, b1, w2, b2, ident, out)


def mdct_matrix():
    length = 2 * HOP
    half = length // 2
    f32 = np.float32
    n = np.arange(length, dtype=f32) + f32(0.5)
    k = f32(np.pi / half) * n[:half]
    n = n + f32(half / 2)
    z = np.sqrt(f32(2.0 / half * 2.0))
    m = z * np.cos(n[:, None] * k[None, :])
    w = np.sin(f32(np.pi) * (np.arange(length, dtype=f32) + f32(0.5)) / f32(length))
    return (w[:, None] * m).astype(f32)


def mask_tables():
    t = np.arange(P)
    same = (t[:, None] // S) == (t[None, :] // S)
    ident = np.eye(P)
    strict = -(same & (t[None, :] < t[:, None])).astype(np.float64)
    causal = (same & (t[:, None] <= t[None, :])).astype(np.float64)
    return np.ascontiguousarray(np.stack([ident, strict, causal], 1).astype(np.float32))


def kernel(x, L0_attn_W_slow, L0_attn_W_out, L0_attn_ln_gamma, L0_attn_ln_beta, L0_ffn_gate_w, L0_ffn_gate_b,
           L0_ffn_sw1, L0_ffn_sb1, L0_ffn_sw2, L0_ffn_sb2, L0_ffn_rw1, L0_ffn_rb1, L0_ffn_rw2, L0_ffn_rb2):
    import concourse.bacc as bacc
    from concourse.bass_utils import run_bass_kernel_spmd

    arr = np.asarray
    x = arr(x)
    blocks = FRAMES + 1
    xp = np.zeros((S, blocks * HOP), x.dtype)
    xp[:, HOP:HOP + LEN] = x
    frames = xp.reshape(S, blocks, HOP).transpose(2, 1, 0).reshape(HOP, blocks * S)
    mdct = mdct_matrix().reshape(2, HOP, IN).transpose(1, 0, 2)
    ws = arr(L0_attn_W_slow).reshape(H, 5 * D + 2, IN)
    part = [ws[:, n * D:(n + 1) * D].reshape(HD, IN) for n in (1, 0, 3, 2, 4)]
    wslow = np.concatenate(part + [ws[:, 5 * D], ws[:, 5 * D + 1]], 0).T
    wout = arr(L0_attn_W_out).T.reshape(HD // P, P, IN).transpose(1, 0, 2)
    w1 = np.concatenate([arr(L0_ffn_rw1), arr(L0_ffn_sw1)], 0).transpose(2, 0, 1)
    b1 = np.concatenate([arr(L0_ffn_rb1), arr(L0_ffn_sb1)], 0).reshape(EXPERTS * FC, P).T
    w2 = np.concatenate([arr(L0_ffn_rw2), arr(L0_ffn_sw2)], 0).reshape(EXPERTS, IN, FC, P).transpose(3, 0, 2, 1)
    b2 = np.concatenate([arr(L0_ffn_rb2), arr(L0_ffn_sb2)], 0)
    gateb = np.broadcast_to(arr(L0_ffn_gate_b)[None, :], (P, NE))
    arrays = {
        "frames": frames, "mdct": mdct, "wslow": wslow, "gamma": arr(L0_attn_ln_gamma).reshape(IN, 1),
        "beta": arr(L0_attn_ln_beta).reshape(IN, 1), "masks": mask_tables(), "wout": wout,
        "gatew": arr(L0_ffn_gate_w).T, "gateb": gateb, "w1": w1, "b1": b1, "w2": w2, "b2": b2,
        "ident": np.eye(P, dtype=np.float32),
    }
    nc = bacc.Bacc("TRN2", target_bir_lowering=False, num_devices=1)
    named, args = {}, []
    for name, a in arrays.items():
        a = np.ascontiguousarray(a)
        named[f"in_{name}"] = a
        args.append(nc.dram_tensor(f"in_{name}", a.shape, mybir.dt.from_np(a.dtype), kind="ExternalInput").ap())
    args.append(nc.dram_tensor("out_0", (S, NF, IN), F32, kind="ExternalOutput").ap())
    audio_tower(nc, *args)
    r = run_bass_kernel_spmd(nc, [named], core_ids=[0])
    return r.results[0]["out_0"]
```
